# Optimizing a Trainium2 kernel written in Bass

```python
import numpy as np
import jax
import jax.numpy as jnp

def _softmax(x, axis=-1):
    return jax.nn.softmax(x, axis=axis)

def _gelu(x):
    return jax.nn.gelu(x, approximate=True)

def _silu(x):
    return jax.nn.silu(x)

def _sigmoid(x):
    return jax.nn.sigmoid(x)

def _layernorm(x, axis=-1, eps=1e-05):
    m = jnp.mean(x, axis=axis, keepdims=True)
    v = jnp.var(x, axis=axis, keepdims=True)
    return (x - m) / jnp.sqrt(v + eps)

def _scatter_add(tgt, idx, src, axis=0):
    return tgt.at[idx].add(src)

def _segment_sum(src, seg, n):
    return jax.ops.segment_sum(src, seg, n)
kernel_name = 'mk_adj_ffn_d2_adj_r2_6200ca'

def setup_inputs(seed: int=0):
    np.random.seed(seed)
    _w = jnp.asarray

    def _rec_inputs():
        import jax
        import jax.numpy as jnp
        _gk = jax.random.key(seed)
        x = -0.0002928 + 1 * jax.random.normal(jax.random.fold_in(_gk, 1), (2048, 256), jnp.float32)
        _a = jax.random.bernoulli(jax.random.fold_in(_gk, 2), 0.000976562, (2048, 2048))
        _a = jnp.logical_or(_a, jnp.swapaxes(_a, -1, -2))
        _a = jnp.logical_or(_a, jnp.eye(2048, dtype=bool))
        _af = _a.astype(jnp.float32)
        adj = _af
        return (x, adj)
    x, adj = _rec_inputs()

    def _L0_gnn_setup():
        import jax, jax.numpy as jnp
        import numpy as np
        N = 4096
        D_IN = 256
        D_OUT = 256
        NEG_BIG = -9000000000000000.0
        key = jax.random.key(seed)
        kx, ka, kw, kb, kn, ke = jax.random.split(key, 6)
        x = jax.random.normal(kx, (N, D_IN), dtype=jnp.float32)
        adj = (jax.random.uniform(ka, (N, N)) > 0.9).astype(jnp.float32)
        stdv = 1.0 / np.sqrt(D_OUT)
        weight = jax.random.uniform(kw, (D_IN, D_OUT), minval=-stdv, maxval=stdv, dtype=jnp.float32)
        bias = jax.random.uniform(kb, (D_OUT,), minval=-stdv, maxval=stdv, dtype=jnp.float32)
        node_w = jax.random.uniform(kn, (D_IN, 1), minval=-1.0, maxval=1.0, dtype=jnp.float32)
        stdv_e = 1.0 / np.sqrt(D_IN)
        edge_w = jax.random.uniform(ke, (D_IN, D_IN), minval=-stdv_e, maxval=stdv_e, dtype=jnp.float32)
        return {'x': x, 'adj': adj, 'weight': weight, 'bias': bias, 'node_w': node_w, 'edge_w': edge_w}
    _L0_gnn_all = _L0_gnn_setup()
    _L0_gnn_in = {k: v for k, v in _L0_gnn_all.items() if k in ('weight', 'bias', 'node_w', 'edge_w')}
    del _L0_gnn_all

    def _L0_ffn_setup():
        import jax, jax.numpy as jnp
        import numpy as np
        B, T, H = (8, 4096, 256)
        E, R = (4, 16)
        SCALE = 0.04
        key = jax.random.key(seed)
        ks = jax.random.split(key, 7)
        return {'x': jax.random.normal(ks[0], (B, T, H), jnp.float32), 'gate_w': jax.random.normal(ks[1], (E, H), jnp.float32) * SCALE, 'thr_w': jax.random.normal(ks[2], (1, H), jnp.float32) * SCALE, 'fc1_w': jax.random.normal(ks[3], (E, H, H), jnp.float32) * SCALE, 'lora_A': jax.random.normal(ks[4], (E, H, R), jnp.float32) * SCALE, 'lora_B': jax.random.normal(ks[5], (E, R, H), jnp.float32) * SCALE, 'fc2_w': jax.random.normal(ks[6], (E, H, H), jnp.float32) * SCALE}
    _L0_ffn_all = _L0_ffn_setup()
    _L0_ffn_in = {k: v for k, v in _L0_ffn_all.items() if k in ('gate_w', 'thr_w', 'fc1_w', 'lora_A', 'lora_B', 'fc2_w')}
    del _L0_ffn_all

    def _L1_gnn_setup():
        import jax, jax.numpy as jnp
        import numpy as np
        N = 2048
        INPUT_DIM = 256
        KEY_DIM = 64
        OUT_DIM = 256
        N_HEADS = 8
        IDENTITY_BIAS = 0.01
        MASK_VAL = 1e+16

        def _xavier(key, shape, gain=np.sqrt(2.0)):
            std = gain * np.sqrt(2.0 / (shape[-2] + shape[-1]))
            return jax.random.normal(key, shape, dtype=jnp.float32) * np.float32(std)
        key = jax.random.key(seed)
        kx, ka, kk, kq, kv, ko = jax.random.split(key, 6)
        node_matrix = jax.random.normal(kx, (N, INPUT_DIM), dtype=jnp.float32)
        adjacency_matrix = jax.random.bernoulli(ka, 0.01, (N, N)).astype(jnp.float32)
        Wks = _xavier(kk, (N_HEADS, INPUT_DIM, KEY_DIM))
        Wqs = _xavier(kq, (N_HEADS, INPUT_DIM, KEY_DIM))
        Wvs = _xavier(kv, (N_HEADS, INPUT_DIM, KEY_DIM))
        Wo = _xavier(ko, (N_HEADS, KEY_DIM, OUT_DIM))
        return {'node_matrix': node_matrix, 'adjacency_matrix': adjacency_matrix, 'Wks': Wks, 'Wqs': Wqs, 'Wvs': Wvs, 'Wo': Wo}
    _L1_gnn_all = _L1_gnn_setup()
    _L1_gnn_in = {k: v for k, v in _L1_gnn_all.items() if k in ('Wks', 'Wqs', 'Wvs', 'Wo')}
    del _L1_gnn_all

    def _L1_ffn_setup():
        import jax, jax.numpy as jnp
        import numpy as np
        B, S, D_IN, D_OUT, K = (4, 2048, 256, 256, 8)
        key = jax.random.key(seed)
        k1, k2, k3, k4 = jax.random.split(key, 4)
        scale_w = 1.0 / np.sqrt(D_IN)
        return {'x': jax.random.normal(k1, (B, S, D_IN), dtype=jnp.float32), 'expert_weights': jax.random.normal(k2, (K, D_OUT, D_IN), dtype=jnp.float32) * scale_w, 'expert_biases': jax.random.normal(k3, (K, D_OUT), dtype=jnp.float32) * 0.02, 'mixer_w': jax.random.normal(k4, (K, D_IN), dtype=jnp.float32) * scale_w, 'mixer_b': jnp.zeros((K,), dtype=jnp.float32)}
    _L1_ffn_all = _L1_ffn_setup()
    _L1_ffn_in = {k: v for k, v in _L1_ffn_all.items() if k in ('expert_weights', 'expert_biases', 'mixer_w', 'mixer_b')}
    del _L1_ffn_all
    return {'x': x, 'adj': adj, 'L0_gnn_weight': _L0_gnn_in['weight'], 'L0_gnn_bias': _L0_gnn_in['bias'], 'L0_gnn_node_w': _L0_gnn_in['node_w'], 'L0_gnn_edge_w': _L0_gnn_in['edge_w'], 'L0_ffn_gate_w': _L0_ffn_in['gate_w'], 'L0_ffn_thr_w': _L0_ffn_in['thr_w'], 'L0_ffn_fc1_w': _L0_ffn_in['fc1_w'], 'L0_ffn_lora_A': _L0_ffn_in['lora_A'], 'L0_ffn_lora_B': _L0_ffn_in['lora_B'], 'L0_ffn_fc2_w': _L0_ffn_in['fc2_w'], 'L1_gnn_Wks': _L1_gnn_in['Wks'], 'L1_gnn_Wqs': _L1_gnn_in['Wqs'], 'L1_gnn_Wvs': _L1_gnn_in['Wvs'], 'L1_gnn_Wo': _L1_gnn_in['Wo'], 'L1_ffn_expert_weights': _L1_ffn_in['expert_weights'], 'L1_ffn_expert_biases': _L1_ffn_in['expert_biases'], 'L1_ffn_mixer_w': _L1_ffn_in['mixer_w'], 'L1_ffn_mixer_b': _L1_ffn_in['mixer_b']}

def reference(x, adj, L0_gnn_weight, L0_gnn_bias, L0_gnn_node_w, L0_gnn_edge_w, L0_ffn_gate_w, L0_ffn_thr_w, L0_ffn_fc1_w, L0_ffn_lora_A, L0_ffn_lora_B, L0_ffn_fc2_w, L1_gnn_Wks, L1_gnn_Wqs, L1_gnn_Wvs, L1_gnn_Wo, L1_ffn_expert_weights, L1_ffn_expert_biases, L1_ffn_mixer_w, L1_ffn_mixer_b):
    import jax
    import jax.numpy as jnp

    def _L0_gnn_ref(x, adj, weight, bias, node_w, edge_w):
        import jax, jax.numpy as jnp
        import numpy as np
        N = 4096
        D_IN = 256
        D_OUT = 256
        NEG_BIG = -9000000000000000.0
        node_att = jax.nn.softmax(x @ node_w, axis=0)
        h = x @ edge_w
        e = h @ h.T
        e = jnp.where(adj > 0, e, NEG_BIG)
        edge_att = jax.nn.softmax(e, axis=1)
        combined_att = node_att * edge_att
        support = x @ weight
        output = adj * combined_att @ support
        return output + bias

    def _L0_ffn_ref(x, gate_w, thr_w, fc1_w, lora_A, lora_B, fc2_w):
        import jax, jax.numpy as jnp
        import numpy as np
        B, T, H = (8, 4096, 256)
        E, R = (4, 16)
        SCALE = 0.04
        b, t, h = x.shape
        e = gate_w.shape[0]
        xf = x.reshape(-1, h)
        gate_logits = jax.nn.softmax(xf @ gate_w.T, axis=-1)
        thresholds = jax.nn.sigmoid(xf @ thr_w.T) * (1.0 / e)
        adapted = gate_logits - thresholds
        selected = (adapted >= 0).astype(xf.dtype)
        weights = adapted * selected
        wsum = jnp.sum(weights, axis=-1, keepdims=True)
        wsum = jnp.where(wsum == 0, jnp.ones_like(wsum), wsum)
        weights = weights / wsum
        hidden = jax.nn.relu(jnp.einsum('ni,ehi->neh', xf, fc1_w))
        lo = jnp.einsum('neh,ehr->ner', hidden, lora_A)
        lo = jnp.einsum('ner,ero->neo', lo, lora_B)
        expert_out = jnp.einsum('neo,edo->ned', lo, fc2_w)
        out = jnp.einsum('ne,ned->nd', weights, expert_out)
        return out.reshape(b, t, h)

    def _L1_gnn_ref(node_matrix, adjacency_matrix, Wks, Wqs, Wvs, Wo):
        import jax, jax.numpy as jnp
        import numpy as np
        N = 2048
        INPUT_DIM = 256
        KEY_DIM = 64
        OUT_DIM = 256
        N_HEADS = 8
        IDENTITY_BIAS = 0.01
        MASK_VAL = 1e+16

        def _xavier(key, shape, gain=np.sqrt(2.0)):
            std = gain * np.sqrt(2.0 / (shape[-2] + shape[-1]))
            return jax.random.normal(key, shape, dtype=jnp.float32) * np.float32(std)
        n = node_matrix.shape[0]
        kd = Wks.shape[-1]
        eye = jnp.eye(n, dtype=node_matrix.dtype)
        adj = jnp.maximum(adjacency_matrix, eye)
        q = jnp.einsum('nd,hdk->hnk', node_matrix, Wqs)
        k = jnp.einsum('nd,hdk->hnk', node_matrix, Wks)
        v = jnp.einsum('nd,hdk->hnk', node_matrix, Wvs)
        scores = jnp.einsum('hqk,hmk->hqm', q, k) * kd ** (-0.5)
        scores = scores + IDENTITY_BIAS * eye - MASK_VAL * (1.0 - adj)
        att = jax.nn.softmax(scores, axis=-1)
        return jnp.einsum('hqm,hmk,hko->qo', att, v, Wo)

    def _L1_ffn_ref(x, expert_weights, expert_biases, mixer_w, mixer_b):
        import jax, jax.numpy as jnp
        import numpy as np
        B, S, D_IN, D_OUT, K = (4, 2048, 256, 256, 8)
        logits = jnp.einsum('bsi,ki->bsk', x, mixer_w) + mixer_b
        coeffs = jax.nn.softmax(logits, axis=-1)
        expert_out = jnp.einsum('bsi,koi->bsko', x, expert_weights)
        y = jnp.einsum('bsk,bsko->bso', coeffs, expert_out)
        y = y + jnp.einsum('bsk,ko->bso', coeffs, expert_biases)
        return y
    x = x + _L0_gnn_ref(_layernorm(x, axis=-1), adj, L0_gnn_weight, L0_gnn_bias, L0_gnn_node_w, L0_gnn_edge_w)
    x = x + _L0_ffn_ref(_layernorm(x, axis=-1)[None], L0_ffn_gate_w, L0_ffn_thr_w, L0_ffn_fc1_w, L0_ffn_lora_A, L0_ffn_lora_B, L0_ffn_fc2_w)[0]
    x = x + _L1_gnn_ref(_layernorm(x, axis=-1), adj, L1_gnn_Wks, L1_gnn_Wqs, L1_gnn_Wvs, L1_gnn_Wo)
    x = x + _L1_ffn_ref(_layernorm(x, axis=-1)[None], L1_ffn_expert_weights, L1_ffn_expert_biases, L1_ffn_mixer_w, L1_ffn_mixer_b)[0]
    return x

_drawn_inputs = setup_inputs


def setup_inputs(seed=0):
    import zlib

    import numpy as np

    out = dict(_drawn_inputs(seed))
    spreads = {'L1_ffn_mixer_b': (0.0, 0.8)}
    factors = {'L0_gnn_weight': 4.903,
     'L0_gnn_node_w': 3.407,
     'L0_ffn_thr_w': 8.0,
     'L1_ffn_expert_biases': 8.0}
    for name, (base, spread) in spreads.items():
        noise = np.random.default_rng([zlib.crc32(name.encode()), seed]).standard_normal(out[name].shape)
        drawn = base * np.exp(spread * noise) if base else spread * noise
        out[name] = jnp.asarray(drawn.astype(out[name].dtype))
    for name, factor in factors.items():
        out[name] = (out[name] * factor).astype(out[name].dtype)
    return out
```

```python
from contextlib import ExitStack, contextmanager

import numpy as np

import concourse.bass as bass
from concourse import mybir

F32 = mybir.dt.float32
F16 = mybir.dt.float16
BF16 = mybir.dt.bfloat16
ALU = mybir.AluOpType
ACT = mybir.ActivationFunctionType
AX = mybir.AxisListType
RMAX = bass.bass_isa.ReduceOp.max
RADD = bass.bass_isa.ReduceOp.add

P = 128


class Tally:

    def __init__(self, eng, sem):
        self.eng, self.sem, self.n = eng, sem, 0

    def add(self, ins):
        ins.then_inc(self.sem, 1)
        self.n = self.n + 1
        return ins

    def wait(self):
        self.eng.wait_ge(self.sem, self.n)

    @contextmanager
    def loop(self, count, per):
        start = self.n
        with self.eng.Fori(0, count) as i:
            self.n = start + i * per
            yield i
        self.n = start + count * per


def product_pair(value):
    a = np.arange(1024, 2048, dtype=np.float64) / 1024
    b = (value / a).astype(np.float16).astype(np.float64)
    n = int(np.argmin(np.abs(a * b - value)))
    return float(a[n]), float(b[n])


def gnn_moe_program(nc, x, adj, w_gnn0, g_bias, w_ffn0, lora_a, lora_bt, fc2, w_gnn1, wo, w_ffn1, expert_biases, mixer_b, out):
    N, D = x.shape
    NT = N // P
    HT = NT // 2
    KD = D // P
    C = 512
    NCH = N // C
    TPC = C // P
    E, _, R = lora_a.shape
    ER = E * R
    HD = 64
    H = wo.shape[0] // HD
    NE = expert_biases.shape[0]
    EPS = 1e-5
    WS = 64.0
    MASKED = -1e16
    SCALE = float(HD) ** -0.5
    EYE_A, EYE_B = product_pair(0.01 / SCALE)

    with ExitStack() as ctx:
        def sem(name):
            return ctx.enter_context(nc.semaphore(name))

        def sems(name, n):
            return [sem(f"{name}{i}") for i in range(n)]

        def sb(name, shape, dt=F32):
            return ctx.enter_context(nc.sbuf_tensor(name, shape, dt))

        X = sb("X", [P, NT, D])
        MASK = sb("MASK", [P, NT, N], BF16)
        arena = sb("arena", [P, 121 * 256])

        def area(kib, words, dt=F32):
            a = arena[:, int(kib * 256):int(kib * 256) + words]
            return a if dt == F32 else a.bitcast(dt)

        def xt_area(kib):
            return area(kib, KD * N, F16).rearrange("p (h k n) -> p h k n", h=2, k=KD)

        xt_low = xt_area(0)
        XT = [(xt_low[:, 0], xt_low[:, 1])] * 3 + [(xt_area(81)[:, 0], xt_area(81)[:, 1])]

        def weights(kib_stage, kib_parts, cols):
            stage = area(kib_stage, KD * cols).rearrange("p (k n) -> p k n", k=KD)
            parts = area(kib_parts, KD * cols, F16).rearrange("p (h k n) -> p h k n", h=2, k=KD)
            return stage, parts[:, 0], parts[:, 1]

        W_COLS = [D + D + 1, E * D + E + 1, 3 * H * HD, NE * D + NE]
        W_AT = [(104, 109), (48, 57), (61, 49), (16, 33)]
        W = [weights(*W_AT[i], W_COLS[i]) for i in range(4)]

        ht = area(16, KD * N, F16).rearrange("p (h k n) -> p h k n", h=2, k=KD)
        HTh, HTl = ht[:, 0], ht[:, 1]
        SUP = area(32, NT * D).rearrange("p (t n) -> p t n", t=NT)
        PROB = [area(48 + 8 * s, N) for s in range(2)]
        PROBT = [area(64 + 8 * s, N) for s in range(2)]
        ADJ = [area(80 + 8 * s, N) for s in range(2)]
        MROW = [area(96 + 4 * s, N // 2, BF16) for s in range(2)]
        HID = area(16, E * KD * C).rearrange("p (o n) -> p o n", o=E * KD)
        FC2 = area(66, E * KD * D).rearrange("p (o n) -> p o n", o=E * KD)
        BT = area(74, E * KD * ER).rearrange("p (o n) -> p o n", o=E * KD)
        LA = area(76, E * KD * R).rearrange("p (o n) -> p o n", o=E * KD)
        MM = area(77, D)
        LOW = [area(78 + s / 2, P) for s in range(2)]
        LOWT = [area(79 + s / 2, P) for s in range(2)]
        V = area(16, NT * H * (HD + 1)).rearrange("p (t h d) -> p t h d", t=NT, h=H)
        QKS = [[area(90 + 8 * s + 4 * q, N // 2, F16) for q in range(2)] for s in range(2)]
        ATT = area(49, NT * H * HD).rearrange("p (t n) -> p t n", t=NT)
        KS, QD, QL, KO = ([area(81 + 16 * s + 4 * q, N // 2, F16) for s in range(2)] for q in range(4))
        PT = [area(113 + 2 * s, C) for s in range(4)]
        MJUNK = [area(12 + b, C // 2, BF16) for b in range(2)]
        ATS = [area(0 + 2 * s, C) for s in range(2)]
        ATTT = [area(4 + 2 * s, C) for s in range(2)]
        WO = area(8, H * HD // P * D).rearrange("p (k n) -> p k n", k=H * HD // P)
        BB = area(50, NE * D // 2, F16)
        BSTAGE = area(54, NE * D)

        XN = [sb(f"XN{s}", [P, D]) for s in range(2)]
        identf = sb("identf", [P, P])
        identb = sb("identb", [P, P], BF16)
        not_eye = sb("not_eye", [P, P], BF16)
        eye_a = sb("eye_a", [P, P], F16)
        eye_b = sb("eye_b", [P, P], F16)
        ones = sb("ones", [P, P], F16)
        gbias = area(114, D)
        mbias = sb("mbias", [P, NE])
        STATS = sb("STATS", [P, NT, 6])
        small = sb("small", [P, 6, NT])
        MEAN, VAR, RSTD, SD, TA, TB = (small[:, i, :] for i in range(6))
        ZC = sb("ZC", [P, NT])
        NATT = sb("NATT", [P, NT])
        zs = sb("zs", [P, 8])
        MX = sb("MX", [P, 2, NCH])
        NMX = sb("NMX", [P, 2])
        RSUM = sb("RSUM", [P, 2])
        RSC = sb("RSC", [P, 4])
        LG = sb("LG", [P, NT, 8])
        GW = sb("GW", [P, NT, 8])
        GS = sb("GS", [P, 4, NT])
        MQ = sb("MQ", [P, TPC, NCH])
        MR = sb("MR", [P, TPC])
        MNEG = sb("MNEG", [P, 2, TPC])
        RD = sb("RD", [P, 2, TPC])
        idle_cells = sb("idle_cells", [P, NT])
        QK = nc.dram_tensor("qk_scratch", [2, 2, H, HD, N], F16).ap()

        PS = [ctx.enter_context(nc.psum_tensor(f"PS{b}", [P, C], F32)) for b in range(8)]

        dve_done = sem("dve_done")
        x_in, small_in = sem("x_in"), sem("small_in")
        w_in, w_high, w_low = sems("w_in", 4), sem("w_high"), sem("w_low")
        ident_zero, ident_ready, consts_ready = sem("ident_zero"), sem("ident_ready"), sem("consts_ready")
        var_ready, std_ready = sem("var_ready"), sem("std_ready")
        xn_ready, xn_transposed = sems("xn_ready", 2), sems("xn_transposed", 2)
        xh_ready, xl_ready = sems("xh_ready", 2), sems("xl_ready", 2)
        h_psum, hh_ready, hl_ready = sems("h_psum", 2), sems("hh_ready", 2), sems("hl_ready", 2)
        sup_psum, sup_copied, z_copied = sems("sup_psum", 2), sems("sup_copied", 2), sems("z_copied", 2)
        z_max, z_allmax, z_neg, z_exp, z_sum = (sem(f"z_{n}") for n in ("max", "allmax", "neg", "exp", "sum"))
        adj_in, mask_ready, mask_stored = sems("adj_in", 2), sems("mask_ready", 2), sems("mask_stored", 2)
        e_ready, e_read = sems("e_ready", NCH), sems("e_read", NCH)
        nmax_ready, p_ready = sems("nmax_ready", 2), sems("p_ready", 2)
        pt_psum, pt_ready = sems("pt_psum", 2), sems("pt_ready", 2)
        o_ready, o_read = sems("o_ready", 2), sems("o_read", 2)
        x_ready = sem("x_ready")
        bt_zero, f0_in = sem("bt_zero"), sem("f0_in")
        lg_ready, sh_ready, ex_ready = sem("lg_ready"), sem("sh_ready"), sem("ex_ready")
        m_product, m_copied = sem("m_product"), sem("m_copied")
        hid_psum, hid_ready = sems("hid_psum", 4), sems("hid_ready", 4)
        low_psum, low_ready, lowt_psum, lowt_ready = (sems(n, 2) for n in ("low_psum", "low_ready", "lowt_psum", "lowt_ready"))
        f0_psum, f0_read = sems("f0_psum", 2), sems("f0_read", 2)
        v_ones, v_psum, v_read = sem("v_ones"), sems("v_psum", 2), sems("v_read", 2)
        qk_psum, qk_high, qk_low, qk_stored = sems("qk_psum", 2), sems("qk_high", 2), sems("qk_low", 2), sems("qk_stored", 2)
        stack_in, row_ones = sems("stack_in", 2), sem("row_ones")
        rmax_psum, rmax_read = sems("rmax_psum", 2), sems("rmax_read", 2)
        rmax_ready, rneg_ready, rrow_psum, rrow_ready = (sem(n) for n in ("rmax_ready", "rneg_ready", "rrow_psum", "rrow_ready"))
        st_ready, exp_done, pv_done = sems("st_ready", 2), sems("exp_done", 4), sems("pv_done", 4)
        rden_ready, att_read = sem("rden_ready"), sems("att_read", 2)
        wo_in, att_copied, at_psum, at_ready = sem("wo_in"), sems("att_copied", 2), sems("at_psum", 2), sems("at_ready", 2)
        wo_psum, wo_read = sems("wo_psum", 2), sems("wo_read", 2)
        eb_in, eb_zero, eb_high, eb_low = sem("eb_in"), sem("eb_zero"), sem("eb_high"), sem("eb_low")
        y_psum, y_read, y_tile = sems("y_psum", 4), sems("y_read", 4), sem("y_tile")
        stored = sem("stored")

        start_at_one = [*mask_ready, *xn_transposed, *xl_ready, *hl_ready, *z_copied, *e_read, *pt_ready, *o_read, *o_ready,
                        *mask_stored, *nmax_ready, *hid_ready, *f0_read, *qk_low, *qk_stored, *v_read, *rmax_read, *exp_done,
                        *att_read, *pv_done, *at_psum, *at_ready, *wo_read, *wo_psum, *y_read, *lowt_psum]

        block = ctx.enter_context(nc.Block())
        x_tiles = x.rearrange("(t p) d -> p t d", p=P)
        out_tiles = out.rearrange("(t p) d -> p t d", p=P)
        adj_tiles = adj.rearrange("(t p) n -> t p n", p=P)

        @block.sync
        def _(sp):
            def load_weights(layer, w):
                sp.dma_start(W[layer][0], w.rearrange("(k p) n -> p k n", p=P)).then_inc(w_in[layer], 16)

            sp.dma_start(X[:, :, :], x_tiles).then_inc(x_in, 16)
            load_weights(0, w_gnn0)
            sp.dma_start(gbias[:, :], g_bias.rearrange("(a d) -> a d", a=1).to_broadcast([P, D])).then_inc(small_in, 16)
            sp.dma_start(mbias[:, :], mixer_b.rearrange("(a d) -> a d", a=1).to_broadcast([P, NE])).then_inc(small_in, 16)

            with sp.Fori(0, HT) as it:
                for s in range(2):
                    sp.wait_ge(mask_ready[s], it + 1)
                    sp.dma_start(ADJ[s], adj_tiles[2 * it + s, :, :]).then_inc(adj_in[s], 16)
                for s in range(2):
                    sp.wait_ge(mask_ready[s], it + 2)
                    sp.dma_start(MASK[:, 2 * it + s, :], MROW[s]).then_inc(mask_stored[s], 16)

            sp.wait_ge(x_ready, 1)
            load_weights(1, w_ffn0)
            sp.dma_start(FC2, fc2.rearrange("e (k p) d -> p (e k) d", p=P)).then_inc(f0_in, 16)
            sp.dma_start(LA, lora_a.rearrange("e (k p) r -> p (e k) r", p=P)).then_inc(f0_in, 16)
            sp.wait_ge(bt_zero, 1)
            for e in range(E):
                sp.dma_start(BT[:, e * KD:(e + 1) * KD, e * R:(e + 1) * R],
                             lora_bt[e].rearrange("(k p) r -> p k r", p=P)).then_inc(f0_in, 16)

            sp.wait_ge(x_ready, 2)
            load_weights(2, w_gnn1)
            with sp.Fori(0, H // 2) as pair:
                for q in range(2):
                    sp.wait_ge(qk_low[q], NCH * pair + NCH + 1)
                    for part in range(2):
                        sp.dma_start(QK[q, part, bass.ds(2 * pair, 2), :, :].rearrange("h d n -> (h d) n"),
                                     QKS[q][part]).then_inc(qk_stored[q], 16)

            def load_stack(h, s):
                for tile, at, q, part in ((KS, 0, 1, 0), (KS, HD, 1, 1), (QD, 0, 0, 0), (QD, HD, 0, 0),
                                          (QL, 0, 0, 1), (KO, 0, 1, 0)):
                    sp.dma_start(tile[s][at:at + HD, :], QK[q, part, h, :, :]).then_inc(stack_in[s], 16)

            for q in range(2):
                sp.wait_ge(qk_stored[q], 32 * H // 2 + 1)
            for s in range(2):
                load_stack(s, s)
            with sp.Fori(1, H // 2) as pair:
                for s in range(2):
                    sp.wait_ge(pv_done[3], 32 * pair + 16 * s - 15)
                    load_stack(2 * pair + s, s)

            sp.dma_start(WO, wo.rearrange("(k p) n -> p k n", p=P)).then_inc(wo_in, 16)
            sp.wait_ge(pv_done[3], 16 * H + 1)
            load_weights(3, w_ffn1)
            sp.wait_ge(x_ready, 3)
            sp.dma_start(BSTAGE[0:1, :], expert_biases.rearrange("k d -> (k d)").rearrange("(a n) -> a n", a=1)).then_inc(eb_in, 16)
            with sp.Fori(0, NT) as t:
                sp.wait_ge(y_tile, t + 1)
                sp.dma_start(out_tiles[:, t, :], X[:, t, :]).then_inc(stored, 16)
            sp.wait_ge(stored, 16 * NT)

        @block.gpsimd
        def _(pool):
            for first in start_at_one:
                pool.sem_inc(first, 1)
            nc.gpsimd.memset(identf[:, :], 0.0).then_inc(ident_zero, 1)
            pool.wait_ge(ident_zero, 1)
            nc.gpsimd.affine_select(out=identf[:, :], in_=identf[:, :], compare_op=ALU.not_equal, fill=1.0, base=0,
                                    pattern=[[-1, P]], channel_multiplier=1).then_inc(ident_ready, 1)
            nc.gpsimd.memset(ones[:, :], 1.0).then_inc(ident_ready, 1)
            def node_max():
                pool.wait_ge(z_max, 1)
                nc.gpsimd.partition_all_reduce(zs[:, 1:2], zs[:, 0:1], P, RMAX).then_inc(z_allmax, 1)
                pool.wait_ge(z_exp, 1)
                nc.gpsimd.partition_all_reduce(zs[:, 4:5], zs[:, 3:4], P, RADD).then_inc(z_sum, 1)

            node_max()
            pool.wait_ge(x_ready, 1)
            nc.gpsimd.memset(BT, 0.0).then_inc(bt_zero, 1)
            for s in range(2):
                nc.gpsimd.memset(LOW[s], 0.0).then_inc(bt_zero, 1)
            pool.wait_ge(x_ready, 2)
            nc.gpsimd.memset(V[:, :, :, HD:HD + 1], 1.0).then_inc(v_ones, 1)
            pool.wait_ge(v_ones, 1)
            for q in range(2):
                pool.wait_ge(qk_stored[q], 32 * H // 2 + 1)
            for s in range(2):
                pool.wait_ge(v_read[s], HT + 1)
                if s:
                    pool.wait_ge(row_ones, 1)
                nc.gpsimd.memset(KO[s][HD:HD + 1, :], 1.0).then_inc(row_ones, 1)
            with pool.Fori(0, HT) as it:
                for s in range(2):
                    for b in range(2):
                        pool.wait_ge(att_read[b], 2 * H + 1)
                    pool.wait_ge(at_psum[s], it + 1)
                    nc.gpsimd.tensor_copy(ATS[s], ATT[:, 2 * it + s, :]).then_inc(att_copied[s], 1)
            pool.wait_ge(x_ready, 3)
            nc.gpsimd.memset(BB[0:33, :], 0.0).then_inc(eb_zero, 1)

        @block.tensor
        def _(pe):
            def split_product(ps, left, right, last_of=None):
                n = 0
                for k in range(KD):
                    for a, b in ((0, 0), (0, 1), (1, 0)):
                        n += 1
                        last = pe.matmul(ps, left(a, k), right(b, k), start=(n == 1), stop=(n == 3 * KD),
                                         skip_group_check=True)
                return last

            def transpose_nodes(f):
                with pe.Fori(0, HT) as it:
                    for s in range(2):
                        pe.wait_ge(xn_ready[s], f * HT + it + 1)
                        pe.wait_ge(xl_ready[s], f * HT + it + 1)
                        for k in range(KD):
                            last = pe.transpose(PS[s][:, k * P:(k + 1) * P], XN[s][:, k * P:(k + 1) * P], identf[:, :])
                        last.then_inc(xn_transposed[s], 1)
                for s in range(2):
                    pe.wait_ge(xl_ready[s], (f + 1) * HT + 1)
                pe.wait_ge(w_low, f + 1)
                pe.wait_ge(w_high, f + 1)

            pe.wait_ge(ident_ready, 2)
            pe.wait_ge(consts_ready, 1)

            transpose_nodes(0)
            xt, w = XT[0], W[0][1:]
            with pe.Fori(0, NCH) as c:
                for o in range(KD):
                    pe.wait_ge(hl_ready[o], c + 1)
                    split_product(PS[2 + o][:, :], lambda a, k: w[a][:, k, o * P:(o + 1) * P],
                                  lambda b, k: xt[b][:, k, bass.ds(c * C, C)]).then_inc(h_psum[o], 1)
            with pe.Fori(0, HT) as it:
                for s in range(2):
                    pe.wait_ge(z_copied[s], it + 1)
                    split_product(PS[4 + s][:, 0:D + 1], lambda a, k: xt[a][:, k, bass.ds((2 * it + s) * P, P)],
                                  lambda b, k: w[b][:, k, D:2 * D + 1]).then_inc(sup_psum[s], 1)

            def edge_scores(t):
                for c in range(NCH):
                    pe.wait_ge(e_read[c], t + 1)
                    split_product(PS[c][:, :], lambda a, k: (HTh, HTl)[a][:, k, bass.ds(t * P, P)],
                                  lambda b, k: (HTh, HTl)[b][:, k, c * C:(c + 1) * C]).then_inc(e_ready[c], 1)

            def edge_output(it, s):
                t = 2 * it + s

                def transposes(g):
                    pe.wait_ge(pt_ready[g % 2], 2 * t + g // 2 + 1)
                    for q in range(TPC):
                        j = g * TPC + q
                        last = pe.transpose(PS[4 + g % 2][:, q * P:(q + 1) * P], PROB[s][:, j * P:(j + 1) * P], identf[:, :])
                    last.then_inc(pt_psum[g % 2], 1)

                def products(g):
                    pe.wait_ge(pt_ready[g % 2], 2 * t + g // 2 + 2)
                    for q in range(TPC):
                        j = g * TPC + q
                        last = pe.matmul(PS[6 + s][:, 0:D], PROBT[s][:, j * P:(j + 1) * P], SUP[:, j, :],
                                         start=(j == 0), stop=(j == NT - 1))
                    if g == NCH - 1:
                        last.then_inc(o_ready[s], 1)

                pe.wait_ge(p_ready[s], it + 1)
                transposes(0)
                pe.wait_ge(o_read[s], it + 1)
                for g in range(1, NCH):
                    transposes(g)
                    products(g - 1)
                products(NCH - 1)

            for s in range(2):
                pe.wait_ge(hl_ready[s], NCH + 1)
                pe.wait_ge(z_copied[s], HT + 1)
            edge_scores(0)
            with pe.Fori(0, HT - 1) as it:
                edge_scores(2 * it + 1)
                edge_output(it, 0)
                edge_scores(2 * it + 2)
                edge_output(it, 1)
            edge_scores(NT - 1)
            edge_output(HT - 1, 0)
            edge_output(HT - 1, 1)

            pe.wait_ge(x_ready, 1)
            transpose_nodes(1)
            xt, w = XT[1], W[1][1:]
            GC = E * D
            with pe.Fori(0, NT) as t:
                split_product(PS[2][:, bass.ds(t * (E + 1), E + 1)], lambda a, k: xt[a][:, k, bass.ds(t * P, P)],
                              lambda b, k: w[b][:, k, GC:GC + E + 1]).then_inc(lg_ready, 1)
            pe.wait_ge(f0_in, 16 * (2 + E))
            for o in range(E * KD):
                last = pe.matmul(PS[3][0:ER, 0:D], BT[:, o, :], FC2[:, o, :], start=(o == 0), stop=(o == E * KD - 1))
            last.then_inc(m_product, 1)
            pe.wait_ge(m_copied, 1)
            with pe.Fori(0, NCH) as c:
                for o in range(E * KD):
                    b = o % 4
                    pe.wait_ge(hid_ready[b], 2 * c + o // 4 + 1)
                    split_product(PS[4 + b][:, :], lambda a, k: w[a][:, k, o * P:(o + 1) * P],
                                  lambda bb, k: xt[bb][:, k, bass.ds(c * C, C)]).then_inc(hid_psum[b], 1)
                for b in range(4):
                    pe.wait_ge(hid_ready[b], 2 * c + 3)
                for u in range(TPC // 2):
                    for s in range(2):
                        n = 2 * u + s
                        pe.wait_ge(f0_read[s], 2 * c + u + 1)
                        for e in range(E):
                            for k in range(KD):
                                last = pe.matmul(PS[s][:, e * R:(e + 1) * R], HID[:, e * KD + k, n * P:(n + 1) * P],
                                                 LA[:, e * KD + k, :], start=(k == 0), stop=(k == KD - 1))
                        last.then_inc(low_psum[s], 1)
                    for s in range(2):
                        pe.wait_ge(low_ready[s], 2 * c + u + 1)
                        pe.transpose(PS[2 + s][:, 0:P], LOW[s], identf[:, :]).then_inc(lowt_psum[s], 1)
                    for s in range(2):
                        pe.wait_ge(lowt_ready[s], 2 * c + u + 1)
                        pe.matmul(PS[s][:, 0:D], LOWT[s][0:ER, :], MM[0:ER, :], start=True, stop=True).then_inc(f0_psum[s], 1)

            pe.wait_ge(x_ready, 2)
            transpose_nodes(2)
            xt, w = XT[2], W[2][1:]
            with pe.Fori(0, H // 2) as pair:
                for q in range(2):
                    pe.wait_ge(qk_low[q], NCH * pair + 1)
                    for c in range(NCH):
                        b = NCH * q + c
                        split_product(PS[b][:, :], lambda a, k: w[a][:, k, bass.ds(q * H * HD + pair * P, P)],
                                      lambda bb, k: xt[bb][:, k, c * C:(c + 1) * C]).then_inc(qk_psum[q], 1)
            for q in range(2):
                pe.wait_ge(qk_low[q], NCH * H // 2 + 1)
            with pe.Fori(0, HT) as it:
                for s in range(2):
                    pe.wait_ge(v_read[s], it + 1)
                    split_product(PS[s][:, :], lambda a, k: xt[a][:, k, bass.ds((2 * it + s) * P, P)],
                                  lambda b, k: w[b][:, k, 2 * H * HD:3 * H * HD]).then_inc(v_psum[s], 1)

            def max_scores(head, s, g, q):
                b, i = q % 2, (g * TPC + q // NCH)
                pe.wait_ge(rmax_read[b], head * 32 + g * 8 + q // 2 + 1)
                c = q % NCH
                pe.matmul(PS[5 + b][:, :], QD[s][0:HD, i * P:(i + 1) * P], KO[s][0:HD, c * C:(c + 1) * C],
                          start=True, stop=True).then_inc(rmax_psum[b], 1)

            def max_row(n):
                pe.wait_ge(rneg_ready, n + 1)
                pe.wait_ge(rrow_ready, n)
                for r in range(TPC):
                    last = pe.matmul(PS[4][HD:HD + 1, r * P:(r + 1) * P], MNEG[:, (n_parity(n)), r:r + 1], identf[:, :],
                                     start=True, stop=True, skip_group_check=True)
                last.then_inc(rrow_psum, 1)

            def attend(head, s, ic, ahead, row):
                u = head * NCH + ic
                for j in range(NT + 1):
                    if j < NT:
                        b = j % 2
                        if j == 0:
                            pe.wait_ge(rrow_ready, u + 1)
                        if j >= 2:
                            pe.wait_ge(exp_done[(j - 2) % 4], u * 4 + (j - 2) // 4 + 2)
                        else:
                            pe.wait_ge(exp_done[(j + 2) % 4], u * 4 + 1)
                        cols, keys = slice(ic * C, (ic + 1) * C), slice(j * P, (j + 1) * P)
                        pe.matmul(PS[b][:, :], KS[s][:, keys], QD[s][:, cols], start=True, stop=False, skip_group_check=True)
                        pe.matmul(PS[b][:, :], KO[s][0:HD + 1, keys], QL[s][0:HD + 1, cols], start=False, stop=False,
                                  skip_group_check=True)
                        if j // TPC == ic:
                            d = (j % TPC) * P
                            pe.matmul(PS[b][:, d:d + P], eye_a[:, :], eye_b[:, :], start=False, stop=False, skip_group_check=True)
                        for q in range(TPC):
                            last = pe.matmul(PS[b][:, q * P:(q + 1) * P], MASK[:, ic * TPC + q, keys], identb[:, :],
                                             start=False, stop=(q == TPC - 1), skip_group_check=True)
                        last.then_inc(st_ready[b], 1)
                    if j >= 1:
                        i = j - 1
                        pe.wait_ge(exp_done[i % 4], u * 4 + i // 4 + 2)
                        if i == 0:
                            pe.wait_ge(att_read[ic % 2], 2 * head + ic // 2 + 1)
                        for q in range(TPC):
                            last = pe.matmul(PS[2 + ic % 2][:, q * (HD + 1):(q + 1) * (HD + 1)], PT[i % 4][:, q * P:(q + 1) * P],
                                             V[:, i, head, :], start=(i == 0 and q == 0), stop=(i == NT - 1),
                                             skip_group_check=True)
                        last.then_inc(pv_done[i % 4], 1)
                    if j == 2 and row is not None:
                        max_row(row)
                    if ahead is not None:
                        if ic == 0:
                            if j == NT // 2:
                                pe.wait_ge(stack_in[1 - s], 96 * (half(ahead) + 1))
                            todo = range(2 * (j - NT // 2), 2 * (j - NT // 2) + 2) if NT // 2 <= j < NT else ()
                        else:
                            todo = (j,) if j < NT else ()
                        for q in todo:
                            max_scores(ahead, 1 - s, ic, q)

            def half(head):
                return head // 2 if isinstance(head, int) else head_half[0]

            def n_parity(n):
                return n % 2 if isinstance(n, int) else parity[0]

            head_half, parity = [0], [0]
            pe.wait_ge(row_ones, 2)
            for s in range(2):
                pe.wait_ge(v_read[s], HT + 1)
            pe.wait_ge(stack_in[0], 96)
            for g in range(NCH):
                for q in range(NT):
                    max_scores(0, 0, g, q)
                if g:
                    max_row(g - 1)
            with pe.Fori(0, H // 2 - 1) as pair:
                for s in range(2):
                    for ic in range(NCH):
                        head_half[0], parity[0] = pair + s, (ic + 3) % 2
                        attend(2 * pair + s, s, ic, 2 * pair + s + 1, (2 * pair + s) * NCH + ic + 3)
            for s in range(2):
                for ic in range(NCH):
                    row = (H - 2 + s) * NCH + ic + 3
                    attend(H - 2 + s, s, ic, H - 1 if s == 0 else None, row if row < H * NCH else None)

            pe.wait_ge(wo_in, 16)
            for b in range(2):
                pe.wait_ge(att_read[b], 2 * H + 1)
            KC = H * HD // P
            with pe.Fori(0, HT) as it:
                for s in range(2):
                    pe.wait_ge(att_copied[s], it + 1)
                    pe.wait_ge(at_ready[s], it + 1)
                    for k in range(KC):
                        last = pe.transpose(PS[s][:, k * P:(k + 1) * P], ATS[s][:, k * P:(k + 1) * P], identf[:, :])
                    last.then_inc(at_psum[s], 1)
                for s in range(2):
                    pe.wait_ge(at_ready[s], it + 2)
                    pe.wait_ge(wo_read[s], it + 1)
                    for k in range(KC):
                        last = pe.matmul(PS[2 + s][:, 0:D], ATTT[s][:, k * P:(k + 1) * P], WO[:, k, :],
                                         start=(k == 0), stop=(k == KC - 1))
                    last.then_inc(wo_psum[s], 1)

            pe.wait_ge(x_ready, 3)
            transpose_nodes(3)
            xt, w = XT[3], W[3][1:]
            GC = NE * D
            with pe.Fori(0, NT) as t:
                split_product(PS[4][:, bass.ds(t * NE, NE)], lambda a, k: xt[a][:, k, bass.ds(t * P, P)],
                              lambda b, k: w[b][:, k, GC:GC + NE]).then_inc(lg_ready, 1)
            pe.wait_ge(eb_high, 1)
            pe.wait_ge(eb_low, 1)
            with pe.Fori(0, NT) as t:
                for e in range(NE // 2):
                    pe.wait_ge(y_read[e], t + 1)
                    pe.matmul(PS[e][:, :], ones[0:33, :], BB[0:33, e * C:(e + 1) * C], start=True, stop=False,
                              skip_group_check=True)
                    n = 0
                    for k in range(KD):
                        for a, b in ((0, 0), (0, 1), (1, 0)):
                            n += 1
                            last = pe.matmul(PS[e][:, :], xt[a][:, k, bass.ds(t * P, P)], w[b][:, k, e * C:(e + 1) * C],
                                             start=False, stop=(n == 3 * KD), skip_group_check=True)
                    last.then_inc(y_psum[e], 1)

        @block.scalar
        def _(act):
            def high_weights(layer):
                act.wait_ge(w_in[layer], 16)
                act.activation(W[layer][1], W[layer][0], ACT.Copy, scale=WS).then_inc(w_high, 1)

            def transposed_nodes(f):
                act.wait_ge(var_ready, f + 1)
                act.activation(SD, VAR, ACT.Sqrt).then_inc(std_ready, 1)
                with act.Fori(0, HT) as it:
                    for s in range(2):
                        act.wait_ge(xn_transposed[s], f * HT + it + 2)
                        act.activation(XT[f][0][:, :, bass.ds((2 * it + s) * P, P)],
                                       PS[s][:, 0:KD * P].rearrange("p (k n) -> p k n", k=KD), ACT.Copy).then_inc(xh_ready[s], 1)

            high_weights(0)
            transposed_nodes(0)
            with act.Fori(0, NCH) as c:
                for o in range(KD):
                    act.wait_ge(h_psum[o], c + 1)
                    act.activation(HTh[:, o, bass.ds(c * C, C)], PS[2 + o][:, :], ACT.Copy, scale=1 / WS).then_inc(hh_ready[o], 1)
            with act.Fori(0, HT) as it:
                for s in range(2):
                    act.wait_ge(sup_psum[s], it + 1)
                    act.activation(SUP[:, 2 * it + s, :], PS[4 + s][:, 0:D], ACT.Copy, scale=1 / WS).then_inc(sup_copied[s], 1)

            def edge_exp(it, s):
                act.wait_ge(nmax_ready[s], it + 2)
                act.activation(PROB[s], PROB[s], ACT.Exp, bias=NMX[:, s:s + 1], accum_out=RSUM[:, s:s + 1]).then_inc(p_ready[s], 1)

            def edge_evacuate(it, s):
                for g in range(NCH):
                    act.wait_ge(pt_psum[g % 2], 2 * (2 * it + s) + g // 2 + 1)
                    if g == 0:
                        act.wait_ge(o_ready[s], it + 1)
                    act.activation(PROBT[s][:, g * C:(g + 1) * C], PS[4 + g % 2][:, :], ACT.Copy).then_inc(pt_ready[g % 2], 1)

            def mask_row(it, s):
                act.wait_ge(adj_in[s], 16 * (it + 1))
                act.wait_ge(nmax_ready[s], it + 1)
                act.wait_ge(mask_stored[s], 16 * it + 1)
                act.activation(MROW[s], ADJ[s], ACT.Copy, scale=-MASKED, bias=MASKED).then_inc(mask_ready[s], 1)

            for s in range(2):
                mask_row(0, s)
            act.wait_ge(z_neg, 1)
            act.activation(NATT[:, :], ZC[:, :], ACT.Exp, bias=zs[:, 2:3], accum_out=zs[:, 3:4]).then_inc(z_exp, 1)
            with act.Fori(0, HT - 1) as it:
                for s in range(2):
                    edge_exp(it, s)
                    edge_evacuate(it, s)
                    mask_row(it + 1, s)
            for s in range(2):
                edge_exp(HT - 1, s)
                edge_evacuate(HT - 1, s)

            high_weights(1)
            transposed_nodes(1)
            act.wait_ge(sh_ready, 1)
            act.activation(GW[:, :, 0:E], LG[:, :, 0:E], ACT.Exp).then_inc(ex_ready, 1)
            act.activation(GS[:, 3, :], LG[:, :, E], ACT.Exp, scale=-1.0).then_inc(ex_ready, 1)
            act.wait_ge(m_product, 1)
            act.activation(MM[0:ER, :], PS[3][0:ER, 0:D], ACT.Copy).then_inc(m_copied, 1)
            with act.Fori(0, NCH) as c:
                for o in range(0, E * KD, 2):
                    act.wait_ge(hid_psum[o % 4], 2 * c + o // 4 + 1)
                    act.activation(HID[:, o, :], PS[4 + o % 4][:, :], ACT.Relu, scale=1 / WS).then_inc(hid_ready[o % 4], 1)
                for u in range(TPC // 2):
                    for s in range(2):
                        act.wait_ge(lowt_psum[s], 2 * c + u + 2)
                        act.activation(LOWT[s][0:ER, :], PS[2 + s][0:ER, 0:P], ACT.Copy).then_inc(lowt_ready[s], 1)

            high_weights(2)
            transposed_nodes(2)
            with act.Fori(0, H // 2) as pair:
                for q in range(2):
                    act.wait_ge(qk_stored[q], 32 * pair + 1)
                    for c in range(NCH):
                        act.wait_ge(qk_psum[q], NCH * pair + c + 1)
                        act.activation(QKS[q][0][:, c * C:(c + 1) * C], PS[4 * q + c][:, :], ACT.Copy,
                                       scale=1 / WS).then_inc(qk_high[q], 1)
            with act.Fori(0, HT) as it:
                act.wait_ge(v_psum[0], it + 1)
                act.activation(V[:, 2 * it, :, 0:HD], PS[0][:, :].rearrange("p (h d) -> p h d", h=H), ACT.Copy,
                               scale=1 / WS).then_inc(v_read[0], 1)

            def max_row(s, n, g):
                act.wait_ge(rrow_psum, n + 1)
                act.activation(QL[s][HD:HD + 1, g * C:(g + 1) * C], PS[4][HD:HD + 1, :], ACT.Copy).then_inc(rrow_ready, 1)

            def exps(head, s, ic, row):
                u = head * NCH + ic
                for j in range(NT):
                    act.wait_ge(st_ready[j % 2], u * 8 + j // 2 + 1)
                    act.wait_ge(pv_done[j % 4], u * 4 + j // 4 + 1)
                    act.activation(PT[j % 4], PS[j % 2][:, :], ACT.Exp, scale=SCALE).then_inc(exp_done[j % 4], 1)
                    if j == 3 and row is not None:
                        max_row(s if ic == 0 else 1 - s, row, (ic + 3) % 4)

            for q in range(2):
                act.wait_ge(qk_stored[q], 32 * H // 2 + 1)
            for g in range(NCH - 1):
                max_row(0, g, g)
            with act.Fori(0, H // 2 - 1) as pair:
                for s in range(2):
                    for ic in range(NCH):
                        exps(2 * pair + s, s, ic, (2 * pair + s) * NCH + ic + 3)
            for s in range(2):
                for ic in range(NCH):
                    row = (H - 2 + s) * NCH + ic + 3
                    exps(H - 2 + s, s, ic, row if row < H * NCH else None)
            with act.Fori(0, HT) as it:
                for s in range(2):
                    act.wait_ge(at_psum[s], it + 2)
                    act.wait_ge(wo_psum[s], it + 1)
                    act.activation(ATTT[s], PS[s][:, :], ACT.Copy).then_inc(at_ready[s], 1)

            high_weights(3)
            transposed_nodes(3)
            act.wait_ge(eb_in, 16)
            act.wait_ge(eb_zero, 1)
            act.activation(BB[0:1, :], BSTAGE[0:1, :], ACT.Copy, scale=WS).then_inc(eb_high, 1)
            act.wait_ge(sh_ready, 2)
            act.activation(GW[:, :, 0:NE], LG[:, :, 0:NE], ACT.Exp).then_inc(ex_ready, 1)

        @block.vector
        def _(dve):
            own = Tally(dve, dve_done)

            def take_waits(n):
                dve.memset(idle_cells[:, n:n + 1], 0.0)

            tt, ts, stt = dve.tensor_tensor, dve.tensor_scalar, dve.scalar_tensor_tensor

            def low_weights(layer):
                dve.wait_ge(w_high, layer + 1)
                stt(out=W[layer][2], in0=W[layer][0], scalar=WS, in1=W[layer][1], op0=ALU.mult,
                    op1=ALU.subtract).then_inc(w_low, 1)

            def layernorm(f):
                with own.loop(NT, 1) as t:
                    own.add(dve.bn_stats(STATS[:, t, :], X[:, t, :]))
                own.wait()
                me, ve, mo, vo = (STATS[:, :, i] for i in (1, 2, 4, 5))
                own.add(tt(MEAN, me, mo, ALU.add))
                own.add(tt(TA, me, mo, ALU.subtract))
                own.add(tt(TB, ve, vo, ALU.add))
                own.wait()
                own.add(ts(MEAN, MEAN, 0.5, None, ALU.mult))
                own.add(tt(TA, TA, TA, ALU.mult))
                own.add(ts(TB, TB, 1.0 / D, EPS, ALU.mult, ALU.add))
                own.wait()
                stt(out=VAR, in0=TA, scalar=0.25, in1=TB, op0=ALU.mult, op1=ALU.add).then_inc(var_ready, 1)
                dve.wait_ge(std_ready, f + 1)
                own.add(dve.reciprocal(RSTD, SD))
                own.wait()
                own.add(tt(TA, RSTD, RSTD, ALU.mult))
                own.wait()
                own.add(tt(TA, TA, VAR, ALU.mult))
                own.wait()
                own.add(ts(TA, TA, -0.5, 1.5, ALU.mult, ALU.add))
                own.wait()
                own.add(tt(RSTD, RSTD, TA, ALU.mult))
                own.wait()
                with dve.Fori(0, HT) as it:
                    for s in range(2):
                        t = 2 * it + s
                        dve.wait_ge(xn_transposed[s], f * HT + it + 1)
                        ts(XN[s][:, :], X[:, t, :], MEAN[:, bass.ds(t, 1)], RSTD[:, bass.ds(t, 1)], ALU.subtract,
                           ALU.mult).then_inc(xn_ready[s], 1)
                    for s in range(2):
                        cols = bass.ds((2 * it + s) * P, P)
                        dve.wait_ge(xh_ready[s], f * HT + it + 1)
                        tt(XT[f][1][:, :, cols], PS[s][:, 0:KD * P].rearrange("p (k n) -> p k n", k=KD), XT[f][0][:, :, cols],
                           ALU.subtract).then_inc(xl_ready[s], 1)

            dve.wait_ge(ident_ready, 2)
            own.add(dve.tensor_copy(identb[:, :], identf[:, :]))
            own.add(ts(not_eye[:, :], identf[:, :], -1.0, 1.0, ALU.mult, ALU.add))
            own.add(ts(eye_a[:, :], identf[:, :], EYE_A, None, ALU.mult))
            ts(eye_b[:, :], identf[:, :], EYE_B, None, ALU.mult).then_inc(consts_ready, 1)

            dve.wait_ge(x_in, 16)
            low_weights(0)
            layernorm(0)
            with dve.Fori(0, NCH) as c:
                for o in range(KD):
                    cols = bass.ds(c * C, C)
                    dve.wait_ge(hh_ready[o], c + 1)
                    stt(out=HTl[:, o, cols], in0=PS[2 + o][:, :], scalar=1 / WS, in1=HTh[:, o, cols], op0=ALU.mult,
                        op1=ALU.subtract).then_inc(hl_ready[o], 1)
            with dve.Fori(0, HT) as it:
                for s in range(2):
                    dve.wait_ge(sup_copied[s], it + 1)
                    ts(ZC[:, bass.ds(2 * it + s, 1)], PS[4 + s][:, D:D + 1], 1 / WS, None, ALU.mult).then_inc(z_copied[s], 1)
            dve.wait_ge(small_in, 32)
            with own.loop(NT, 1) as t:
                own.add(tt(X[:, t, :], X[:, t, :], gbias[:, :], ALU.add))
            for s in range(2):
                dve.wait_ge(z_copied[s], HT + 1)
            dve.tensor_reduce(zs[:, 0:1], ZC[:, :], AX.X, ALU.max).then_inc(z_max, 1)
            dve.wait_ge(z_allmax, 1)
            ts(zs[:, 2:3], zs[:, 1:2], -1.0, None, ALU.mult).then_inc(z_neg, 1)
            dve.wait_ge(z_sum, 1)
            own.add(dve.reciprocal(zs[:, 5:6], zs[:, 4:5]))
            own.wait()
            own.add(ts(NATT[:, :], NATT[:, :], zs[:, 5:6], None, ALU.mult))
            own.wait()

            def edge_max(it, s, t):
                for c in range(NCH):
                    dve.wait_ge(e_ready[c], t + 1)
                    if c == 0:
                        dve.wait_ge(mask_ready[s], it + 2)
                        dve.wait_ge(o_ready[s], it + 1)
                    take_waits(c)
                    dve.tensor_tensor_reduce(out=PROB[s][:, c * C:(c + 1) * C], in0=PS[c][:, :], in1=MROW[s][:, c * C:(c + 1) * C],
                                             scale=1.0, scalar=-3e38, op0=ALU.add, op1=ALU.max,
                                             accum_out=MX[:, s, c:c + 1]).then_inc(e_read[c], 1)
                dve.wait_ge(e_read[NCH - 1], t + 2)
                own.add(dve.tensor_reduce(RSC[:, 2:3], MX[:, s, :], AX.X, ALU.max))
                own.wait()
                ts(NMX[:, s:s + 1], RSC[:, 2:3], -1.0, None, ALU.mult).then_inc(nmax_ready[s], 1)

            def edge_update(it, s, t):
                dve.wait_ge(o_ready[s], it + 2)
                own.add(dve.reciprocal(RSC[:, 0:1], RSUM[:, s:s + 1]))
                own.wait()
                own.add(tt(RSC[:, 1:2], RSC[:, 0:1], NATT[:, bass.ds(t, 1)], ALU.mult))
                own.wait()
                stt(out=X[:, t, :], in0=PS[6 + s][:, 0:D], scalar=RSC[:, 1:2], in1=X[:, t, :], op0=ALU.mult,
                    op1=ALU.add).then_inc(o_read[s], 1)

            edge_max(0, 0, 0)
            with own.loop(HT - 1, 6) as it:
                edge_max(it, 1, 2 * it + 1)
                edge_update(it, 0, 2 * it)
                edge_max(it + 1, 0, 2 * it + 2)
                edge_update(it, 1, 2 * it + 1)
            edge_max(HT - 1, 1, NT - 1)
            edge_update(HT - 1, 0, NT - 2)
            edge_update(HT - 1, 1, NT - 1)
            for s in range(2):
                dve.wait_ge(o_read[s], HT + 1)
            for s in range(2):
                dve.wait_ge(mask_stored[s], 16 * HT + 1)
            with dve.Fori(0, NT) as t:
                last = tt(MASK[:, t, bass.ds(t * P, P)], MASK[:, t, bass.ds(t * P, P)], not_eye[:, :], ALU.mult)
                last.then_inc(dve_done, 1)
            own.n = own.n + NT
            own.wait()
            dve.nop().then_inc(x_ready, 1)
            low_weights(1)
            layernorm(1)
            dve.wait_ge(lg_ready, NT)

            def softmax_shift(n, bias):
                lg, ps = LG[:, :, 0:n], PS[2 if n == E else 4]
                cols = n + (n == E)
                own.add(ts(LG[:, :, 0:cols], ps[:, 0:NT * cols].rearrange("p (t e) -> p t e", e=cols), 1 / WS, None, ALU.mult))
                own.wait()
                if bias is not None:
                    own.add(tt(lg, lg, bias.unsqueeze(1).to_broadcast([P, NT, n]), ALU.add))
                    own.wait()
                own.add(dve.tensor_reduce(GS[:, 0, :], lg, AX.X, ALU.max))
                own.wait()
                tt(lg, lg, GS[:, 0, :].unsqueeze(2).to_broadcast([P, NT, n]), ALU.subtract).then_inc(sh_ready, 1)

            def softmax_divide(n):
                own.add(dve.tensor_reduce(GS[:, 0, :], GW[:, :, 0:n], AX.X, ALU.add))
                own.wait()
                own.add(dve.reciprocal(GS[:, 1, :], GS[:, 0, :]))
                own.wait()
                own.add(tt(GW[:, :, 0:n], GW[:, :, 0:n], GS[:, 1, :].unsqueeze(2).to_broadcast([P, NT, n]), ALU.mult))
                own.wait()

            softmax_shift(E, None)
            dve.wait_ge(ex_ready, 2)
            softmax_divide(E)
            own.add(ts(GS[:, 3, :], GS[:, 3, :], 1.0, None, ALU.add))
            own.wait()
            own.add(dve.reciprocal(GS[:, 2, :], GS[:, 3, :]))
            own.wait()
            own.add(ts(GS[:, 2, :], GS[:, 2, :], 1.0 / E, None, ALU.mult))
            own.wait()
            own.add(tt(GW[:, :, 0:E], GW[:, :, 0:E], GS[:, 2, :].unsqueeze(2).to_broadcast([P, NT, E]), ALU.subtract))
            own.wait()
            own.add(ts(GW[:, :, 0:E], GW[:, :, 0:E], 0.0, None, ALU.max))
            own.wait()
            own.add(dve.tensor_reduce(GS[:, 0, :], GW[:, :, 0:E], AX.X, ALU.add))
            own.wait()
            own.add(ts(GS[:, 1, :], GS[:, 0, :], 0.0, None, ALU.is_equal))
            own.wait()
            own.add(tt(GS[:, 0, :], GS[:, 0, :], GS[:, 1, :], ALU.add))
            own.wait()
            own.add(dve.reciprocal(GS[:, 1, :], GS[:, 0, :]))
            own.wait()
            own.add(tt(GW[:, :, 0:E], GW[:, :, 0:E], GS[:, 1, :].unsqueeze(2).to_broadcast([P, NT, E]), ALU.mult))
            own.wait()
            dve.wait_ge(bt_zero, 3)
            with dve.Fori(0, NCH) as c:
                for o in range(1, E * KD, 2):
                    dve.wait_ge(hid_psum[o % 4], 2 * c + o // 4 + 1)
                    ts(HID[:, o, :], PS[4 + o % 4][:, :], 1 / WS, 0.0, ALU.mult, ALU.max).then_inc(hid_ready[o % 4], 1)
                for u in range(TPC // 2):
                    for s in range(2):
                        t = c * TPC + 2 * u + s
                        dve.wait_ge(low_psum[s], 2 * c + u + 1)
                        dve.wait_ge(lowt_psum[s], 2 * c + u + 1)
                        tt(LOW[s][:, 0:ER].rearrange("p (e r) -> p e r", e=E), PS[s][:, 0:ER].rearrange("p (e r) -> p e r", e=E),
                           GW[:, t, 0:E].unsqueeze(2).to_broadcast([P, E, R]), ALU.mult).then_inc(low_ready[s], 1)
                    for s in range(2):
                        t = c * TPC + 2 * u + s
                        dve.wait_ge(f0_psum[s], 2 * c + u + 1)
                        tt(X[:, t, :], PS[s][:, 0:D], X[:, t, :], ALU.add).then_inc(f0_read[s], 1)
            for s in range(2):
                dve.wait_ge(f0_read[s], HT + 1)
            dve.nop().then_inc(x_ready, 1)
            low_weights(2)
            layernorm(2)
            with dve.Fori(0, H // 2) as pair:
                for q in range(2):
                    dve.wait_ge(qk_stored[q], 32 * pair + 1)
                    for c in range(NCH):
                        b = 4 * q + c
                        dve.wait_ge(qk_high[q], NCH * pair + c + 1)
                        stt(out=QKS[q][1][:, c * C:(c + 1) * C], in0=PS[b][:, :], scalar=1 / WS, in1=QKS[q][0][:, c * C:(c + 1) * C],
                            op0=ALU.mult, op1=ALU.subtract).then_inc(qk_low[q], 1)
            with dve.Fori(0, HT) as it:
                dve.wait_ge(v_psum[1], it + 1)
                ts(V[:, 2 * it + 1, :, 0:HD], PS[1][:, :].rearrange("p (h d) -> p h d", h=H), 1 / WS, None,
                   ALU.mult).then_inc(v_read[1], 1)

            def row_max(n, g):
                for q in range(NT):
                    b, i, c = q % 2, g * TPC + q // NCH, q % NCH
                    dve.wait_ge(rmax_psum[b], n * 8 + q // 2 + 1)
                    take_waits(q)
                    dve.tensor_tensor_reduce(out=MJUNK[b], in0=PS[5 + b][:, :], in1=MASK[:, i, c * C:(c + 1) * C],
                                             scale=1.0, scalar=-3e38, op0=ALU.add, op1=ALU.max,
                                             accum_out=MQ[:, q // NCH, c:c + 1]).then_inc(rmax_read[b], 1)
                dve.wait_ge(rmax_read[1], n * 8 + 9)
                dve.tensor_reduce(MR[:, :], MQ[:, :, :], AX.X, ALU.max).then_inc(rmax_ready, 1)
                dve.wait_ge(rmax_ready, n + 1)
                ts(MNEG[:, g % 2, :], MR[:, :], -1.0, None, ALU.mult).then_inc(rneg_ready, 1)

            def normalise(head, ic):
                u = head * NCH + ic
                dve.wait_ge(pv_done[3], u * 4 + 5)
                o = PS[2 + ic % 2][:, 0:TPC * (HD + 1)].rearrange("p (q d) -> p q d", q=TPC)
                dve.reciprocal(RD[:, ic % 2, :], o[:, :, HD]).then_inc(rden_ready, 1)
                dve.wait_ge(rden_ready, u + 1)
                tt(ATT[:, ic * TPC:(ic + 1) * TPC, bass.ds(head * HD, HD)], o[:, :, 0:HD],
                   RD[:, ic % 2, :].unsqueeze(2).to_broadcast([P, TPC, HD]), ALU.mult).then_inc(att_read[ic % 2], 1)

            for g in range(NCH):
                if g >= 2:
                    dve.wait_ge(rrow_psum, g - 1)
                row_max(g, g)
            with dve.Fori(0, H // 2 - 1) as pair:
                for s in range(2):
                    for ic in range(NCH):
                        head = 2 * pair + s
                        dve.wait_ge(rrow_psum, head * NCH + ic + 3)
                        row_max((head + 1) * NCH + ic, ic)
                        normalise(head, ic)
            for s in range(2):
                for ic in range(NCH):
                    head = H - 2 + s
                    if s == 0:
                        dve.wait_ge(rrow_psum, head * NCH + ic + 3)
                        row_max((head + 1) * NCH + ic, ic)
                    normalise(head, ic)
            with dve.Fori(0, HT) as it:
                for s in range(2):
                    t = 2 * it + s
                    dve.wait_ge(wo_psum[s], it + 2)
                    tt(X[:, t, :], PS[2 + s][:, 0:D], X[:, t, :], ALU.add).then_inc(wo_read[s], 1)
            for s in range(2):
                dve.wait_ge(wo_read[s], HT + 1)
            dve.nop().then_inc(x_ready, 1)
            low_weights(3)
            layernorm(3)
            dve.wait_ge(eb_high, 1)
            dve.wait_ge(eb_zero, 1)
            own.add(ts(BSTAGE[32:33, :], BSTAGE[0:1, :], WS, None, ALU.mult))
            own.add(dve.tensor_copy(BSTAGE[64:65, :], BB[0:1, :]))
            own.wait()
            own.add(tt(BB[32:33, :], BSTAGE[32:33, :], BSTAGE[64:65, :], ALU.subtract))
            own.wait()
            dve.nop().then_inc(eb_low, 1)
            dve.wait_ge(lg_ready, 2 * NT)
            softmax_shift(NE, mbias[:, :])
            dve.wait_ge(ex_ready, 3)
            softmax_divide(NE)
            own.add(ts(GW[:, :, 0:NE], GW[:, :, 0:NE], 1 / WS, None, ALU.mult))
            own.wait()
            with own.loop(NT, NE // 2) as t:
                for e in range(NE):
                    if e % 2 == 0:
                        dve.wait_ge(y_psum[e // 2], t + 1)
                    ins = stt(out=X[:, t, :], in0=PS[e // 2][:, (e % 2) * D:(e % 2 + 1) * D], scalar=GW[:, t, e:e + 1],
                              in1=X[:, t, :], op0=ALU.mult, op1=ALU.add)
                    if e % 2 == 0:
                        own.add(ins)
                        own.wait()
                    else:
                        ins.then_inc(y_read[e // 2], 1)
                        dve.wait_ge(y_read[e // 2], t + 2)
                dve.nop().then_inc(y_tile, 1)


def kernel(x, adj, L0_gnn_weight, L0_gnn_bias, L0_gnn_node_w, L0_gnn_edge_w, L0_ffn_gate_w, L0_ffn_thr_w, L0_ffn_fc1_w,
           L0_ffn_lora_A, L0_ffn_lora_B, L0_ffn_fc2_w, L1_gnn_Wks, L1_gnn_Wqs, L1_gnn_Wvs, L1_gnn_Wo,
           L1_ffn_expert_weights, L1_ffn_expert_biases, L1_ffn_mixer_w, L1_ffn_mixer_b):
    import concourse.bacc as bacc
    from concourse.bass_utils import run_bass_kernel_spmd

    def heads(w):
        w = np.asarray(w).transpose(1, 0, 2)
        return w.reshape(w.shape[0], -1)

    def by_input(w):
        w = np.asarray(w).transpose(2, 0, 1)
        return w.reshape(w.shape[0], -1)

    def side_by_side(*ws):
        return np.concatenate([np.asarray(w) for w in ws], axis=1)

    wo = np.asarray(L1_gnn_Wo)
    arrays = {
        "x": x, "adj": adj, "w_gnn0": side_by_side(L0_gnn_edge_w, L0_gnn_weight, L0_gnn_node_w), "g_bias": L0_gnn_bias,
        "w_ffn0": side_by_side(by_input(L0_ffn_fc1_w), np.asarray(L0_ffn_gate_w).T, np.asarray(L0_ffn_thr_w).T),
        "lora_a": L0_ffn_lora_A, "lora_bt": np.asarray(L0_ffn_lora_B).transpose(0, 2, 1),
        "fc2": np.asarray(L0_ffn_fc2_w).transpose(0, 2, 1),
        "w_gnn1": side_by_side(heads(L1_gnn_Wqs), heads(L1_gnn_Wks), heads(L1_gnn_Wvs)), "wo": wo.reshape(-1, wo.shape[2]),
        "w_ffn1": side_by_side(by_input(L1_ffn_expert_weights), np.asarray(L1_ffn_mixer_w).T),
        "expert_biases": L1_ffn_expert_biases, "mixer_b": L1_ffn_mixer_b,
    }
    arrays = {name: np.ascontiguousarray(a) for name, a in arrays.items()}
    nc = bacc.Bacc("TRN2", target_bir_lowering=False, num_devices=1)
    ins = {name: nc.dram_tensor(name, a.shape, mybir.dt.from_np(a.dtype), kind="ExternalInput").ap()
           for name, a in arrays.items()}
    out = nc.dram_tensor("y", arrays["x"].shape, F32, kind="ExternalOutput").ap()
    gnn_moe_program(nc, **ins, out=out)
    r = run_bass_kernel_spmd(nc, [arrays], core_ids=[0])
    return r.results[0]["y"]
```

```python
from contextlib import ExitStack, contextmanager

import numpy as np

import concourse.bass as bass
from concourse import mybir

F32 = mybir.dt.float32
F16 = mybir.dt.float16
BF16 = mybir.dt.bfloat16
ALU = mybir.AluOpType
ACT = mybir.ActivationFunctionType
AX = mybir.AxisListType
RMAX = bass.bass_isa.ReduceOp.max
RADD = bass.bass_isa.ReduceOp.add

P = 128


class Tally:

    def __init__(self, eng, sem):
        self.eng, self.sem, self.n = eng, sem, 0

    def add(self, ins):
        ins.then_inc(self.sem, 1)
        self.n = self.n + 1
        return ins

    def wait(self):
        self.eng.wait_ge(self.sem, self.n)

    @contextmanager
    def loop(self, count, per):
        start = self.n
        with self.eng.Fori(0, count) as i:
            self.n = start + i * per
            yield i
        self.n = start + count * per


def product_pair(value):
    a = np.arange(1024, 2048, dtype=np.float64) / 1024
    b = (value / a).astype(np.float16).astype(np.float64)
    n = int(np.argmin(np.abs(a * b - value)))
    return float(a[n]), float(b[n])


def gnn_moe_program(nc, x, adj, w_gnn0, g_bias, w_ffn0, lora_a, lora_bt, fc2, w_gnn1, wo, w_ffn1, expert_biases, mixer_b, out):
    N, D = x.shape
    NT = N // P
    HT = NT // 2
    QT = NT // 4
    KD = D // P
    C = 512
    NCH = N // C
    TPC = C // P
    E, _, R = lora_a.shape
    ER = E * R
    HD = 64
    H = wo.shape[0] // HD
    NE = expert_biases.shape[0]
    EPS = 1e-5
    WS = 64.0
    MASKED = -1e16
    SCALE = float(HD) ** -0.5
    EYE_A, EYE_B = product_pair(0.01 / SCALE)

    with ExitStack() as ctx:
        def sem(name):
            return ctx.enter_context(nc.semaphore(name))

        def sems(name, n):
            return [sem(f"{name}{i}") for i in range(n)]

        def sb(name, shape, dt=F32):
            return ctx.enter_context(nc.sbuf_tensor(name, shape, dt))

        X = sb("X", [P, NT, D])
        MASK = sb("MASK", [P, NT, N], BF16)
        arena = sb("arena", [P, 121 * 256])

        def area(kib, words, dt=F32):
            a = arena[:, int(kib * 256):int(kib * 256) + words]
            return a if dt == F32 else a.bitcast(dt)

        def xt_area(kib):
            return area(kib, KD * N, F16).rearrange("p (h k n) -> p h k n", h=2, k=KD)

        xt_low = xt_area(0)
        XT = [(xt_low[:, 0], xt_low[:, 1])] * 3 + [(xt_area(81)[:, 0], xt_area(81)[:, 1])]

        def weights(kib_stage, kib_parts, cols):
            stage = area(kib_stage, KD * cols).rearrange("p (k n) -> p k n", k=KD)
            parts = area(kib_parts, KD * cols, F16).rearrange("p (h k n) -> p h k n", h=2, k=KD)
            return stage, parts[:, 0], parts[:, 1]

        W_COLS = [D + D + 1, E * D + E + 1, 3 * H * HD, NE * D + NE]
        W_AT = [(104, 109), (104, 112.25), (83, 49), (16, 33)]
        W = [weights(*W_AT[i], W_COLS[i]) for i in range(4)]

        ht = area(16, KD * N, F16).rearrange("p (h k n) -> p h k n", h=2, k=KD)
        HTh, HTl = ht[:, 0], ht[:, 1]
        SUP = area(32, NT * D).rearrange("p (t n) -> p t n", t=NT)
        PROB = [area(48 + 8 * s, N) for s in range(2)]
        PROBT = [area(64 + 8 * s, N) for s in range(2)]
        ADJ = [area(80 + 8 * s, N) for s in range(2)]
        MROW = [area(96 + 4 * s, N // 2, BF16) for s in range(2)]
        HID = area(16, E * KD * C).rearrange("p (o n) -> p o n", o=E * KD)
        FC2 = area(66, E * KD * D).rearrange("p (o n) -> p o n", o=E * KD)
        BT = area(74, E * KD * ER).rearrange("p (o n) -> p o n", o=E * KD)
        LA = area(76, E * KD * ER).rearrange("p (o n) -> p o n", o=E * KD)
        MM = area(78, D)
        LOWT = area(79, C)
        GX = area(32, NT * P).rearrange("p (t n) -> p t n", t=NT)
        GT = area(40, N)
        VW = 2 * HD + 1
        V = area(16.25, NT * H * VW // 2, F16).rearrange("p (t h d) -> p t h d", t=NT, h=H)
        QKS = [[area(97 + 8 * s + 4 * q, N // 2, F16) for q in range(2)] for s in range(2)]
        ATT = area(49, NT * H * HD).rearrange("p (t n) -> p t n", t=NT)
        KS, QD, QL, KO = ([area(81 + 16 * s + 4 * q, N // 2, F16) for s in range(2)] for q in range(4))
        PF = [area(113 + 2 * s, C) for s in range(4)]
        PH = [area(s, C // 2, F16) for s in range(4)]
        PL = [area(4 + s, C // 2, F16) for s in range(4)]
        MJUNK = [area(12 + b, C // 2, BF16) for b in range(2)]
        MJUNK0 = [area(66 + b, C // 2, BF16) for b in range(2)]
        ATS = [area(0 + 2 * s, C) for s in range(2)]
        ATTT = [area(4 + 2 * s, C) for s in range(2)]
        WO = area(8, H * HD // P * D).rearrange("p (k n) -> p k n", k=H * HD // P)
        BB = area(50, NE * D // 2, F16)
        BSTAGE = area(54, NE * D)

        XN = [area(62 + 2 * s, 2 * D).rearrange("p (t d) -> p t d", t=2) for s in range(2)]
        identf = sb("identf", [P, P])
        identb = sb("identb", [P, P], BF16)
        not_eye = sb("not_eye", [P, P], BF16)
        eye_a = sb("eye_a", [P, P], F16)
        eye_b = sb("eye_b", [P, P], F16)
        ones = sb("ones", [P, P], F16)
        gbias = area(114, D)
        mbias = sb("mbias", [P, NE])
        STATS = sb("STATS", [P, NT, 6])
        small = sb("small", [P, 6, NT])
        MEAN, VAR, RSTD, SD, TA, TB = (small[:, i, :] for i in range(6))
        ZC = sb("ZC", [P, NT])
        NATT = sb("NATT", [P, NT])
        zs = sb("zs", [P, 8])
        MX = sb("MX", [P, 2, NCH])
        NMX = sb("NMX", [P, 2])
        RSUM = sb("RSUM", [P, 2])
        RSC = sb("RSC", [P, 4])
        LG = sb("LG", [P, NT, 8])
        GW = sb("GW", [P, NT, 8])
        GS = sb("GS", [P, 4, NT])
        MQ = sb("MQ", [P, TPC, NCH])
        MQ0 = sb("MQ0", [P, TPC * (NCH - 1), NCH])
        MR = sb("MR", [P, TPC])
        MNEG = sb("MNEG", [P, 2, TPC])
        RD = sb("RD", [P, TPC])
        OC = area(14, TPC * VW).rearrange("p (q d) -> p q d", q=TPC)
        idle_cells = sb("idle_cells", [P, NT])
        ST_BANKS, O_BANKS, MAX_BANKS = (0, 1, 4, 7), (2, 3), (5, 6)
        QK = nc.dram_tensor("qk_scratch", [2, 2, H, HD, N], F16).ap()

        PS = [ctx.enter_context(nc.psum_tensor(f"PS{b}", [P, C], F32)) for b in range(8)]

        dve_done = sem("dve_done")
        x_in, small_in = sem("x_in"), sem("small_in")
        w_in, w_high, w_low = sem("w_in"), sem("w_high"), sem("w_low")
        ident_zero, ident_ready, consts_ready = sem("ident_zero"), sem("ident_ready"), sem("consts_ready")
        var_ready, std_ready = sem("var_ready"), sem("std_ready")
        xn_ready, xn_transposed = sems("xn_ready", 2), sems("xn_transposed", 2)
        xh_ready, xl_ready = sems("xh_ready", 2), sems("xl_ready", 2)
        h_psum, hh_ready, hl_ready = sems("h_psum", 2), sems("hh_ready", 2), sems("hl_ready", 2)
        sup_psum, sup_copied, z_copied = sems("sup_psum", 2), sems("sup_copied", 2), sems("z_copied", 2)
        z_max, z_allmax, z_neg, z_exp, z_sum = (sem(f"z_{n}") for n in ("max", "allmax", "neg", "exp", "sum"))
        adj_in, mask_ready, mask_stored = sems("adj_in", 2), sems("mask_ready", 2), sems("mask_stored", 2)
        e_ready, e_read = sems("e_ready", NCH), sems("e_read", NCH)
        nmax_ready, p_ready = sems("nmax_ready", 2), sems("p_ready", 2)
        pt_psum, pt_ready = sems("pt_psum", 2), sems("pt_ready", 2)
        o_ready, o_read = sems("o_ready", 2), sems("o_read", 2)
        x_ready, bias_added, eye_cleared = sem("x_ready"), sem("bias_added"), sem("eye_cleared")
        bt_zero, f0_in = sem("bt_zero"), sem("f0_in")
        lg_ready, sh_ready, ex_ready = sem("lg_ready"), sem("sh_ready"), sem("ex_ready")
        m_product, m_copied = sem("m_product"), sem("m_copied")
        hid_psum, hid_ready = sems("hid_psum", 4), sems("hid_ready", 4)
        low_psum, low_ready = sem("low_psum"), sem("low_ready")
        gx_ready, gt_psum, gt_ready = sem("gx_ready"), sems("gt_psum", 2), sem("gt_ready")
        f0_psum, f0_read = sems("f0_psum", 2), sems("f0_read", 2)
        v_ones, v_psum, v_read = sem("v_ones"), sems("v_psum", 2), sems("v_read", 2)
        qk_psum, qk_high, qk_low, qk_stored = sem("qk_psum"), sem("qk_high"), sems("qk_low", 2), sems("qk_stored", 2)
        stack_in, row_ones = sems("stack_in", 2), sem("row_ones")
        rmax_psum, rmax_read = sems("rmax_psum", 2), sems("rmax_read", 2)
        rmax_ready, rneg_ready, rrow_psum, rrow_ready = (sem(n) for n in ("rmax_ready", "rneg_ready", "rrow_psum", "rrow_ready"))
        st_ready, exp_done, pv_done = sems("st_ready", 4), sems("exp_done", 4), sems("pv_done", 4)
        pl_ready, att_ready = sems("pl_ready", 4), sem("att_ready")
        v_high = sems("v_high", 2)
        rden_ready, att_read, halves_added = sem("rden_ready"), sems("att_read", 2), sem("halves_added")
        wo_in, att_copied, at_psum, at_ready = sem("wo_in"), sems("att_copied", 2), sems("at_psum", 2), sems("at_ready", 2)
        wo_psum, wo_read = sems("wo_psum", 2), sems("wo_read", 2)
        eb_in, eb_zero, eb_high, eb_low = sem("eb_in"), sem("eb_zero"), sem("eb_high"), sem("eb_low")
        y_psum, y_read, y_tile = sem("y_psum"), sems("y_read", 4), sem("y_tile")
        stored = sem("stored")

        start_at_one = [*mask_ready, *xn_transposed, *xl_ready, *hl_ready, *z_copied, *e_read, *pt_ready, *o_read, *o_ready,
                        *mask_stored, *nmax_ready, *hid_ready, *f0_read, *qk_low, *qk_stored, *v_read, *rmax_read, *exp_done,
                        *att_read, att_ready, *pv_done, *at_psum, *at_ready, *wo_read, *wo_psum, *y_read, low_ready]

        block = ctx.enter_context(nc.Block())
        x_tiles = x.rearrange("(t p) d -> p t d", p=P)
        out_tiles = out.rearrange("(t p) d -> p t d", p=P)
        adj_tiles = adj.rearrange("(t p) n -> t p n", p=P)

        LAG = 3
        SHIFT = 7
        ROW_AT = SHIFT + 2

        def maxima_piece(ic, j):
            if j < SHIFT:
                return 3, ic > 0, (ic - 1) % NCH, NT - SHIFT + j
            return 4, True, ic, j - SHIFT

        @block.sync
        def _(sp):
            def load_weights(layer, w):
                sp.dma_start(W[layer][0], w.rearrange("(k p) n -> p k n", p=P)).then_inc(w_in, 16)

            sp.dma_start(X[:, :, :], x_tiles).then_inc(x_in, 16)
            load_weights(0, w_gnn0)
            sp.dma_start(gbias[:, :], g_bias.rearrange("(a d) -> a d", a=1).to_broadcast([P, D])).then_inc(small_in, 16)
            sp.dma_start(mbias[:, :], mixer_b.rearrange("(a d) -> a d", a=1).to_broadcast([P, NE])).then_inc(small_in, 16)

            def adjacency(it):
                for s in range(2):
                    sp.wait_ge(mask_ready[s], it + 1)
                    sp.dma_start(ADJ[s], adj_tiles[2 * it + s, :, :]).then_inc(adj_in[s], 16)
                for s in range(2):
                    sp.wait_ge(mask_ready[s], it + 2)
                    sp.dma_start(MASK[:, 2 * it + s, :], MROW[s]).then_inc(mask_stored[s], 16)

            adjacency(0)
            sp.wait_ge(z_max, 1)
            sp.wait_ge(bias_added, 1)
            load_weights(1, w_ffn0)
            with sp.Fori(1, HT) as it:
                adjacency(it)

            sp.wait_ge(x_ready, 1)
            sp.dma_start(FC2, fc2.rearrange("e (k p) d -> p (e k) d", p=P)).then_inc(f0_in, 16)
            sp.wait_ge(bt_zero, 2)
            for e in range(E):
                sp.dma_start(LA[:, e * KD:(e + 1) * KD, e * R:(e + 1) * R],
                             lora_a[e].rearrange("(k p) r -> p k r", p=P)).then_inc(f0_in, 16)
                sp.dma_start(BT[:, e * KD:(e + 1) * KD, e * R:(e + 1) * R],
                             lora_bt[e].rearrange("(k p) r -> p k r", p=P)).then_inc(f0_in, 16)

            load_weights(2, w_gnn1)
            def store_pair(pair):
                for q in range(2):
                    sp.wait_ge(qk_low[q], NCH * pair + NCH + 1)
                    for part in range(2):
                        sp.dma_start(QK[q, part, bass.ds(2 * pair, 2), :, :].rearrange("h d n -> (h d) n"),
                                     QKS[q][part]).then_inc(qk_stored[q], 16)

            def load_stack(h, s):
                for tile, at, q, part in ((KS, 0, 1, 0), (KS, HD, 1, 1), (QD, 0, 0, 0), (QD, HD, 0, 0),
                                          (QL, 0, 0, 1), (KO, 0, 1, 0)):
                    sp.dma_start(tile[s][at:at + HD, :], QK[q, part, h, :, :]).then_inc(stack_in[s], 16)

            store_pair(0)
            for q in range(2):
                sp.wait_ge(qk_stored[q], 33)
            load_stack(0, 0)
            with sp.Fori(1, H // 2) as pair:
                store_pair(pair)
            for q in range(2):
                sp.wait_ge(qk_stored[q], 32 * H // 2 + 1)
            load_stack(1, 1)
            with sp.Fori(1, H // 2) as pair:
                for s in range(2):
                    sp.wait_ge(st_ready[3], 32 * pair + 16 * s - 16)
                    load_stack(2 * pair + s, s)

            sp.dma_start(WO, wo.rearrange("(k p) n -> p k n", p=P)).then_inc(wo_in, 16)
            sp.wait_ge(pv_done[3], 16 * H + 1)
            sp.wait_ge(att_ready, NCH * H + 1)
            load_weights(3, w_ffn1)
            sp.wait_ge(x_ready, 3)
            sp.dma_start(BSTAGE[0:1, :], expert_biases.rearrange("k d -> (k d)").rearrange("(a n) -> a n", a=1)).then_inc(eb_in, 16)
            with sp.Fori(0, NT) as t:
                sp.wait_ge(y_tile, t + 1)
                sp.dma_start(out_tiles[:, t, :], X[:, t, :]).then_inc(stored, 16)
            sp.wait_ge(stored, 16 * NT)

        @block.gpsimd
        def _(pool):
            for first in start_at_one:
                pool.sem_inc(first, 1)
            nc.gpsimd.memset(identf[:, :], 0.0).then_inc(ident_zero, 1)
            pool.wait_ge(ident_zero, 1)
            nc.gpsimd.affine_select(out=identf[:, :], in_=identf[:, :], compare_op=ALU.not_equal, fill=1.0, base=0,
                                    pattern=[[-1, P]], channel_multiplier=1).then_inc(ident_ready, 1)
            nc.gpsimd.memset(ones[:, :], 1.0).then_inc(ident_ready, 1)
            pool.wait_ge(small_in, 32)
            for s in range(2):
                pool.wait_ge(xn_transposed[s], QT + 1)
            nc.gpsimd.tensor_tensor(X[:, :, :], X[:, :, :], gbias[:, :].unsqueeze(1).to_broadcast([P, NT, D]),
                                    ALU.add).then_inc(bias_added, 1)
            def node_max():
                pool.wait_ge(z_max, 1)
                nc.gpsimd.partition_all_reduce(zs[:, 1:2], zs[:, 0:1], P, RMAX).then_inc(z_allmax, 1)
                pool.wait_ge(z_exp, 1)
                nc.gpsimd.partition_all_reduce(zs[:, 4:5], zs[:, 3:4], P, RADD).then_inc(z_sum, 1)

            node_max()
            pool.wait_ge(x_ready, 1)
            nc.gpsimd.memset(BT, 0.0).then_inc(bt_zero, 1)
            nc.gpsimd.memset(LA, 0.0).then_inc(bt_zero, 1)
            for padded in (GX, MM, LOWT):
                nc.gpsimd.memset(padded, 0.0).then_inc(bt_zero, 1)
            for s in range(2):
                pool.wait_ge(mask_stored[s], 16 * HT + 1)
            pool.wait_ge(consts_ready, 1)
            for t in range(NT):
                own_block = MASK[:, t, t * P:(t + 1) * P]
                nc.gpsimd.tensor_tensor(own_block, own_block, not_eye[:, :], ALU.mult).then_inc(eye_cleared, 1)
            pool.wait_ge(x_ready, 2)
            nc.gpsimd.memset(V[:, :, :, HD:HD + 1], 1.0).then_inc(v_ones, 1)
            pool.wait_ge(v_ones, 1)
            for n, (rows, value) in enumerate(((KO[0][HD:P, :], 0.0), (QL[0][HD:P, :], 0.0), (KO[0][HD:HD + 1, :], 1.0),
                                               (KO[1][HD:P, :], 0.0), (QL[1][HD:P, :], 0.0), (KO[1][HD:HD + 1, :], 1.0))):
                if n == 0:
                    pool.wait_ge(w_low, 3)
                elif n == 3:
                    for q in range(2):
                        pool.wait_ge(qk_stored[q], 32 * H // 2 + 1)
                if n:
                    pool.wait_ge(row_ones, n)
                nc.gpsimd.memset(rows, value).then_inc(row_ones, 1)

            def low_probs(head, ic, before):
                u = head * NCH + ic
                for j in range(1, NT, 2):
                    b = j % 4
                    pool.wait_ge(exp_done[b], u * 4 + j // 4 + 2)
                    nc.gpsimd.tensor_tensor(PL[b], PF[b], PH[b], ALU.subtract).then_inc(pl_ready[b], 1)
                    if j == 5 and before:
                        join_halves(u - 1, head - (ic == 0), (ic - 1) % NCH)

            def join_halves(u, head, ic):
                pool.wait_ge(rden_ready, u + 1)
                nc.gpsimd.tensor_tensor(OC[:, :, 0:HD], OC[:, :, 0:HD], OC[:, :, HD + 1:VW], ALU.add).then_inc(halves_added, 1)
                pool.wait_ge(halves_added, u + 1)
                nc.gpsimd.tensor_tensor(ATT[:, ic * TPC:(ic + 1) * TPC, bass.ds(head * HD, HD)], OC[:, :, 0:HD],
                                        RD[:, :].unsqueeze(2).to_broadcast([P, TPC, HD]), ALU.mult).then_inc(att_ready, 1)

            with pool.Fori(0, H // 2) as pair:
                for s in range(2):
                    for ic in range(NCH):
                        low_probs(2 * pair + s, ic, s or ic)
                join_halves(NCH * (2 * pair + 2) - 1, 2 * pair + 1, NCH - 1)
            with pool.Fori(0, HT) as it:
                for s in range(2):
                    pool.wait_ge(att_ready, NCH * H + 1)
                    pool.wait_ge(at_psum[s], it + 1)
                    nc.gpsimd.tensor_copy(ATS[s], ATT[:, 2 * it + s, :]).then_inc(att_copied[s], 1)
            pool.wait_ge(x_ready, 3)
            nc.gpsimd.memset(BB, 0.0).then_inc(eb_zero, 1)

        @block.tensor
        def _(pe):
            def split_product(ps, left, right, last_of=None):
                n = 0
                for k in range(KD):
                    for a, b in ((0, 0), (0, 1), (1, 0)):
                        n += 1
                        last = pe.matmul(ps, left(a, k), right(b, k), start=(n == 1), stop=(n == 3 * KD),
                                         skip_group_check=True)
                return last

            def transpose_nodes(f):
                for it in range(QT):
                    for s in range(2):
                        pe.wait_ge(xn_ready[s], f * QT + it + 1)
                        pe.wait_ge(xl_ready[s], f * QT + it + 1)
                        for k in range(KD):
                            for r in range(2):
                                at = (2 * k + r) * P
                                last = pe.transpose(PS[s][:, at:at + P], XN[s][:, r, k * P:(k + 1) * P], identf[:, :])
                        last.then_inc(xn_transposed[s], 1)
                for s in range(2):
                    pe.wait_ge(xl_ready[s], (f + 1) * QT + 1)
                pe.wait_ge(w_low, f + 1)
                pe.wait_ge(w_high, f + 1)

            pe.wait_ge(ident_ready, 2)
            pe.wait_ge(consts_ready, 1)

            transpose_nodes(0)
            xt, w = XT[0], W[0][1:]
            with pe.Fori(0, NCH) as c:
                for o in range(KD):
                    pe.wait_ge(hl_ready[o], c + 1)
                    split_product(PS[2 + o][:, :], lambda a, k: w[a][:, k, o * P:(o + 1) * P],
                                  lambda b, k: xt[b][:, k, bass.ds(c * C, C)]).then_inc(h_psum[o], 1)
            with pe.Fori(0, HT) as it:
                for s in range(2):
                    pe.wait_ge(z_copied[s], it + 1)
                    split_product(PS[4 + s][:, 0:D + 1], lambda a, k: xt[a][:, k, bass.ds((2 * it + s) * P, P)],
                                  lambda b, k: w[b][:, k, D:2 * D + 1]).then_inc(sup_psum[s], 1)

            def edge_scores(t):
                for c in range(NCH):
                    pe.wait_ge(e_read[c], t + 1)
                    split_product(PS[c][:, :], lambda a, k: (HTh, HTl)[a][:, k, bass.ds(t * P, P)],
                                  lambda b, k: (HTh, HTl)[b][:, k, c * C:(c + 1) * C]).then_inc(e_ready[c], 1)

            def edge_output(it, s):
                t = 2 * it + s

                def transposes(g):
                    pe.wait_ge(pt_ready[g % 2], 2 * t + g // 2 + 1)
                    for q in range(TPC):
                        j = g * TPC + q
                        last = pe.transpose(PS[4 + g % 2][:, q * P:(q + 1) * P], PROB[s][:, j * P:(j + 1) * P], identf[:, :])
                    last.then_inc(pt_psum[g % 2], 1)

                def products(g):
                    pe.wait_ge(pt_ready[g % 2], 2 * t + g // 2 + 2)
                    for q in range(TPC):
                        j = g * TPC + q
                        last = pe.matmul(PS[6 + s][:, 0:D], PROBT[s][:, j * P:(j + 1) * P], SUP[:, j, :],
                                         start=(j == 0), stop=(j == NT - 1))
                    if g == NCH - 1:
                        last.then_inc(o_ready[s], 1)

                pe.wait_ge(p_ready[s], it + 1)
                transposes(0)
                pe.wait_ge(o_read[s], it + 1)
                for g in range(1, NCH):
                    transposes(g)
                    products(g - 1)
                products(NCH - 1)

            for s in range(2):
                pe.wait_ge(hl_ready[s], NCH + 1)
                pe.wait_ge(z_copied[s], HT + 1)
            edge_scores(0)
            with pe.Fori(0, HT - 1) as it:
                edge_scores(2 * it + 1)
                edge_output(it, 0)
                edge_scores(2 * it + 2)
                edge_output(it, 1)
            edge_scores(NT - 1)
            edge_output(HT - 1, 0)
            edge_output(HT - 1, 1)

            pe.wait_ge(x_ready, 1)
            transpose_nodes(1)
            xt, w = XT[1], W[1][1:]
            GC = E * D
            with pe.Fori(0, QT) as it:
                for r in range(4):
                    t = 4 * it + r
                    split_product(PS[2][:, bass.ds(t * (E + 1), E + 1)], lambda a, k: xt[a][:, k, bass.ds(t * P, P)],
                                  lambda b, k: w[b][:, k, GC:GC + E + 1]).then_inc(lg_ready, 1)
            pe.wait_ge(f0_in, 16 * (1 + 2 * E))
            for o in range(E * KD):
                last = pe.matmul(PS[3][0:ER, 0:D], BT[:, o, :], FC2[:, o, :], start=(o == 0), stop=(o == E * KD - 1))
            last.then_inc(m_product, 1)
            pe.wait_ge(m_copied, 1)

            LOW_LAG = 2

            def hidden(c, o):
                b = o % 4
                pe.wait_ge(hid_ready[b], 2 * c + o // 4 + 1)
                split_product(PS[4 + b][:, :], lambda a, k: w[a][:, k, o * P:(o + 1) * P],
                              lambda bb, k: xt[bb][:, k, bass.ds(c * C, C)]).then_inc(hid_psum[b], 1)

            def adapter(c, o):
                pe.wait_ge(hid_ready[o % 4], 2 * c + o // 4 + 2)
                if o == 0:
                    pe.wait_ge(low_ready, c + 1)
                last = pe.matmul(PS[0][0:ER, :], LA[:, o, :], HID[:, o, :], start=(o == 0), stop=(o == E * KD - 1))
                if o == E * KD - 1:
                    last.then_inc(low_psum, 1)

            def expert_outputs(c):
                pe.wait_ge(low_ready, c + 2)
                for s in range(2):
                    pe.wait_ge(f0_read[s], c + 1)
                    for r in range(2):
                        n = 2 * s + r
                        last = pe.matmul(PS[2 + s][:, r * D:(r + 1) * D], LOWT[:, n * P:(n + 1) * P], MM, start=True, stop=True)
                    last.then_inc(f0_psum[s], 1)

            def gates_transposed():
                pe.wait_ge(gx_ready, 1)
                for g in range(NCH):
                    if g >= 2:
                        pe.wait_ge(gt_ready, g - 1)
                    for q in range(TPC):
                        last = pe.transpose(PS[1 + g % 2][:, q * P:(q + 1) * P], GX[:, g * TPC + q, :], identf[:, :])
                    last.then_inc(gt_psum[g % 2], 1)

            def expert_chunk(c, before):
                for o in range(E * KD):
                    hidden(c, o)
                    if o >= LOW_LAG:
                        adapter(c, o - LOW_LAG)
                    elif before is not None:
                        adapter(before, E * KD + o - LOW_LAG)
                    if o == 4 and before is not None:
                        expert_outputs(before)

            expert_chunk(0, None)
            gates_transposed()
            pe.wait_ge(gt_ready, NCH)
            with pe.Fori(1, NCH) as c:
                expert_chunk(c, c - 1)
            for o in range(E * KD - LOW_LAG, E * KD):
                adapter(NCH - 1, o)
            expert_outputs(NCH - 1)

            pe.wait_ge(x_ready, 2)
            transpose_nodes(2)
            xt, w = XT[2], W[2][1:]
            with pe.Fori(0, H // 2) as pair:
                for q in range(2):
                    pe.wait_ge(qk_low[q], NCH * pair + 1)
                    for c in range(NCH):
                        b = NCH * q + c
                        split_product(PS[b][:, :], lambda a, k: w[a][:, k, bass.ds(q * H * HD + pair * P, P)],
                                      lambda bb, k: xt[bb][:, k, c * C:(c + 1) * C]).then_inc(qk_psum, 1)
            for q in range(2):
                pe.wait_ge(qk_low[q], NCH * H // 2 + 1)
            STEP = NCH * (NCH - 1)

            def early_piece(n):
                return n // (NCH - 1), n // NCH, n % NCH

            pe.wait_ge(stack_in[0], 96)
            with pe.Fori(0, QT) as it:
                for v in range(TPC):
                    t, s = TPC * it + v, v % 2
                    pe.wait_ge(v_read[s], 2 * it + v // 2 + 1)
                    split_product(PS[s][:, :], lambda a, k: xt[a][:, k, bass.ds(t * P, P)],
                                  lambda b, k: w[b][:, k, 2 * H * HD:3 * H * HD]).then_inc(v_psum[s], 1)
                    for n in range(STEP):
                        beside, i, c = early_piece(n)
                        if beside == v:
                            b = (n + 1) % 2
                            pe.wait_ge(rmax_read[b], STEP // 2 * it + n // 2 + 1)
                            pe.matmul(PS[MAX_BANKS[b]][:, :], QD[0][:, bass.ds(((NCH - 1) * it + i) * P, P)],
                                      KS[0][:, c * C:(c + 1) * C], start=True, stop=True).then_inc(rmax_psum[b], 1)

            def max_scores(n, s, g, q, rows_out, after=ROW_AT - SHIFT + 1):
                b, i, c = (q + 1) % 2, g * TPC + q // NCH, q % NCH
                pe.wait_ge(rmax_read[b], n * 8 + q // 2 + 1)
                if q == after:
                    pe.wait_ge(rrow_ready, rows_out)
                pe.matmul(PS[MAX_BANKS[b]][:, :], QD[s][:, i * P:(i + 1) * P], KS[s][:, c * C:(c + 1) * C],
                          start=True, stop=True).then_inc(rmax_psum[b], 1)

            def max_row(n, parity, read):
                pe.wait_ge(rneg_ready, n + 1)
                pe.wait_ge(rmax_read[0], read)
                for r in range(TPC):
                    last = pe.matmul(PS[MAX_BANKS[0]][HD:HD + 1, r * P:(r + 1) * P], MNEG[:, parity, r:r + 1], identf[:, :],
                                     start=True, stop=True, skip_group_check=True)
                last.then_inc(rrow_psum, 1)

            def scores(u, s, ic, j):
                b = j % 4
                if j == 0:
                    pe.wait_ge(rrow_ready, u + 1)
                pe.wait_ge(exp_done[b], u * 4 + j // 4 + 1)
                ps, cols, keys = PS[ST_BANKS[b]], slice(ic * C, (ic + 1) * C), slice(j * P, (j + 1) * P)
                pe.matmul(ps[:, :], KS[s][:, keys], QD[s][:, cols], start=True, stop=False, skip_group_check=True)
                pe.matmul(ps[:, :], KO[s][:, keys], QL[s][:, cols], start=False, stop=False, skip_group_check=True)
                if j // TPC == ic:
                    d = (j % TPC) * P
                    pe.matmul(ps[:, d:d + P], eye_a[:, :], eye_b[:, :], start=False, stop=False, skip_group_check=True)
                for q in range(TPC):
                    last = pe.matmul(ps[:, q * P:(q + 1) * P], MASK[:, ic * TPC + q, keys], identb[:, :],
                                     start=False, stop=(q == TPC - 1), skip_group_check=True)
                last.then_inc(st_ready[b], 1)

            def products(head, u, j):
                pe.wait_ge(pl_ready[j % 4], u * 4 + j // 4 + 1)
                for q in range(TPC):
                    if j == 0 and q % 2 == 0:
                        pe.wait_ge(att_read[q // 2], u + 1)
                    o, at, rows = PS[O_BANKS[q // 2]], (q % 2) * VW, slice(q * P, (q + 1) * P)
                    pe.matmul(o[:, at:at + VW], PH[j % 4][:, rows], V[:, j, head, :], start=(j == 0 and q % 2 == 0),
                              stop=False, skip_group_check=True)
                    last = pe.matmul(o[:, at:at + HD + 1], PL[j % 4][:, rows], V[:, j, head, 0:HD + 1], start=False,
                                     stop=(j == NT - 1), skip_group_check=True)
                last.then_inc(pv_done[j % 4], 1)

            def attend(head, s, ic, before, ahead, row, last):
                u = head * NCH + ic
                for j in range(NT):
                    scores(u, s, ic, j)
                    if j >= LAG:
                        products(head, u, j - LAG)
                    elif before is not None:
                        products(before, u - 1, NT + j - LAG)
                    if j == ROW_AT and row:
                        max_row(u + 3, (ic + 3) % 2, 8 * (u + 4) + (2 if ahead is not None else 1))
                    n, next_head, g, q = maxima_piece(ic, j)
                    if ahead is not None and ic == 0 and j == SHIFT:
                        pe.wait_ge(stack_in[1 - s], ahead)
                    if ahead is not None or not next_head:
                        max_scores(u + n, 1 - s if next_head else s, g, q, u + 4)
                if last:
                    for j in range(NT - LAG, NT):
                        products(head, u, j)

            pe.wait_ge(row_ones, 6)
            pe.wait_ge(eye_cleared, NT)
            for b in range(2):
                pe.wait_ge(v_read[b], HT + 1)
            for g in range(NCH - 1):
                if g:
                    pe.wait_ge(rrow_ready, g)
                max_row(g, g % 2, NT * (NCH - 1) // 2 + 1)
            for q in range(NT - SHIFT):
                max_scores(NCH - 1, 0, NCH - 1, q, NCH - 1, after=1)
            with pe.Fori(0, H // 2 - 1) as pair:
                for s in range(2):
                    head = 2 * pair + s
                    for ic in range(NCH):
                        attend(head, s, ic, (head if ic else head - 1) if s or ic else None, 96 * (pair + s + 1), True,
                               s == 1 and ic == NCH - 1)
            for s in range(2):
                head = H - 2 + s
                for ic in range(NCH):
                    attend(head, s, ic, (head if ic else head - 1) if s or ic else None, 96 * (H // 2) if s == 0 else None,
                           s == 0 or ic == 0, s == 1 and ic == NCH - 1)

            pe.wait_ge(wo_in, 16)
            for b in range(2):
                pe.wait_ge(att_read[b], NCH * H + 1)
            KC = H * HD // P
            with pe.Fori(0, HT) as it:
                for s in range(2):
                    pe.wait_ge(att_copied[s], it + 1)
                    pe.wait_ge(at_ready[s], it + 1)
                    for k in range(KC):
                        last = pe.transpose(PS[s][:, k * P:(k + 1) * P], ATS[s][:, k * P:(k + 1) * P], identf[:, :])
                    last.then_inc(at_psum[s], 1)
                for s in range(2):
                    pe.wait_ge(at_ready[s], it + 2)
                    pe.wait_ge(wo_read[s], it + 1)
                    for k in range(KC):
                        last = pe.matmul(PS[2 + s][:, 0:D], ATTT[s][:, k * P:(k + 1) * P], WO[:, k, :],
                                         start=(k == 0), stop=(k == KC - 1))
                    last.then_inc(wo_psum[s], 1)

            pe.wait_ge(x_ready, 3)
            transpose_nodes(3)
            xt, w = XT[3], W[3][1:]
            GC = NE * D
            with pe.Fori(0, QT) as it:
                for r in range(4):
                    t = 4 * it + r
                    split_product(PS[4][:, bass.ds(t * NE, NE)], lambda a, k: xt[a][:, k, bass.ds(t * P, P)],
                                  lambda b, k: w[b][:, k, GC:GC + NE]).then_inc(lg_ready, 1)
            pe.wait_ge(eb_high, 1)
            pe.wait_ge(eb_low, 1)
            def expert_products(t):
                for e in range(NE // 2):
                    pe.wait_ge(y_read[e], t + 1)
                    pe.matmul(PS[e][:, :], ones[:, :], BB[:, e * C:(e + 1) * C], start=True, stop=False,
                              skip_group_check=True)
                    n = 0
                    for k in range(KD):
                        for a, b in ((0, 0), (0, 1), (1, 0)):
                            n += 1
                            last = pe.matmul(PS[e][:, :], xt[a][:, k, bass.ds(t * P, P)], w[b][:, k, e * C:(e + 1) * C],
                                             start=False, stop=(n == 3 * KD), skip_group_check=True)
                    last.then_inc(y_psum, 1)

            with pe.Fori(0, QT) as it:
                for r in range(4):
                    expert_products(4 * it + r)

        @block.scalar
        def _(act):
            def high_weights(layer):
                act.wait_ge(w_in, 16 * (layer + 1))
                act.activation(W[layer][1], W[layer][0], ACT.Copy, scale=WS).then_inc(w_high, 1)

            def transposed_nodes(f):
                act.wait_ge(var_ready, f + 1)
                act.activation(SD, VAR, ACT.Sqrt).then_inc(std_ready, 1)
                if f == 0:
                    high_weights(f)
                for it in range(QT):
                    for s in range(2):
                        act.wait_ge(xn_transposed[s], f * QT + it + 2)
                        act.activation(XT[f][0][:, :, (2 * it + s) * 2 * P:(2 * it + s + 1) * 2 * P],
                                       PS[s][:, :].rearrange("p (k n) -> p k n", k=KD), ACT.Copy).then_inc(xh_ready[s], 1)

            transposed_nodes(0)
            with act.Fori(0, NCH) as c:
                for o in range(KD):
                    act.wait_ge(h_psum[o], c + 1)
                    act.activation(HTh[:, o, bass.ds(c * C, C)], PS[2 + o][:, :], ACT.Copy, scale=1 / WS).then_inc(hh_ready[o], 1)
            with act.Fori(0, HT) as it:
                for s in range(2):
                    act.wait_ge(sup_psum[s], it + 1)
                    act.activation(SUP[:, 2 * it + s, :], PS[4 + s][:, 0:D], ACT.Copy, scale=1 / WS).then_inc(sup_copied[s], 1)

            def edge_exp(it, s):
                act.wait_ge(nmax_ready[s], it + 2)
                act.activation(PROB[s], PROB[s], ACT.Exp, bias=NMX[:, s:s + 1], accum_out=RSUM[:, s:s + 1]).then_inc(p_ready[s], 1)

            def edge_evacuate(it, s):
                for g in range(NCH):
                    act.wait_ge(pt_psum[g % 2], 2 * (2 * it + s) + g // 2 + 1)
                    if g == 0:
                        act.wait_ge(o_ready[s], it + 1)
                    act.activation(PROBT[s][:, g * C:(g + 1) * C], PS[4 + g % 2][:, :], ACT.Copy).then_inc(pt_ready[g % 2], 1)

            def mask_row(it, s):
                act.wait_ge(adj_in[s], 16 * (it + 1))
                act.wait_ge(nmax_ready[s], it + 1)
                act.wait_ge(mask_stored[s], 16 * it + 1)
                act.activation(MROW[s], ADJ[s], ACT.Copy, scale=-MASKED, bias=MASKED).then_inc(mask_ready[s], 1)

            for s in range(2):
                mask_row(0, s)
            act.wait_ge(z_neg, 1)
            act.activation(NATT[:, :], ZC[:, :], ACT.Exp, bias=zs[:, 2:3], accum_out=zs[:, 3:4]).then_inc(z_exp, 1)
            with act.Fori(0, HT - 1) as it:
                for s in range(2):
                    edge_exp(it, s)
                    edge_evacuate(it, s)
                    mask_row(it + 1, s)
            high_weights(1)
            for s in range(2):
                edge_exp(HT - 1, s)
                edge_evacuate(HT - 1, s)

            transposed_nodes(1)
            high_weights(2)
            act.wait_ge(sh_ready, 1)
            act.activation(GW[:, :, 0:E], LG[:, :, 0:E], ACT.Exp).then_inc(ex_ready, 1)
            act.activation(GS[:, 3, :], LG[:, :, E], ACT.Exp, scale=-1.0).then_inc(ex_ready, 1)
            act.wait_ge(m_product, 1)
            act.wait_ge(bt_zero, 5)
            act.activation(MM[0:ER, :], PS[3][0:ER, 0:D], ACT.Copy).then_inc(m_copied, 1)

            def hidden_relu(c):
                for o in range(E * KD):
                    act.wait_ge(hid_psum[o % 4], 2 * c + o // 4 + 1)
                    act.activation(HID[:, o, :], PS[4 + o % 4][:, :], ACT.Relu, scale=1 / WS).then_inc(hid_ready[o % 4], 1)

            hidden_relu(0)
            for g in range(NCH):
                act.wait_ge(gt_psum[g % 2], g // 2 + 1)
                act.activation(GT[:, g * C:(g + 1) * C], PS[1 + g % 2][:, :], ACT.Copy).then_inc(gt_ready, 1)
            with act.Fori(1, NCH) as c:
                hidden_relu(c)

            transposed_nodes(2)
            with act.Fori(0, H // 2) as pair:
                for q in range(2):
                    act.wait_ge(qk_stored[q], 32 * pair + 1)
                    for c in range(NCH):
                        act.wait_ge(qk_psum, 2 * NCH * pair + NCH * q + c + 1)
                        act.activation(QKS[q][0][:, c * C:(c + 1) * C], PS[4 * q + c][:, :], ACT.Copy,
                                       scale=1 / WS).then_inc(qk_high, 1)
            with act.Fori(0, HT) as it:
                for s in range(2):
                    act.wait_ge(v_psum[s], it + 1)
                    act.activation(V[:, 2 * it + s, :, 0:HD], PS[s][:, :].rearrange("p (h d) -> p h d", h=H), ACT.Copy,
                                   scale=1 / WS).then_inc(v_high[s], 1)

            def max_row(s, n, g):
                act.wait_ge(rrow_psum, n + 1)
                act.activation(QL[s][HD:HD + 1, g * C:(g + 1) * C], PS[MAX_BANKS[0]][HD:HD + 1, :], ACT.Copy).then_inc(rrow_ready, 1)

            def exps(head, s, ic, row):
                u = head * NCH + ic
                for j in range(NT):
                    ps = PS[ST_BANKS[j % 4]][:, :]
                    act.wait_ge(st_ready[j % 4], u * 4 + j // 4 + 1)
                    act.wait_ge(pv_done[j % 4], u * 4 + j // 4 + 1)
                    act.activation(PF[j % 4], ps, ACT.Exp, scale=SCALE)
                    act.activation(PH[j % 4], ps, ACT.Exp, scale=SCALE).then_inc(exp_done[j % 4], 1)
                    if j == ROW_AT and row is not None:
                        max_row(s if ic == 0 else 1 - s, row, (ic + 3) % 4)

            for q in range(2):
                act.wait_ge(qk_stored[q], 32 * H // 2 + 1)
            act.wait_ge(row_ones, 6)
            for g in range(NCH - 1):
                max_row(0, g, g)
            with act.Fori(0, H // 2 - 1) as pair:
                for s in range(2):
                    for ic in range(NCH):
                        exps(2 * pair + s, s, ic, (2 * pair + s) * NCH + ic + 3)
            for s in range(2):
                for ic in range(NCH):
                    row = (H - 2 + s) * NCH + ic + 3
                    exps(H - 2 + s, s, ic, row if row < H * NCH else None)
            for first in (0, HT // 2):
                with act.Fori(first, first + HT // 2) as it:
                    for s in range(2):
                        act.wait_ge(at_psum[s], it + 2)
                        act.wait_ge(wo_psum[s], it + 1)
                        act.activation(ATTT[s], PS[s][:, :], ACT.Copy).then_inc(at_ready[s], 1)
                if first == 0:
                    high_weights(3)

            transposed_nodes(3)
            act.wait_ge(eb_in, 16)
            act.wait_ge(eb_zero, 1)
            act.activation(BB[0:1, :], BSTAGE[0:1, :], ACT.Copy, scale=WS).then_inc(eb_high, 1)
            act.wait_ge(sh_ready, 2)
            act.activation(GW[:, :, 0:NE], LG[:, :, 0:NE], ACT.Exp).then_inc(ex_ready, 1)

        @block.vector
        def _(dve):
            own = Tally(dve, dve_done)

            def take_waits(n):
                dve.memset(idle_cells[:, n:n + 1], 0.0)

            tt, ts, stt = dve.tensor_tensor, dve.tensor_scalar, dve.scalar_tensor_tensor

            def low_weights(layer):
                dve.wait_ge(w_high, layer + 1)
                stt(out=W[layer][2], in0=W[layer][0], scalar=WS, in1=W[layer][1], op0=ALU.mult,
                    op1=ALU.subtract).then_inc(w_low, 1)

            def stats(t):
                own.add(dve.bn_stats(STATS[:, t, :], X[:, t, :]))

            def layernorm(f):
                own.wait()
                me, ve, mo, vo = (STATS[:, :, i] for i in (1, 2, 4, 5))
                own.add(tt(MEAN, me, mo, ALU.add))
                own.add(tt(TA, me, mo, ALU.subtract))
                own.add(tt(TB, ve, vo, ALU.add))
                own.wait()
                own.add(ts(MEAN, MEAN, 0.5, None, ALU.mult))
                own.add(tt(TA, TA, TA, ALU.mult))
                own.add(ts(TB, TB, 1.0 / D, EPS, ALU.mult, ALU.add))
                own.wait()
                stt(out=VAR, in0=TA, scalar=0.25, in1=TB, op0=ALU.mult, op1=ALU.add).then_inc(var_ready, 1)
                dve.wait_ge(std_ready, f + 1)
                own.add(dve.reciprocal(RSTD, SD))
                own.wait()
                own.add(tt(TA, RSTD, RSTD, ALU.mult))
                own.wait()
                own.add(tt(TA, TA, VAR, ALU.mult))
                own.wait()
                own.add(ts(TA, TA, -0.5, 1.5, ALU.mult, ALU.add))
                own.wait()
                own.add(tt(RSTD, RSTD, TA, ALU.mult))
                own.wait()

                def normalised(it, s):
                    dve.wait_ge(xn_transposed[s], f * QT + it + 1)
                    for r in range(2):
                        t = 4 * it + 2 * s + r
                        last = ts(XN[s][:, r, :], X[:, t, :], MEAN[:, t:t + 1], RSTD[:, t:t + 1], ALU.subtract, ALU.mult)
                    last.then_inc(xn_ready[s], 1)

                def low_part(it, s):
                    cols = slice((2 * it + s) * 2 * P, (2 * it + s + 1) * 2 * P)
                    dve.wait_ge(xh_ready[s], f * QT + it + 1)
                    tt(XT[f][1][:, :, cols], PS[s][:, :].rearrange("p (k n) -> p k n", k=KD), XT[f][0][:, :, cols],
                       ALU.subtract).then_inc(xl_ready[s], 1)

                for s in range(2):
                    normalised(0, s)
                if f == 0:
                    low_weights(f)
                for it in range(QT - 1):
                    for s in range(2):
                        low_part(it, s)
                        normalised(it + 1, s)
                for s in range(2):
                    low_part(QT - 1, s)

            dve.wait_ge(ident_ready, 2)
            own.add(dve.tensor_copy(identb[:, :], identf[:, :]))
            own.add(ts(not_eye[:, :], identf[:, :], -1.0, 1.0, ALU.mult, ALU.add))
            own.add(ts(eye_a[:, :], identf[:, :], EYE_A, None, ALU.mult))
            ts(eye_b[:, :], identf[:, :], EYE_B, None, ALU.mult).then_inc(consts_ready, 1)

            dve.wait_ge(x_in, 16)
            with own.loop(QT, 4) as it:
                for r in range(4):
                    stats(4 * it + r)
            layernorm(0)
            with dve.Fori(0, NCH) as c:
                for o in range(KD):
                    cols = bass.ds(c * C, C)
                    dve.wait_ge(hh_ready[o], c + 1)
                    stt(out=HTl[:, o, cols], in0=PS[2 + o][:, :], scalar=1 / WS, in1=HTh[:, o, cols], op0=ALU.mult,
                        op1=ALU.subtract).then_inc(hl_ready[o], 1)
            with dve.Fori(0, HT) as it:
                for s in range(2):
                    dve.wait_ge(sup_copied[s], it + 1)
                    ts(ZC[:, bass.ds(2 * it + s, 1)], PS[4 + s][:, D:D + 1], 1 / WS, None, ALU.mult).then_inc(z_copied[s], 1)
            for s in range(2):
                dve.wait_ge(z_copied[s], HT + 1)
            dve.tensor_reduce(zs[:, 0:1], ZC[:, :], AX.X, ALU.max).then_inc(z_max, 1)
            def edge_max(it, s, t):
                for c in range(NCH):
                    dve.wait_ge(e_ready[c], t + 1)
                    if c == 0:
                        dve.wait_ge(mask_ready[s], it + 2)
                        dve.wait_ge(o_ready[s], it + 1)
                    take_waits(c)
                    dve.tensor_tensor_reduce(out=PROB[s][:, c * C:(c + 1) * C], in0=PS[c][:, :], in1=MROW[s][:, c * C:(c + 1) * C],
                                             scale=1.0, scalar=-3e38, op0=ALU.add, op1=ALU.max,
                                             accum_out=MX[:, s, c:c + 1]).then_inc(e_read[c], 1)
                dve.wait_ge(e_read[NCH - 1], t + 2)
                own.add(dve.tensor_reduce(RSC[:, 2:3], MX[:, s, :], AX.X, ALU.max))
                own.wait()
                ts(NMX[:, s:s + 1], RSC[:, 2:3], -1.0, None, ALU.mult).then_inc(nmax_ready[s], 1)

            def edge_update(it, s, t):
                dve.wait_ge(o_ready[s], it + 2)
                own.add(dve.reciprocal(RSC[:, 0:1], RSUM[:, s:s + 1]))
                own.wait()
                own.add(tt(RSC[:, 1:2], RSC[:, 0:1], NATT[:, bass.ds(t, 1)], ALU.mult))
                own.wait()
                stt(out=X[:, t, :], in0=PS[6 + s][:, 0:D], scalar=RSC[:, 1:2], in1=X[:, t, :], op0=ALU.mult,
                    op1=ALU.add).then_inc(o_read[s], 1)
                dve.wait_ge(o_read[s], it + 2)
                stats(t)

            def edge_pair(it, peeled):
                edge_max(it, 1, 2 * it + 1)
                if peeled:
                    dve.wait_ge(z_sum, 1)
                    own.add(dve.reciprocal(zs[:, 5:6], zs[:, 4:5]))
                    own.wait()
                    own.add(ts(NATT[:, :], NATT[:, :], zs[:, 5:6], None, ALU.mult))
                    own.wait()
                    dve.wait_ge(bias_added, 1)
                edge_update(it, 0, 2 * it)
                edge_max(it + 1, 0, 2 * it + 2)
                edge_update(it, 1, 2 * it + 1)

            dve.wait_ge(z_allmax, 1)
            ts(zs[:, 2:3], zs[:, 1:2], -1.0, None, ALU.mult).then_inc(z_neg, 1)
            edge_max(0, 0, 0)
            edge_pair(0, True)
            with own.loop(HT - 2, 8) as i:
                edge_pair(i + 1, False)
            low_weights(1)
            edge_max(HT - 1, 1, NT - 1)
            edge_update(HT - 1, 0, NT - 2)
            edge_update(HT - 1, 1, NT - 1)
            for s in range(2):
                dve.wait_ge(o_read[s], HT + 1)
            dve.nop().then_inc(x_ready, 1)
            layernorm(1)
            low_weights(2)
            dve.wait_ge(lg_ready, NT)

            def softmax_shift(n, bias):
                lg, ps = LG[:, :, 0:n], PS[2 if n == E else 4]
                cols = n + (n == E)
                own.add(ts(LG[:, :, 0:cols], ps[:, 0:NT * cols].rearrange("p (t e) -> p t e", e=cols), 1 / WS, None, ALU.mult))
                own.wait()
                if bias is not None:
                    own.add(tt(lg, lg, bias.unsqueeze(1).to_broadcast([P, NT, n]), ALU.add))
                    own.wait()
                own.add(dve.tensor_reduce(GS[:, 0, :], lg, AX.X, ALU.max))
                own.wait()
                tt(lg, lg, GS[:, 0, :].unsqueeze(2).to_broadcast([P, NT, n]), ALU.subtract).then_inc(sh_ready, 1)

            def softmax_divide(n):
                own.add(dve.tensor_reduce(GS[:, 0, :], GW[:, :, 0:n], AX.X, ALU.add))
                own.wait()
                own.add(dve.reciprocal(GS[:, 1, :], GS[:, 0, :]))
                own.wait()
                own.add(tt(GW[:, :, 0:n], GW[:, :, 0:n], GS[:, 1, :].unsqueeze(2).to_broadcast([P, NT, n]), ALU.mult))
                own.wait()

            softmax_shift(E, None)
            dve.wait_ge(ex_ready, 2)
            softmax_divide(E)
            own.add(ts(GS[:, 3, :], GS[:, 3, :], 1.0, None, ALU.add))
            own.wait()
            own.add(dve.reciprocal(GS[:, 2, :], GS[:, 3, :]))
            own.wait()
            own.add(ts(GS[:, 2, :], GS[:, 2, :], 1.0 / E, None, ALU.mult))
            own.wait()
            own.add(tt(GW[:, :, 0:E], GW[:, :, 0:E], GS[:, 2, :].unsqueeze(2).to_broadcast([P, NT, E]), ALU.subtract))
            own.wait()
            own.add(ts(GW[:, :, 0:E], GW[:, :, 0:E], 0.0, None, ALU.max))
            own.wait()
            own.add(dve.tensor_reduce(GS[:, 0, :], GW[:, :, 0:E], AX.X, ALU.add))
            own.wait()
            own.add(ts(GS[:, 1, :], GS[:, 0, :], 0.0, None, ALU.is_equal))
            own.wait()
            own.add(tt(GS[:, 0, :], GS[:, 0, :], GS[:, 1, :], ALU.add))
            own.wait()
            own.add(dve.reciprocal(GS[:, 1, :], GS[:, 0, :]))
            own.wait()
            own.add(tt(GW[:, :, 0:E], GW[:, :, 0:E], GS[:, 1, :].unsqueeze(2).to_broadcast([P, NT, E]), ALU.mult))
            own.wait()
            dve.wait_ge(bt_zero, 5)
            ts(GX[:, :, 0:ER].rearrange("p t (e r) -> p t e r", e=E), GW[:, :, 0:E].unsqueeze(3).to_broadcast([P, NT, E, R]),
               1.0, None, ALU.mult).then_inc(gx_ready, 1)
            dve.wait_ge(gt_ready, NCH)
            with own.loop(NCH, TPC) as c:
                dve.wait_ge(low_psum, c + 1)
                tt(LOWT[0:ER, :], PS[0][0:ER, :], GT[0:ER, bass.ds(c * C, C)], ALU.mult).then_inc(low_ready, 1)
                for s in range(2):
                    dve.wait_ge(f0_psum[s], c + 1)
                    pair = X[:, bass.ds(c * TPC + 2 * s, 2), :]
                    tt(pair, PS[2 + s][:, :].rearrange("p (t d) -> p t d", t=2), pair, ALU.add).then_inc(f0_read[s], 1)
                for s in range(2):
                    dve.wait_ge(f0_read[s], c + 2)
                    for r in range(2):
                        stats(c * TPC + 2 * s + r)
            for s in range(2):
                dve.wait_ge(f0_read[s], NCH + 1)
            dve.nop().then_inc(x_ready, 1)
            layernorm(2)
            with dve.Fori(0, H // 2) as pair:
                for q in range(2):
                    dve.wait_ge(qk_stored[q], 32 * pair + 1)
                    for c in range(NCH):
                        b = 4 * q + c
                        dve.wait_ge(qk_high, 2 * NCH * pair + NCH * q + c + 1)
                        stt(out=QKS[q][1][:, c * C:(c + 1) * C], in0=PS[b][:, :], scalar=1 / WS, in1=QKS[q][0][:, c * C:(c + 1) * C],
                            op0=ALU.mult, op1=ALU.subtract).then_inc(qk_low[q], 1)
            dve.wait_ge(eye_cleared, NT)
            for it in range(QT):
                for v in range(TPC):
                    s = v % 2
                    for n in range((NCH - 1) * v, (NCH - 1) * (v + 1)):
                        b, i, c = (n + 1) % 2, n // NCH, n % NCH
                        dve.wait_ge(rmax_psum[b], NCH * (NCH - 1) // 2 * it + n // 2 + 1)
                        rows = (NCH - 1) * it + i
                        dve.tensor_tensor_reduce(out=MJUNK0[b], in0=PS[MAX_BANKS[b]][:, :],
                                                 in1=MASK[:, rows, c * C:(c + 1) * C],
                                                 scale=1.0, scalar=-3e38, op0=ALU.add, op1=ALU.max,
                                                 accum_out=MQ0[:, rows, c:c + 1]).then_inc(rmax_read[b], 1)
                    dve.wait_ge(v_high[s], 2 * it + v // 2 + 1)
                    stt(out=V[:, TPC * it + v, :, HD + 1:VW], in0=PS[s][:, :].rearrange("p (h d) -> p h d", h=H), scalar=1 / WS,
                        in1=V[:, TPC * it + v, :, 0:HD], op0=ALU.mult, op1=ALU.subtract).then_inc(v_read[s], 1)

            def row_max(n, g, qs):
                for q in qs:
                    b, i, c = (q + 1) % 2, g * TPC + q // NCH, q % NCH
                    dve.wait_ge(rmax_psum[b], n * 8 + q // 2 + 1)
                    take_waits(q)
                    dve.tensor_tensor_reduce(out=MJUNK[b], in0=PS[MAX_BANKS[b]][:, :], in1=MASK[:, i, c * C:(c + 1) * C],
                                             scale=1.0, scalar=-3e38, op0=ALU.add, op1=ALU.max,
                                             accum_out=MQ[:, q // NCH, c:c + 1]).then_inc(rmax_read[b], 1)

            def row_negate(n, parity, quarters=MQ):
                if not isinstance(n, int) or n >= 2:
                    dve.wait_ge(rrow_psum, n - 1)
                for b in range(2):
                    dve.wait_ge(rmax_read[b], n * 8 + 9)
                if not isinstance(n, int) or n >= 1:
                    dve.wait_ge(rneg_ready, n)
                dve.tensor_reduce(MR[:, :], quarters[:, :, :], AX.X, ALU.max).then_inc(rmax_ready, 1)
                dve.wait_ge(rmax_ready, n + 1)
                ts(MNEG[:, parity, :], MR[:, :], -1.0, None, ALU.mult).then_inc(rneg_ready, 1)

            def low_probs(u, j):
                dve.wait_ge(exp_done[j % 4], u * 4 + j // 4 + 2)
                tt(PL[j % 4], PF[j % 4], PH[j % 4], ALU.subtract).then_inc(pl_ready[j % 4], 1)

            def take_outputs(u):
                dve.wait_ge(pv_done[3], u * 4 + 5)
                dve.wait_ge(att_ready, u + 1)
                for b in range(2):
                    dve.tensor_copy(OC[:, 2 * b:2 * b + 2, :], PS[O_BANKS[b]][:, 0:2 * VW].rearrange("p (q d) -> p q d", q=2)
                                    ).then_inc(att_read[b], 1)
                for b in range(2):
                    dve.wait_ge(att_read[b], u + 2)
                dve.reciprocal(RD[:, :], OC[:, :, HD]).then_inc(rden_ready, 1)

            for g in range(NCH - 1):
                row_negate(g, g % 2, MQ0[:, g * TPC:(g + 1) * TPC, :])
            row_max(NCH - 1, NCH - 1, range(NT - SHIFT))

            def attend(head, ic, before, ahead, last):
                u = head * NCH + ic
                for j in range(NT):
                    if j == LAG - 1 and before:
                        take_outputs(u - 1)
                    n, next_head, g, q = maxima_piece(ic, j)
                    if ahead or not next_head:
                        row_max(u + n, g, (q,))
                        if q == NT - 1:
                            row_negate(u + n, (ic + 3) % 2)
                    if j % 2 == 0:
                        low_probs(u, j)
                if last:
                    take_outputs(u)

            with dve.Fori(0, H // 2 - 1) as pair:
                for s in range(2):
                    for ic in range(NCH):
                        attend(2 * pair + s, ic, s or ic, True, s == 1 and ic == NCH - 1)
            for s in range(2):
                for ic in range(NCH):
                    attend(H - 2 + s, ic, s or ic, s == 0, s == 1 and ic == NCH - 1)
            for first in (0, HT // 2):
                with own.loop(HT // 2, 2) as i:
                    it = first + i
                    for s in range(2):
                        t = 2 * it + s
                        dve.wait_ge(wo_psum[s], it + 2)
                        tt(X[:, t, :], PS[2 + s][:, 0:D], X[:, t, :], ALU.add).then_inc(wo_read[s], 1)
                        dve.wait_ge(wo_read[s], it + 2)
                        stats(t)
                if first == 0:
                    low_weights(3)
            for s in range(2):
                dve.wait_ge(wo_read[s], HT + 1)
            dve.nop().then_inc(x_ready, 1)
            layernorm(3)
            dve.wait_ge(eb_high, 1)
            dve.wait_ge(eb_zero, 1)
            own.add(ts(BSTAGE[32:33, :], BSTAGE[0:1, :], WS, None, ALU.mult))
            own.add(dve.tensor_copy(BSTAGE[64:65, :], BB[0:1, :]))
            own.wait()
            own.add(tt(BB[32:33, :], BSTAGE[32:33, :], BSTAGE[64:65, :], ALU.subtract))
            own.wait()
            dve.nop().then_inc(eb_low, 1)
            dve.wait_ge(lg_ready, 2 * NT)
            softmax_shift(NE, mbias[:, :])
            dve.wait_ge(ex_ready, 3)
            softmax_divide(NE)
            own.add(ts(GW[:, :, 0:NE], GW[:, :, 0:NE], 1 / WS, None, ALU.mult))
            own.wait()
            def mix(t):
                for e in range(NE):
                    if e % 2 == 0:
                        dve.wait_ge(y_psum, NE // 2 * t + e // 2 + 1)
                    ins = stt(out=X[:, t, :], in0=PS[e // 2][:, (e % 2) * D:(e % 2 + 1) * D], scalar=GW[:, t, e:e + 1],
                              in1=X[:, t, :], op0=ALU.mult, op1=ALU.add)
                    if e % 2 == 0:
                        own.add(ins)
                        own.wait()
                    else:
                        ins.then_inc(y_read[e // 2], 1)
                        dve.wait_ge(y_read[e // 2], t + 2)
                dve.nop().then_inc(y_tile, 1)

            with own.loop(QT, 4 * NE // 2) as it:
                for r in range(4):
                    mix(4 * it + r)


def kernel(x, adj, L0_gnn_weight, L0_gnn_bias, L0_gnn_node_w, L0_gnn_edge_w, L0_ffn_gate_w, L0_ffn_thr_w, L0_ffn_fc1_w,
           L0_ffn_lora_A, L0_ffn_lora_B, L0_ffn_fc2_w, L1_gnn_Wks, L1_gnn_Wqs, L1_gnn_Wvs, L1_gnn_Wo,
           L1_ffn_expert_weights, L1_ffn_expert_biases, L1_ffn_mixer_w, L1_ffn_mixer_b):
    import concourse.bacc as bacc
    from concourse.bass_utils import run_bass_kernel_spmd

    def heads(w):
        w = np.asarray(w).transpose(1, 0, 2)
        return w.reshape(w.shape[0], -1)

    def by_input(w):
        w = np.asarray(w).transpose(2, 0, 1)
        return w.reshape(w.shape[0], -1)

    def side_by_side(*ws):
        return np.concatenate([np.asarray(w) for w in ws], axis=1)

    wo = np.asarray(L1_gnn_Wo)
    arrays = {
        "x": x, "adj": adj, "w_gnn0": side_by_side(L0_gnn_edge_w, L0_gnn_weight, L0_gnn_node_w), "g_bias": L0_gnn_bias,
        "w_ffn0": side_by_side(by_input(L0_ffn_fc1_w), np.asarray(L0_ffn_gate_w).T, np.asarray(L0_ffn_thr_w).T),
        "lora_a": L0_ffn_lora_A, "lora_bt": np.asarray(L0_ffn_lora_B).transpose(0, 2, 1),
        "fc2": np.asarray(L0_ffn_fc2_w).transpose(0, 2, 1),
        "w_gnn1": side_by_side(heads(L1_gnn_Wqs), heads(L1_gnn_Wks), heads(L1_gnn_Wvs)), "wo": wo.reshape(-1, wo.shape[2]),
        "w_ffn1": side_by_side(by_input(L1_ffn_expert_weights), np.asarray(L1_ffn_mixer_w).T),
        "expert_biases": L1_ffn_expert_biases, "mixer_b": L1_ffn_mixer_b,
    }
    arrays = {name: np.ascontiguousarray(a) for name, a in arrays.items()}
    nc = bacc.Bacc("TRN2", target_bir_lowering=False, num_devices=1)
    ins = {name: nc.dram_tensor(name, a.shape, mybir.dt.from_np(a.dtype), kind="ExternalInput").ap()
           for name, a in arrays.items()}
    out = nc.dram_tensor("y", arrays["x"].shape, F32, kind="ExternalOutput").ap()
    gnn_moe_program(nc, **ins, out=out)
    r = run_bass_kernel_spmd(nc, [arrays], core_ids=[0])
    return r.results[0]["y"]
```

```python
from contextlib import ExitStack, contextmanager

import numpy as np

import concourse.bass as bass
from concourse import mybir

F32 = mybir.dt.float32
F16 = mybir.dt.float16
BF16 = mybir.dt.bfloat16
ALU = mybir.AluOpType
ACT = mybir.ActivationFunctionType
AX = mybir.AxisListType
RMAX = bass.bass_isa.ReduceOp.max
RADD = bass.bass_isa.ReduceOp.add

P = 128


class Tally:

    def __init__(self, eng, sem):
        self.eng, self.sem, self.n = eng, sem, 0

    def add(self, ins):
        ins.then_inc(self.sem, 1)
        self.n = self.n + 1
        return ins

    def wait(self):
        self.eng.wait_ge(self.sem, self.n)

    @contextmanager
    def loop(self, count, per):
        start = self.n
        with self.eng.Fori(0, count) as i:
            self.n = start + i * per
            yield i
        self.n = start + count * per


def product_pair(value):
    a = np.arange(1024, 2048, dtype=np.float64) / 1024
    b = (value / a).astype(np.float16).astype(np.float64)
    n = int(np.argmin(np.abs(a * b - value)))
    return float(a[n]), float(b[n])


def gnn_moe_program(nc, x, adj, w_gnn0, g_bias, w_ffn0, lora_a, lora_bt, fc2, w_gnn1, wo, w_ffn1, expert_biases, mixer_b, out):
    N, D = x.shape
    NT = N // P
    HT = NT // 2
    QT = NT // 4
    KD = D // P
    C = 512
    NCH = N // C
    TPC = C // P
    E, _, R = lora_a.shape
    ER = E * R
    HD = 64
    H = wo.shape[0] // HD
    KC = H * HD // P
    NE = expert_biases.shape[0]
    EPS = 1e-5
    WS = 64.0
    MASKED = -1e16
    SCALE = float(HD) ** -0.5
    EYE_A, EYE_B = product_pair(0.01 / SCALE)

    with ExitStack() as ctx:
        def sem(name):
            return ctx.enter_context(nc.semaphore(name))

        def sems(name, n):
            return [sem(f"{name}{i}") for i in range(n)]

        def sb(name, shape, dt=F32):
            return ctx.enter_context(nc.sbuf_tensor(name, shape, dt))

        X = sb("X", [P, NT, D])
        MASK = sb("MASK", [P, NT, N], BF16)
        arena = sb("arena", [P, 121 * 256])

        def area(kib, words, dt=F32):
            a = arena[:, int(kib * 256):int(kib * 256) + words]
            return a if dt == F32 else a.bitcast(dt)

        def xt_area(kib):
            return area(kib, KD * N, F16).rearrange("p (h k n) -> p h k n", h=2, k=KD)

        xt_low = xt_area(0)
        XT = [(xt_low[:, 0], xt_low[:, 1])] * 3 + [(xt_area(81)[:, 0], xt_area(81)[:, 1])]

        def weights(kib_stage, kib_parts, k, cols):
            stage = area(kib_stage, k * cols).rearrange("p (k n) -> p k n", k=k)
            parts = area(kib_parts, k * cols, F16).rearrange("p (h k n) -> p h k n", h=2, k=k)
            return stage, parts[:, 0], parts[:, 1]

        W = [weights(104, 109, KD, D + D + 1), weights(104, 112.25, KD, E * D + E + 1), weights(83, 49, KD, 3 * H * HD),
             weights(8, 81, KC, D), weights(16, 33, KD, NE * D + NE)]
        W_OF = (0, 1, 2, 4)
        PIECES = 3
        SPLITS = (1, 2, 3, 4, 4 + PIECES)

        def piece(part, n):
            cols = part.shape[2]
            return part[:, :, n * cols // PIECES:(n + 1) * cols // PIECES]

        GROUP_ENDS = (HT - 5, HT - 3, HT - 1, HT)
        PROJECTED = tuple(zip((0,) + GROUP_ENDS[:-1], GROUP_ENDS))

        ht = area(16, KD * N, F16).rearrange("p (h k n) -> p h k n", h=2, k=KD)
        HTh, HTl = ht[:, 0], ht[:, 1]
        sup = area(32, NT * D, F16).rearrange("p (h t n) -> p h t n", h=2, t=NT)
        SUPh, SUPl = sup[:, 0], sup[:, 1]
        PROB = [area(48 + 8 * s, N) for s in range(2)]
        PTh, PTl = ([area(64 + 8 * s + 4 * part, N // 2, F16) for s in range(2)] for part in range(2))
        ADJ = [area(80 + 8 * s, N) for s in range(2)]
        MROW = [area(96 + 4 * s, N // 2, BF16) for s in range(2)]
        HID = area(16, E * KD * C).rearrange("p (o n) -> p o n", o=E * KD)
        FC2 = area(66, E * KD * D).rearrange("p (o n) -> p o n", o=E * KD)
        BT = area(74, E * KD * ER).rearrange("p (o n) -> p o n", o=E * KD)
        LA = area(76, E * KD * ER).rearrange("p (o n) -> p o n", o=E * KD)
        MM = area(78, D)
        LOWT = area(79, C)
        GX = area(32, NT * P).rearrange("p (t n) -> p t n", t=NT)
        GT = area(40, N)
        VW = 2 * HD + 1
        V = area(16.25, NT * H * VW // 2, F16).rearrange("p (t h d) -> p t h d", t=NT, h=H)
        QKS = [[area(97 + 8 * s + 4 * q, N // 2, F16) for q in range(2)] for s in range(2)]
        ATT = area(49, NT * H * HD).rearrange("p (t n) -> p t n", t=NT)
        KS, QD, QL, KO = ([area(81 + 16 * s + 4 * q, N // 2, F16) for s in range(2)] for q in range(4))
        PF = [area(113 + 2 * s, C) for s in range(4)]
        PH = [area(s, C // 2, F16) for s in range(4)]
        PL = [area(4 + s, C // 2, F16) for s in range(4)]
        MJUNK = [area(12 + b, C // 2, BF16) for b in range(2)]
        MJUNK0 = [area(66 + b, C // 2, BF16) for b in range(2)]
        ATh, ATl = ([area(2 * part + s, C // 2, F16) for s in range(2)] for part in range(2))
        BIAS_ROWS = (0, 32, 64)
        BSTAGE = area(101, D)
        BB = area(97, D // 2, F16)
        GX1 = area(50, NT * P).rearrange("p (t n) -> p t n", t=NT)
        GT1 = area(58, N // 2, F16)

        XN = [area(62 + 2 * s, 2 * D).rearrange("p (t d) -> p t d", t=2) for s in range(2)]
        identf = sb("identf", [P, P])
        identb = sb("identb", [P, P], BF16)
        not_eye = sb("not_eye", [P, P], BF16)
        eye_a = sb("eye_a", [P, P], F16)
        eye_b = sb("eye_b", [P, P], F16)
        gbias = area(114, D)
        mbias = sb("mbias", [P, NE])
        STATS = sb("STATS", [P, NT, 6])
        small = sb("small", [P, 7, NT])
        MEAN, VAR, RSTD, SD, TA, TB, NMR = (small[:, i, :] for i in range(7))
        ZC = sb("ZC", [P, NT])
        NATT = sb("NATT", [P, NT])
        zs = sb("zs", [P, 8])
        MX = sb("MX", [P, 2, NCH])
        NMX = sb("NMX", [P, 2])
        RSUM = sb("RSUM", [P, 2])
        RSC = sb("RSC", [P, 4])
        LG = sb("LG", [P, NT, 8])
        GW = sb("GW", [P, NT, 8])
        GS = sb("GS", [P, 4, NT])
        MQ = sb("MQ", [P, TPC, NCH])
        MQ0 = sb("MQ0", [P, TPC * (NCH - 1), NCH])
        MR = sb("MR", [P, TPC])
        MNEG = sb("MNEG", [P, 2, TPC])
        RD = sb("RD", [P, TPC])
        OC = area(14, TPC * VW).rearrange("p (q d) -> p q d", q=TPC)
        idle_cells = sb("idle_cells", [P, NT])
        ST_BANKS, O_BANKS, MAX_BANKS = (0, 1, 4, 7), (2, 3), (5, 6)
        QK = nc.dram_tensor("qk_scratch", [2, 2, H, HD, N], F16).ap()

        PS = [ctx.enter_context(nc.psum_tensor(f"PS{b}", [P, C], F32)) for b in range(8)]

        dve_done = sem("dve_done")
        x_in, small_in = sems("x_in", 2), sem("small_in")
        w_in, w_high, w_low = sem("w_in"), sem("w_high"), sem("w_low")
        ident_zero, ident_ready, consts_ready = sem("ident_zero"), sem("ident_ready"), sem("consts_ready")
        var_ready, std_ready, rstd_ready = sem("var_ready"), sem("std_ready"), sem("rstd_ready")
        xn_ready, xn_transposed = sems("xn_ready", 2), sems("xn_transposed", 2)
        xh_ready, xl_ready = sems("xh_ready", 2), sems("xl_ready", 2)
        h_psum, hh_ready, hl_ready = sems("h_psum", 2), sems("hh_ready", 2), sems("hl_ready", 2)
        sup_psum, sup_copied, z_copied = sems("sup_psum", 2), sems("sup_copied", 2), sems("z_copied", 2)
        z_max, z_reduced, z_neg, z_exp = (sem(f"z_{n}") for n in ("max", "reduced", "neg", "exp"))
        adj_in, mask_ready, mask_stored = sems("adj_in", 2), sems("mask_ready", 2), sems("mask_stored", 2)
        e_ready, e_read = sems("e_ready", NCH), sems("e_read", NCH)
        nmax_ready, p_ready = sems("nmax_ready", 2), sems("p_ready", 2)
        pt_psum, pth_ready, ptl_ready = sems("pt_psum", 2), sems("pth_ready", 2), sems("ptl_ready", 2)
        o_ready, o_read = sems("o_ready", 2), sems("o_read", 2)
        x_ready, bias_added, eye_cleared = sem("x_ready"), sem("bias_added"), sem("eye_cleared")
        zeroed = sem("zeroed")
        lg_ready, sh_ready, ex_ready = sem("lg_ready"), sem("sh_ready"), sem("ex_ready")
        m_product, m_copied = sem("m_product"), sem("m_copied")
        hid_psum, hid_ready = sems("hid_psum", 4), sems("hid_ready", 4)
        low_psum, low_ready = sem("low_psum"), sem("low_ready")
        gx_ready, gt_psum, gt_ready = sem("gx_ready"), sems("gt_psum", 2), sem("gt_ready")
        f0_psum, f0_read = sems("f0_psum", 2), sems("f0_read", 2)
        v_ones, v_psum, v_read = sem("v_ones"), sems("v_psum", 2), sems("v_read", 2)
        qk_psum, qk_high, qk_low, qk_stored = sem("qk_psum"), sem("qk_high"), sems("qk_low", 2), sems("qk_stored", 2)
        stack_in, row_ones = sems("stack_in", 2), sem("row_ones")
        rmax_psum, rmax_read = sems("rmax_psum", 2), sems("rmax_read", 2)
        rmax_ready, rneg_ready, rrow_psum, rrow_ready = (sem(n) for n in ("rmax_ready", "rneg_ready", "rrow_psum", "rrow_ready"))
        st_ready, exp_done, pv_done = sems("st_ready", 4), sems("exp_done", 4), sems("pv_done", 4)
        pl_ready, att_ready = sems("pl_ready", 4), sem("att_ready")
        v_high = sems("v_high", 2)
        rden_ready, att_read, halves_added = sem("rden_ready"), sems("att_read", 2), sem("halves_added")
        at_psum, ath_ready, atl_ready = sems("at_psum", 2), sems("ath_ready", 2), sems("atl_ready", 2)
        wo_psum, wo_read = sems("wo_psum", 2), sems("wo_read", 2)
        gtl_ready = sem("gtl_ready")
        y_psum, y_read = sem("y_psum"), sems("y_read", 4)
        bias_psum, bias_read = sem("bias_psum"), sem("bias_read")
        stored = sem("stored")

        start_at_one = [*mask_ready, *xn_transposed, *xl_ready, *hl_ready, *z_copied, *e_read, *ptl_ready, *o_read, *o_ready,
                        *mask_stored, *nmax_ready, *hid_ready, *f0_read, *qk_low, *qk_stored, *v_read, *rmax_read, *exp_done,
                        *att_read, att_ready, *pv_done, *at_psum, *ath_ready, *atl_ready, *wo_read, *wo_psum, *y_read, low_ready, bias_read]

        block = ctx.enter_context(nc.Block())
        x_tiles = x.rearrange("(t p) d -> p t d", p=P)
        out_tiles = out.rearrange("(t p) d -> p t d", p=P)
        adj_tiles = adj.rearrange("(t p) n -> t p n", p=P)

        EARLY = 2
        LAST_CHUNK, FIRST_CHUNKS = range(NCH - 1, NCH), range(NCH - 1)
        LAG = 3
        SHIFT = 7
        ROW_AT = SHIFT + 2

        def maxima_piece(ic, j):
            if j < SHIFT:
                return 3, ic > 0, (ic - 1) % NCH, NT - SHIFT + j
            return 4, True, ic, j - SHIFT

        @block.sync
        def _(sp):
            def load_weights(layer, w):
                sp.dma_start(W[layer][0], w.rearrange("(k p) n -> p k n", p=P)).then_inc(w_in, 16)

            for half in range(2):
                tiles = slice(half * HT, (half + 1) * HT)
                sp.dma_start(X[:, tiles, :], x_tiles[:, tiles, :]).then_inc(x_in[half], 16)
            load_weights(0, w_gnn0)
            sp.dma_start(gbias[:, :], g_bias.rearrange("(a d) -> a d", a=1).to_broadcast([P, D])).then_inc(small_in, 16)
            sp.dma_start(mbias[:, :], mixer_b.rearrange("(a d) -> a d", a=1).to_broadcast([P, NE])).then_inc(small_in, 16)

            def adjacency(it):
                for s in range(2):
                    sp.wait_ge(mask_ready[s], it + 1)
                    sp.dma_start(ADJ[s], adj_tiles[2 * it + s, :, :]).then_inc(adj_in[s], 16)
                for s in range(2):
                    sp.wait_ge(mask_ready[s], it + 2)
                    sp.dma_start(MASK[:, 2 * it + s, :], MROW[s]).then_inc(mask_stored[s], 16)

            adjacency(0)
            sp.wait_ge(z_max, 1)
            sp.wait_ge(bias_added, 1)
            load_weights(1, w_ffn0)
            with sp.Fori(1, HT) as it:
                adjacency(it)

            sp.wait_ge(x_ready, 1)
            sp.dma_start(FC2, fc2.rearrange("e (k p) d -> p (e k) d", p=P)).then_inc(small_in, 16)
            sp.wait_ge(zeroed, 2)
            for e in range(E):
                sp.dma_start(LA[:, e * KD:(e + 1) * KD, e * R:(e + 1) * R],
                             lora_a[e].rearrange("(k p) r -> p k r", p=P)).then_inc(small_in, 16)
                sp.dma_start(BT[:, e * KD:(e + 1) * KD, e * R:(e + 1) * R],
                             lora_bt[e].rearrange("(k p) r -> p k r", p=P)).then_inc(small_in, 16)

            load_weights(2, w_gnn1)
            def store_pair(pair):
                for q in range(2):
                    sp.wait_ge(qk_low[q], NCH * pair + NCH + 1)
                    for part in range(2):
                        sp.dma_start(QK[q, part, bass.ds(2 * pair, 2), :, :].rearrange("h d n -> (h d) n"),
                                     QKS[q][part]).then_inc(qk_stored[q], 16)

            def load_stack(h, s):
                for tile, at, q, part in ((KS, 0, 1, 0), (KS, HD, 1, 1), (QD, 0, 0, 0), (QD, HD, 0, 0),
                                          (QL, 0, 0, 1), (KO, 0, 1, 0)):
                    sp.dma_start(tile[s][at:at + HD, :], QK[q, part, h, :, :]).then_inc(stack_in[s], 16)

            store_pair(0)
            for q in range(2):
                sp.wait_ge(qk_stored[q], 33)
            load_stack(0, 0)
            with sp.Fori(1, H // 2) as pair:
                store_pair(pair)
            for q in range(2):
                sp.wait_ge(qk_stored[q], 32 * H // 2 + 1)
            load_stack(1, 1)
            with sp.Fori(1, H // 2) as pair:
                for s in range(2):
                    sp.wait_ge(st_ready[3], 32 * pair + 16 * s - 16)
                    load_stack(2 * pair + s, s)

            load_weights(3, wo)
            sp.wait_ge(pv_done[3], 16 * H + 1)
            sp.wait_ge(att_ready, NCH * H + 1)
            load_weights(4, w_ffn1)
            sp.wait_ge(zeroed, 7)
            for row in BIAS_ROWS:
                sp.dma_start(BSTAGE[row:row + NE, :], expert_biases).then_inc(small_in, 16)
            with sp.Fori(0, NT) as t:
                sp.wait_ge(bias_read, t + 2)
                sp.dma_start(out_tiles[:, t, :], X[:, t, :]).then_inc(stored, 16)
            sp.wait_ge(stored, 16 * NT)

        @block.gpsimd
        def _(pool):
            for first in start_at_one:
                pool.sem_inc(first, 1)
            nc.gpsimd.memset(identf[:, :], 0.0).then_inc(ident_zero, 1)
            pool.wait_ge(ident_zero, 1)
            nc.gpsimd.affine_select(out=identf[:, :], in_=identf[:, :], compare_op=ALU.not_equal, fill=1.0, base=0,
                                    pattern=[[-1, P]], channel_multiplier=1).then_inc(ident_ready, 1)
            pool.wait_ge(small_in, 32)
            for s in range(2):
                pool.wait_ge(xn_transposed[s], QT + 1)
            nc.gpsimd.tensor_tensor(X[:, :, :], X[:, :, :], gbias[:, :].unsqueeze(1).to_broadcast([P, NT, D]),
                                    ALU.add).then_inc(bias_added, 1)
            def node_max():
                pool.wait_ge(z_max, 1)
                nc.gpsimd.partition_all_reduce(zs[:, 1:2], zs[:, 0:1], P, RMAX).then_inc(z_reduced, 1)
                pool.wait_ge(z_exp, 1)
                nc.gpsimd.partition_all_reduce(zs[:, 4:5], zs[:, 3:4], P, RADD).then_inc(z_reduced, 1)

            node_max()
            pool.wait_ge(x_ready, 1)
            nc.gpsimd.memset(BT, 0.0).then_inc(zeroed, 1)
            nc.gpsimd.memset(LA, 0.0).then_inc(zeroed, 1)
            for padded in (GX, MM, LOWT):
                nc.gpsimd.memset(padded, 0.0).then_inc(zeroed, 1)
            for s in range(2):
                pool.wait_ge(mask_stored[s], 16 * HT + 1)
            pool.wait_ge(consts_ready, 1)
            for t in range(NT):
                own_block = MASK[:, t, t * P:(t + 1) * P]
                nc.gpsimd.tensor_tensor(own_block, own_block, not_eye[:, :], ALU.mult).then_inc(eye_cleared, 1)
            pool.wait_ge(x_ready, 2)
            nc.gpsimd.memset(V[:, :, :, HD:HD + 1], 1.0).then_inc(v_ones, 1)
            pool.wait_ge(v_ones, 1)
            for n, (rows, value) in enumerate(((KO[0][HD:P, :], 0.0), (QL[0][HD:P, :], 0.0), (KO[0][HD:HD + 1, :], 1.0),
                                               (KO[1][HD:P, :], 0.0), (QL[1][HD:P, :], 0.0), (KO[1][HD:HD + 1, :], 1.0))):
                if n == 0:
                    pool.wait_ge(w_low, 3)
                elif n == 3:
                    for q in range(2):
                        pool.wait_ge(qk_stored[q], 32 * H // 2 + 1)
                if n:
                    pool.wait_ge(row_ones, n)
                nc.gpsimd.memset(rows, value).then_inc(row_ones, 1)

            def low_probs(head, ic, before):
                u = head * NCH + ic
                for j in range(1, NT, 2):
                    b = j % 4
                    pool.wait_ge(exp_done[b], u * 4 + j // 4 + 2)
                    nc.gpsimd.tensor_tensor(PL[b], PF[b], PH[b], ALU.subtract).then_inc(pl_ready[b], 1)
                    if j == 5 and before:
                        join_halves(u - 1, head - (ic == 0), (ic - 1) % NCH)

            def join_halves(u, head, ic):
                pool.wait_ge(rden_ready, u + 1)
                nc.gpsimd.tensor_tensor(OC[:, :, 0:HD], OC[:, :, 0:HD], OC[:, :, HD + 1:VW], ALU.add).then_inc(halves_added, 1)
                pool.wait_ge(halves_added, u + 1)
                nc.gpsimd.tensor_tensor(ATT[:, ic * TPC:(ic + 1) * TPC, bass.ds(head * HD, HD)], OC[:, :, 0:HD],
                                        RD[:, :].unsqueeze(2).to_broadcast([P, TPC, HD]), ALU.mult).then_inc(att_ready, 1)

            with pool.Fori(0, H // 2) as pair:
                for s in range(2):
                    for ic in range(NCH):
                        low_probs(2 * pair + s, ic, s or ic)
                join_halves(NCH * (2 * pair + 2) - 1, 2 * pair + 1, NCH - 1)
            pool.wait_ge(pv_done[3], 16 * H + 1)
            nc.gpsimd.memset(BB, 0.0).then_inc(zeroed, 1)
            nc.gpsimd.memset(BSTAGE, 0.0).then_inc(zeroed, 1)
            pool.wait_ge(x_ready, 3)
            nc.gpsimd.memset(GX1, 0.0).then_inc(zeroed, 1)

        @block.tensor
        def _(pe):
            def split_product(ps, left, right, last_of=None):
                n = 0
                for k in range(KD):
                    for a, b in ((0, 0), (0, 1), (1, 0)):
                        n += 1
                        last = pe.matmul(ps, left(a, k), right(b, k), start=(n == 1), stop=(n == 3 * KD),
                                         skip_group_check=True)
                return last

            def transpose_nodes(f, beside=None):
                if beside is not None:
                    pe.wait_ge(w_low, SPLITS[W_OF[f]])
                    pe.wait_ge(w_high, SPLITS[W_OF[f]])
                for it in range(QT):
                    for s in range(2):
                        pe.wait_ge(xn_ready[s], 2 * (f * QT + it + 1))
                        pe.wait_ge(xl_ready[s], f * QT + it + 1)
                        for k in range(KD):
                            for r in range(2):
                                at = (2 * k + r) * P
                                last = pe.transpose(PS[s][:, at:at + P], XN[s][:, r, k * P:(k + 1) * P], identf[:, :])
                        last.then_inc(xn_transposed[s], 1)
                        if beside is not None and it > 0:
                            beside(2 * it + s - 2)
                for s in range(2):
                    pe.wait_ge(xl_ready[s], (f + 1) * QT + 1)
                    if beside is not None:
                        beside(2 * QT - 2 + s)
                if beside is None:
                    pe.wait_ge(w_low, SPLITS[W_OF[f]])
                    pe.wait_ge(w_high, SPLITS[W_OF[f]])

            pe.wait_ge(ident_ready, 1)
            pe.wait_ge(consts_ready, 1)

            transpose_nodes(0)
            xt, w = XT[0], W[0][1:]
            with pe.Fori(0, NCH) as c:
                for o in range(KD):
                    pe.wait_ge(hl_ready[o], c + 1)
                    split_product(PS[2 + o][:, :], lambda a, k: w[a][:, k, o * P:(o + 1) * P],
                                  lambda b, k: xt[b][:, k, bass.ds(c * C, C)]).then_inc(h_psum[o], 1)
            with pe.Fori(0, QT) as it:
                for r in range(4):
                    s = r % 2
                    pe.wait_ge(z_copied[s], 2 * it + 1)
                    split_product(PS[4 + r][:, 0:D + 1], lambda a, k: xt[a][:, k, bass.ds((4 * it + r) * P, P)],
                                  lambda b, k: w[b][:, k, D:2 * D + 1]).then_inc(sup_psum[s], 1)

            def edge_scores(t, chunks):
                for c in chunks:
                    pe.wait_ge(e_read[c], t + 1)
                    split_product(PS[c][:, :], lambda a, k: (HTh, HTl)[a][:, k, bass.ds(t * P, P)],
                                  lambda b, k: (HTh, HTl)[b][:, k, c * C:(c + 1) * C]).then_inc(e_ready[c], 1)

            def edge_output(it, s, next_tile):
                t = 2 * it + s

                def transposes(g):
                    pe.wait_ge(ptl_ready[g % 2], 2 * t + g // 2 + 1)
                    for q in range(TPC):
                        j = g * TPC + q
                        last = pe.transpose(PS[4 + g % 2][:, q * P:(q + 1) * P], PROB[s][:, j * P:(j + 1) * P], identf[:, :])
                    last.then_inc(pt_psum[g % 2], 1)

                def products(g):
                    pe.wait_ge(ptl_ready[g % 2], 2 * t + g // 2 + 2)
                    for q in range(TPC):
                        j = g * TPC + q
                        for n, (p, v) in enumerate(((PTh, SUPh), (PTh, SUPl), (PTl, SUPh))):
                            last = pe.matmul(PS[6 + s][:, 0:D], p[s][:, j * P:(j + 1) * P], v[:, j, :],
                                             start=(j == 0 and n == 0), stop=(j == NT - 1 and n == 2), skip_group_check=True)
                    if g == NCH - 1:
                        last.then_inc(o_ready[s], 1)

                pe.wait_ge(p_ready[s], it + 1)
                transposes(0)
                transposes(1)
                if next_tile is not None:
                    edge_scores(next_tile, LAST_CHUNK)
                pe.wait_ge(o_read[s], it + 1)
                products(0)
                for g in range(2, NCH):
                    transposes(g)
                    products(g - 1)
                products(NCH - 1)

            for s in range(2):
                pe.wait_ge(hl_ready[s], NCH + 1)
                pe.wait_ge(z_copied[s], HT + 1)
            edge_scores(0, range(NCH))
            with pe.Fori(0, HT - 1) as it:
                edge_scores(2 * it + 1, FIRST_CHUNKS)
                edge_output(it, 0, 2 * it + 1)
                edge_scores(2 * it + 2, FIRST_CHUNKS)
                edge_output(it, 1, 2 * it + 2)
            edge_scores(NT - 1, FIRST_CHUNKS)
            edge_output(HT - 1, 0, NT - 1)
            edge_output(HT - 1, 1, None)

            pe.wait_ge(x_ready, 1)
            xt, w = XT[1], W[1][1:]

            def narrow_products(bank, first, cols):
                def pair_of_tiles(n):
                    for t in (2 * n, 2 * n + 1):
                        split_product(PS[bank][:, t * cols:(t + 1) * cols], lambda a, k: xt[a][:, k, t * P:(t + 1) * P],
                                      lambda b, k: w[b][:, k, first:first + cols]).then_inc(lg_ready, 1)
                return pair_of_tiles

            transpose_nodes(1, narrow_products(2, E * D, E + 1))
            pe.wait_ge(small_in, 16 * (2 + 1 + 2 * E))
            for o in range(E * KD):
                last = pe.matmul(PS[3][0:ER, 0:D], BT[:, o, :], FC2[:, o, :], start=(o == 0), stop=(o == E * KD - 1))
            last.then_inc(m_product, 1)
            pe.wait_ge(m_copied, 1)

            LOW_LAG = 2

            def hidden(c, o):
                b = o % 4
                pe.wait_ge(hid_ready[b], 2 * c + o // 4 + 1)
                split_product(PS[4 + b][:, :], lambda a, k: w[a][:, k, o * P:(o + 1) * P],
                              lambda bb, k: xt[bb][:, k, bass.ds(c * C, C)]).then_inc(hid_psum[b], 1)

            def adapter(c, o):
                pe.wait_ge(hid_ready[o % 4], 2 * c + o // 4 + 2)
                if o == 0:
                    pe.wait_ge(low_ready, c + 1)
                last = pe.matmul(PS[0][0:ER, :], LA[:, o, :], HID[:, o, :], start=(o == 0), stop=(o == E * KD - 1))
                if o == E * KD - 1:
                    last.then_inc(low_psum, 1)

            def expert_outputs(c):
                pe.wait_ge(low_ready, c + 2)
                for s in range(2):
                    pe.wait_ge(f0_read[s], c + 1)
                    for r in range(2):
                        n = 2 * s + r
                        last = pe.matmul(PS[2 + s][:, r * D:(r + 1) * D], LOWT[:, n * P:(n + 1) * P], MM, start=True, stop=True)
                    last.then_inc(f0_psum[s], 1)

            def gates_transposed():
                pe.wait_ge(gx_ready, 1)
                for g in range(NCH):
                    if g >= 2:
                        pe.wait_ge(gt_ready, g - 1)
                    for q in range(TPC):
                        last = pe.transpose(PS[1 + g % 2][:, q * P:(q + 1) * P], GX[:, g * TPC + q, :], identf[:, :])
                    last.then_inc(gt_psum[g % 2], 1)

            def expert_chunk(c, before):
                for o in range(E * KD):
                    hidden(c, o)
                    if o >= LOW_LAG:
                        adapter(c, o - LOW_LAG)
                    elif before is not None:
                        adapter(before, E * KD + o - LOW_LAG)
                    if o == 4 and before is not None:
                        expert_outputs(before)

            expert_chunk(0, None)
            gates_transposed()
            pe.wait_ge(gt_ready, NCH)
            with pe.Fori(1, NCH) as c:
                expert_chunk(c, c - 1)
            for o in range(E * KD - LOW_LAG, E * KD):
                adapter(NCH - 1, o)
            expert_outputs(NCH - 1)

            pe.wait_ge(x_ready, 2)
            transpose_nodes(2)
            xt, w = XT[2], W[2][1:]
            def early_piece(row, c, n, before):
                b = (n + 1) % 2
                pe.wait_ge(rmax_read[b], before + n // 2 + 1)
                pe.matmul(PS[MAX_BANKS[b]][:, :], QD[0][:, bass.ds(row * P, P)], KS[0][:, c * C:(c + 1) * C],
                          start=True, stop=True).then_inc(rmax_psum[b], 1)

            def project_pair(pair, pieces):
                for q in range(2):
                    for c in range(NCH):
                        if q == 1:
                            pe.wait_ge(qk_low[0], NCH * pair + c + 2)
                        elif not isinstance(pair, int) or pair > 0:
                            pe.wait_ge(qk_low[1], NCH * pair + c - 2)
                        split_product(PS[c][:, :], lambda a, k: w[a][:, k, bass.ds(q * H * HD + pair * P, P)],
                                      lambda bb, k: xt[bb][:, k, c * C:(c + 1) * C]).then_inc(qk_psum, 1)
                        if pieces:
                            if q == 0 and c == 0:
                                pe.wait_ge(stack_in[0], 96)
                            early_piece(2 * (pair - EARLY) + q, c, c, NCH * (pair - EARLY) + 2 * q)

            for pair in range(EARLY):
                project_pair(pair, False)
            with pe.Fori(EARLY, H // 2) as pair:
                project_pair(pair, True)
            for q in range(2):
                pe.wait_ge(qk_low[q], NCH * H // 2 + 1)
            with pe.Fori(0, QT) as it:
                for v in range(TPC):
                    t, s = TPC * it + v, v % 2
                    pe.wait_ge(v_read[s], 2 * it + v // 2 + 1)
                    split_product(PS[s][:, :], lambda a, k: xt[a][:, k, bass.ds(t * P, P)],
                                  lambda b, k: w[b][:, k, 2 * H * HD:3 * H * HD]).then_inc(v_psum[s], 1)
                    for n in (2 * v, 2 * v + 1):
                        early_piece(TPC + 2 * it + n // NCH, n % NCH, n, NT // 2 + NCH * it)

            def max_scores(n, s, g, q, rows_out, after=ROW_AT - SHIFT + 1):
                b, i, c = (q + 1) % 2, g * TPC + q // NCH, q % NCH
                pe.wait_ge(rmax_read[b], n * 8 + q // 2 + 1)
                if q == after:
                    pe.wait_ge(rrow_ready, rows_out)
                pe.matmul(PS[MAX_BANKS[b]][:, :], QD[s][:, i * P:(i + 1) * P], KS[s][:, c * C:(c + 1) * C],
                          start=True, stop=True).then_inc(rmax_psum[b], 1)

            def max_row(n, parity, read):
                pe.wait_ge(rneg_ready, n + 1)
                pe.wait_ge(rmax_read[0], read)
                for r in range(TPC):
                    last = pe.matmul(PS[MAX_BANKS[0]][HD:HD + 1, r * P:(r + 1) * P], MNEG[:, parity, r:r + 1], identf[:, :],
                                     start=True, stop=True, skip_group_check=True)
                last.then_inc(rrow_psum, 1)

            def scores(u, s, ic, j):
                b = j % 4
                if j == 0:
                    pe.wait_ge(rrow_ready, u + 1)
                pe.wait_ge(exp_done[b], u * 4 + j // 4 + 1)
                ps, cols, keys = PS[ST_BANKS[b]], slice(ic * C, (ic + 1) * C), slice(j * P, (j + 1) * P)
                pe.matmul(ps[:, :], KS[s][:, keys], QD[s][:, cols], start=True, stop=False, skip_group_check=True)
                pe.matmul(ps[:, :], KO[s][:, keys], QL[s][:, cols], start=False, stop=False, skip_group_check=True)
                if j // TPC == ic:
                    d = (j % TPC) * P
                    pe.matmul(ps[:, d:d + P], eye_a[:, :], eye_b[:, :], start=False, stop=False, skip_group_check=True)
                for q in range(TPC):
                    last = pe.matmul(ps[:, q * P:(q + 1) * P], MASK[:, ic * TPC + q, keys], identb[:, :],
                                     start=False, stop=(q == TPC - 1), skip_group_check=True)
                last.then_inc(st_ready[b], 1)

            def products(head, u, j):
                pe.wait_ge(pl_ready[j % 4], u * 4 + j // 4 + 1)
                for q in range(TPC):
                    if j == 0 and q % 2 == 0:
                        pe.wait_ge(att_read[q // 2], u + 1)
                    o, at, rows = PS[O_BANKS[q // 2]], (q % 2) * VW, slice(q * P, (q + 1) * P)
                    pe.matmul(o[:, at:at + VW], PH[j % 4][:, rows], V[:, j, head, :], start=(j == 0 and q % 2 == 0),
                              stop=False, skip_group_check=True)
                    last = pe.matmul(o[:, at:at + HD + 1], PL[j % 4][:, rows], V[:, j, head, 0:HD + 1], start=False,
                                     stop=(j == NT - 1), skip_group_check=True)
                last.then_inc(pv_done[j % 4], 1)

            def attend(head, s, ic, before, ahead, row, last):
                u = head * NCH + ic
                for j in range(NT):
                    scores(u, s, ic, j)
                    if j >= LAG:
                        products(head, u, j - LAG)
                    elif before is not None:
                        products(before, u - 1, NT + j - LAG)
                    if j == ROW_AT and row:
                        max_row(u + 3, (ic + 3) % 2, 8 * (u + 4) + (2 if ahead is not None else 1))
                    n, next_head, g, q = maxima_piece(ic, j)
                    if ahead is not None and ic == 0 and j == SHIFT:
                        pe.wait_ge(stack_in[1 - s], ahead)
                    if ahead is not None or not next_head:
                        max_scores(u + n, 1 - s if next_head else s, g, q, u + 4)
                if last:
                    for j in range(NT - LAG, NT):
                        products(head, u, j)

            pe.wait_ge(row_ones, 6)
            pe.wait_ge(eye_cleared, NT)
            for b in range(2):
                pe.wait_ge(v_read[b], HT + 1)
            for g in range(NCH - 1):
                if g:
                    pe.wait_ge(rrow_ready, g)
                max_row(g, g % 2, NT * (NCH - 1) // 2 + 1)
            for q in range(NT - SHIFT):
                max_scores(NCH - 1, 0, NCH - 1, q, NCH - 1, after=1)
            with pe.Fori(0, H // 2 - 1) as pair:
                for s in range(2):
                    head = 2 * pair + s
                    for ic in range(NCH):
                        attend(head, s, ic, (head if ic else head - 1) if s or ic else None, 96 * (pair + s + 1), True,
                               s == 1 and ic == NCH - 1)
            for s in range(2):
                head = H - 2 + s
                for ic in range(NCH):
                    attend(head, s, ic, (head if ic else head - 1) if s or ic else None, 96 * (H // 2) if s == 0 else None,
                           s == 0 or ic == 0, s == 1 and ic == NCH - 1)

            pe.wait_ge(w_high, 4)
            pe.wait_ge(w_low, 4)
            pe.wait_ge(att_ready, NCH * H + 1)
            for b in range(2):
                pe.wait_ge(att_read[b], NCH * H + 1)
            w = W[3][1:]

            def heads_transposed(t):
                it, s = t // 2, t % 2
                pe.wait_ge(atl_ready[s], it + 1)
                for k in range(KC):
                    last = pe.transpose(PS[s][:, k * P:(k + 1) * P], ATT[:, t, k * P:(k + 1) * P], identf[:, :])
                last.then_inc(at_psum[s], 1)

            def heads_projected(t):
                it, s = t // 2, t % 2
                pe.wait_ge(atl_ready[s], it + 2)
                pe.wait_ge(wo_read[s], it + 1)
                for k in range(KC):
                    for n, (a, b) in enumerate(((ATh, 0), (ATh, 1), (ATl, 0))):
                        last = pe.matmul(PS[2 + s][:, 0:D], a[s][:, k * P:(k + 1) * P], w[b][:, k, :],
                                         start=(k == 0 and n == 0), stop=(k == KC - 1 and n == 2), skip_group_check=True)
                last.then_inc(wo_psum[s], 1)

            heads_transposed(0)
            for t in range(NT):
                if t + 1 < NT:
                    heads_transposed(t + 1)
                heads_projected(t)

            pe.wait_ge(x_ready, 3)
            xt, w = XT[3], W[4][1:]
            transpose_nodes(3, narrow_products(4, NE * D, NE))

            def expert_products(t):
                for e in range(NE // 2):
                    pe.wait_ge(y_read[e], t + 1)
                    split_product(PS[e][:, :], lambda a, k: xt[a][:, k, bass.ds(t * P, P)],
                                  lambda b, k: w[b][:, k, e * C:(e + 1) * C]).then_inc(y_psum, 1)

            def bias_product(t):
                pe.wait_ge(bias_read, t + 1)
                pe.matmul(PS[7][:, 0:D], GT1[:, bass.ds(t * P, P)], BB, start=True, stop=True).then_inc(bias_psum, 1)

            expert_products(0)
            pe.wait_ge(gx_ready, 2)
            for g in range(NCH):
                if g >= 2:
                    pe.wait_ge(gtl_ready, g - 1)
                for q in range(TPC):
                    last = pe.transpose(PS[5 + g % 2][:, q * P:(q + 1) * P], GX1[:, g * TPC + q, :], identf[:, :])
                last.then_inc(gt_psum[g % 2], 1)
            expert_products(1)
            pe.wait_ge(gtl_ready, NCH)
            pe.wait_ge(w_low, SPLITS[4] + 1)
            for t in range(2):
                bias_product(t)
            with pe.Fori(0, HT - 1) as it:
                for r in range(2):
                    expert_products(2 * it + 2 + r)
                    bias_product(2 * it + 2 + r)

        @block.scalar
        def _(act):
            def high_weights(layer):
                act.wait_ge(w_in, 16 * (layer + 1))
                act.activation(W[layer][1], W[layer][0], ACT.Copy, scale=WS).then_inc(w_high, 1)

            def high_piece(n):
                act.wait_ge(w_in, 16 * len(W))
                act.activation(piece(W[4][1], n), piece(W[4][0], n), ACT.Copy, scale=WS).then_inc(w_high, 1)

            def deviations(f, half):
                act.wait_ge(var_ready, 2 * f + half + 1)
                cols = slice(half * HT, (half + 1) * HT)
                act.activation(SD[:, cols], VAR[:, cols], ACT.Sqrt).then_inc(std_ready, 1)

            def transposed_nodes(f):
                if f == 0:
                    high_weights(f)
                else:
                    act.wait_ge(x_ready, f)
                act.wait_ge(rstd_ready, 2 * f + 1)

                def normalised(it, s):
                    act.wait_ge(xn_transposed[s], f * QT + it + 1)
                    t = 4 * it + 2 * s + 1
                    act.activation(XN[s][:, 1, :], X[:, t, :], ACT.Identity, scale=RSTD[:, t:t + 1],
                                   bias=NMR[:, t:t + 1]).then_inc(xn_ready[s], 1)

                for s in range(2):
                    normalised(0, s)
                for it in range(QT):
                    for s in range(2):
                        act.wait_ge(xn_transposed[s], f * QT + it + 2)
                        act.activation(XT[f][0][:, :, (2 * it + s) * 2 * P:(2 * it + s + 1) * 2 * P],
                                       PS[s][:, :].rearrange("p (k n) -> p k n", k=KD), ACT.Copy).then_inc(xh_ready[s], 1)
                        if it == 0 and s == 1:
                            deviations(f, 1)
                        if it == QT // 2 - 1 and s == 0:
                            act.wait_ge(rstd_ready, 2 * f + 2)
                        if it + 1 < QT:
                            normalised(it + 1, s)

            deviations(0, 0)
            transposed_nodes(0)
            with act.Fori(0, NCH) as c:
                for o in range(KD):
                    act.wait_ge(h_psum[o], c + 1)
                    act.activation(HTh[:, o, bass.ds(c * C, C)], PS[2 + o][:, :], ACT.Copy, scale=1 / WS).then_inc(hh_ready[o], 1)
            with act.Fori(0, QT) as it:
                for r in range(4):
                    s = r % 2
                    act.wait_ge(sup_psum[s], 2 * it + r // 2 + 1)
                    act.activation(SUPh[:, 4 * it + r, :], PS[4 + r][:, 0:D], ACT.Copy).then_inc(sup_copied[s], 1)

            def edge_exp(it, s):
                act.wait_ge(nmax_ready[s], it + 2)
                act.activation(PROB[s], PROB[s], ACT.Exp, bias=NMX[:, s:s + 1], accum_out=RSUM[:, s:s + 1]).then_inc(p_ready[s], 1)

            def edge_evacuate(it, s):
                for g in range(NCH):
                    act.wait_ge(pt_psum[g % 2], 2 * (2 * it + s) + g // 2 + 1)
                    if g == 0:
                        act.wait_ge(o_ready[s], it + 1)
                    act.activation(PTh[s][:, g * C:(g + 1) * C], PS[4 + g % 2][:, :], ACT.Copy).then_inc(pth_ready[g % 2], 1)

            def mask_row(it, s):
                act.wait_ge(adj_in[s], 16 * (it + 1))
                act.wait_ge(nmax_ready[s], it + 1)
                act.wait_ge(mask_stored[s], 16 * it + 1)
                act.activation(MROW[s], ADJ[s], ACT.Copy, scale=-MASKED, bias=MASKED).then_inc(mask_ready[s], 1)

            for s in range(2):
                mask_row(0, s)
            act.wait_ge(z_neg, 1)
            act.activation(NATT[:, :], ZC[:, :], ACT.Exp, bias=zs[:, 2:3], accum_out=zs[:, 3:4]).then_inc(z_exp, 1)
            def edge_pairs(first, end):
                with act.Fori(first, end) as it:
                    for s in range(2):
                        edge_exp(it, s)
                        edge_evacuate(it, s)
                        mask_row(it + 1, s)

            edge_pairs(0, HT // 2)
            high_weights(1)
            edge_pairs(HT // 2, HT - 1)
            for s in range(2):
                if s == 1:
                    deviations(1, 0)
                edge_exp(HT - 1, s)
                edge_evacuate(HT - 1, s)

            transposed_nodes(1)
            high_weights(2)
            act.wait_ge(sh_ready, 1)
            act.activation(GW[:, :, 0:E], LG[:, :, 0:E], ACT.Exp).then_inc(ex_ready, 1)
            act.activation(GS[:, 3, :], LG[:, :, E], ACT.Exp, scale=-1.0).then_inc(ex_ready, 1)
            act.wait_ge(m_product, 1)
            act.wait_ge(zeroed, 5)
            act.activation(MM[0:ER, :], PS[3][0:ER, 0:D], ACT.Copy).then_inc(m_copied, 1)

            def hidden_relu(c):
                for o in range(E * KD):
                    act.wait_ge(hid_psum[o % 4], 2 * c + o // 4 + 1)
                    act.activation(HID[:, o, :], PS[4 + o % 4][:, :], ACT.Relu, scale=1 / WS).then_inc(hid_ready[o % 4], 1)

            hidden_relu(0)
            for g in range(NCH):
                act.wait_ge(gt_psum[g % 2], g // 2 + 1)
                act.activation(GT[:, g * C:(g + 1) * C], PS[1 + g % 2][:, :], ACT.Copy).then_inc(gt_ready, 1)
            with act.Fori(1, NCH) as c:
                hidden_relu(c)
            deviations(2, 0)

            transposed_nodes(2)
            with act.Fori(0, H // 2) as pair:
                for q in range(2):
                    act.wait_ge(qk_stored[q], 32 * pair + 1)
                    for c in range(NCH):
                        act.wait_ge(qk_psum, 2 * NCH * pair + NCH * q + c + 1)
                        act.activation(QKS[q][0][:, c * C:(c + 1) * C], PS[c][:, :], ACT.Copy,
                                       scale=1 / WS).then_inc(qk_high, 1)
            with act.Fori(0, HT) as it:
                for s in range(2):
                    act.wait_ge(v_psum[s], it + 1)
                    act.activation(V[:, 2 * it + s, :, 0:HD], PS[s][:, :].rearrange("p (h d) -> p h d", h=H), ACT.Copy,
                                   scale=1 / WS).then_inc(v_high[s], 1)

            def max_row(s, n, g):
                act.wait_ge(rrow_psum, n + 1)
                act.activation(QL[s][HD:HD + 1, g * C:(g + 1) * C], PS[MAX_BANKS[0]][HD:HD + 1, :], ACT.Copy).then_inc(rrow_ready, 1)

            def exps(head, s, ic, row):
                u = head * NCH + ic
                for j in range(NT):
                    ps = PS[ST_BANKS[j % 4]][:, :]
                    act.wait_ge(st_ready[j % 4], u * 4 + j // 4 + 1)
                    act.wait_ge(pv_done[j % 4], u * 4 + j // 4 + 1)
                    act.activation(PF[j % 4], ps, ACT.Exp, scale=SCALE)
                    act.activation(PH[j % 4], ps, ACT.Exp, scale=SCALE).then_inc(exp_done[j % 4], 1)
                    if j == ROW_AT and row is not None:
                        max_row(s if ic == 0 else 1 - s, row, (ic + 3) % 4)

            for q in range(2):
                act.wait_ge(qk_stored[q], 32 * H // 2 + 1)
            act.wait_ge(row_ones, 6)
            for g in range(NCH - 1):
                max_row(0, g, g)
            with act.Fori(0, H // 2 - 1) as pair:
                for s in range(2):
                    for ic in range(NCH):
                        exps(2 * pair + s, s, ic, (2 * pair + s) * NCH + ic + 3)
            for s in range(2):
                for ic in range(NCH):
                    if s == 1 and ic == NCH - 1:
                        high_weights(3)
                    row = (H - 2 + s) * NCH + ic + 3
                    exps(H - 2 + s, s, ic, row if row < H * NCH else None)
            for n, (first, end) in enumerate(PROJECTED):
                with act.Fori(first, end) as it:
                    for s in range(2):
                        act.wait_ge(at_psum[s], it + 2)
                        act.wait_ge(wo_psum[s], it + 1)
                        act.activation(ATh[s], PS[s][:, :], ACT.Copy).then_inc(ath_ready[s], 1)
                if n < PIECES:
                    high_piece(n)
                if n == 2:
                    deviations(3, 0)
            act.wait_ge(small_in, 16 * (2 + 1 + 2 * E + len(BIAS_ROWS)))
            act.activation(BB, BSTAGE, ACT.Copy, scale=WS).then_inc(w_high, 1)

            transposed_nodes(3)
            act.wait_ge(sh_ready, 2)
            act.activation(GW[:, :, 0:NE], LG[:, :, 0:NE], ACT.Exp).then_inc(ex_ready, 1)
            for g in range(NCH):
                act.wait_ge(gt_psum[g % 2], NCH // 2 + g // 2 + 1)
                act.activation(GT1[:, g * C:(g + 1) * C], PS[5 + g % 2][:, :], ACT.Copy).then_inc(gt_ready, 1)

        @block.vector
        def _(dve):
            own = Tally(dve, dve_done)

            def take_waits(n):
                dve.memset(idle_cells[:, n:n + 1], 0.0)

            tt, ts, stt = dve.tensor_tensor, dve.tensor_scalar, dve.scalar_tensor_tensor

            def low_weights(layer):
                dve.wait_ge(w_high, layer + 1)
                stt(out=W[layer][2], in0=W[layer][0], scalar=WS, in1=W[layer][1], op0=ALU.mult,
                    op1=ALU.subtract).then_inc(w_low, 1)

            def low_piece(n):
                dve.wait_ge(w_high, 4 + n + 1)
                stt(out=piece(W[4][2], n), in0=piece(W[4][0], n), scalar=WS, in1=piece(W[4][1], n), op0=ALU.mult,
                    op1=ALU.subtract).then_inc(w_low, 1)

            def stats(t):
                own.add(dve.bn_stats(STATS[:, t, :], X[:, t, :]))

            def variances(half):
                own.wait()
                cols = slice(half * HT, (half + 1) * HT)
                me, ve, mo, vo = (STATS[:, cols, i] for i in (1, 2, 4, 5))
                mean, ta, tb = MEAN[:, cols], TA[:, cols], TB[:, cols]
                own.add(tt(mean, me, mo, ALU.add))
                own.add(tt(ta, me, mo, ALU.subtract))
                own.add(tt(tb, ve, vo, ALU.add))
                own.wait()
                own.add(ts(mean, mean, 0.5, None, ALU.mult))
                own.add(tt(ta, ta, ta, ALU.mult))
                own.add(ts(tb, tb, 1.0 / D, EPS, ALU.mult, ALU.add))
                own.wait()
                stt(out=VAR[:, cols], in0=ta, scalar=0.25, in1=tb, op0=ALU.mult, op1=ALU.add).then_inc(var_ready, 1)

            def reciprocals(f, half):
                cols = slice(half * HT, (half + 1) * HT)
                ta, rstd = TA[:, cols], RSTD[:, cols]
                dve.wait_ge(std_ready, 2 * f + half + 1)
                own.add(dve.reciprocal(rstd, SD[:, cols]))
                own.wait()
                own.add(tt(ta, rstd, rstd, ALU.mult))
                own.wait()
                own.add(tt(ta, ta, VAR[:, cols], ALU.mult))
                own.wait()
                own.add(ts(ta, ta, -0.5, 1.5, ALU.mult, ALU.add))
                own.wait()
                own.add(tt(rstd, rstd, ta, ALU.mult))
                own.wait()
                stt(out=NMR[:, cols], in0=MEAN[:, cols], scalar=-1.0, in1=rstd, op0=ALU.mult, op1=ALU.mult).then_inc(rstd_ready, 1)

            def layernorm(f):
                def normalised(it, s):
                    dve.wait_ge(xn_transposed[s], f * QT + it + 1)
                    t = 4 * it + 2 * s
                    ts(XN[s][:, 0, :], X[:, t, :], MEAN[:, t:t + 1], RSTD[:, t:t + 1], ALU.subtract,
                       ALU.mult).then_inc(xn_ready[s], 1)

                def low_part(it, s):
                    cols = slice((2 * it + s) * 2 * P, (2 * it + s + 1) * 2 * P)
                    dve.wait_ge(xh_ready[s], f * QT + it + 1)
                    tt(XT[f][1][:, :, cols], PS[s][:, :].rearrange("p (k n) -> p k n", k=KD), XT[f][0][:, :, cols],
                       ALU.subtract).then_inc(xl_ready[s], 1)

                for s in range(2):
                    normalised(0, s)
                variances(1)
                for it in range(QT - 1):
                    if it == QT // 2 - 1:
                        reciprocals(f, 1)
                    for s in range(2):
                        low_part(it, s)
                        normalised(it + 1, s)
                if f == 0:
                    low_weights(f)
                for s in range(2):
                    low_part(QT - 1, s)

            dve.wait_ge(ident_ready, 1)
            own.add(dve.tensor_copy(identb[:, :], identf[:, :]))
            own.add(ts(not_eye[:, :], identf[:, :], -1.0, 1.0, ALU.mult, ALU.add))
            own.add(ts(eye_a[:, :], identf[:, :], EYE_A, None, ALU.mult))
            ts(eye_b[:, :], identf[:, :], EYE_B, None, ALU.mult).then_inc(consts_ready, 1)

            for half in range(2):
                dve.wait_ge(x_in[half], 16)
                for t in range(half * HT, (half + 1) * HT):
                    stats(t)
                if half == 0:
                    variances(0)
            reciprocals(0, 0)
            layernorm(0)
            with dve.Fori(0, NCH) as c:
                for o in range(KD):
                    cols = bass.ds(c * C, C)
                    dve.wait_ge(hh_ready[o], c + 1)
                    stt(out=HTl[:, o, cols], in0=PS[2 + o][:, :], scalar=1 / WS, in1=HTh[:, o, cols], op0=ALU.mult,
                        op1=ALU.subtract).then_inc(hl_ready[o], 1)
            with dve.Fori(0, QT) as it:
                for r in range(4):
                    s, t = r % 2, 4 * it + r
                    dve.wait_ge(sup_copied[s], 2 * it + r // 2 + 1)
                    tt(SUPl[:, t, :], PS[4 + r][:, 0:D], SUPh[:, t, :], ALU.subtract)
                    ts(ZC[:, bass.ds(t, 1)], PS[4 + r][:, D:D + 1], 1 / WS, None, ALU.mult).then_inc(z_copied[s], 1)
            for s in range(2):
                dve.wait_ge(z_copied[s], HT + 1)
            dve.tensor_reduce(zs[:, 0:1], ZC[:, :], AX.X, ALU.max).then_inc(z_max, 1)
            def edge_max(it, s, t, chunks):
                for c in chunks:
                    dve.wait_ge(e_ready[c], t + 1)
                    if c == 0:
                        dve.wait_ge(mask_ready[s], it + 2)
                        dve.wait_ge(o_ready[s], it + 1)
                    take_waits(c)
                    dve.tensor_tensor_reduce(out=PROB[s][:, c * C:(c + 1) * C], in0=PS[c][:, :], in1=MROW[s][:, c * C:(c + 1) * C],
                                             scale=1.0, scalar=-3e38, op0=ALU.add, op1=ALU.max,
                                             accum_out=MX[:, s, c:c + 1]).then_inc(e_read[c], 1)
                if chunks == FIRST_CHUNKS:
                    return
                dve.wait_ge(e_read[NCH - 1], t + 2)
                own.add(dve.tensor_reduce(RSC[:, 2:3], MX[:, s, :], AX.X, ALU.max))
                own.wait()
                ts(NMX[:, s:s + 1], RSC[:, 2:3], -1.0, None, ALU.mult).then_inc(nmax_ready[s], 1)

            def edge_low(s, t, groups=range(NCH)):
                for g in groups:
                    dve.wait_ge(pth_ready[g % 2], 2 * t + g // 2 + 1)
                    tt(PTl[s][:, g * C:(g + 1) * C], PS[4 + g % 2][:, :], PTh[s][:, g * C:(g + 1) * C],
                       ALU.subtract).then_inc(ptl_ready[g % 2], 1)

            def edge_update(it, s, t):
                dve.wait_ge(o_ready[s], it + 2)
                own.add(dve.reciprocal(RSC[:, 0:1], RSUM[:, s:s + 1]))
                own.wait()
                own.add(tt(RSC[:, 1:2], RSC[:, 0:1], NATT[:, bass.ds(t, 1)], ALU.mult))
                own.wait()
                stt(out=X[:, t, :], in0=PS[6 + s][:, 0:D], scalar=RSC[:, 1:2], in1=X[:, t, :], op0=ALU.mult,
                    op1=ALU.add).then_inc(o_read[s], 1)
                dve.wait_ge(o_read[s], it + 2)
                stats(t)

            def edge_step(it, s, t, nodes_left=False):
                edge_max(it + s, 1 - s, t + 1, FIRST_CHUNKS)
                if nodes_left:
                    dve.wait_ge(z_reduced, 2)
                    own.add(dve.reciprocal(zs[:, 5:6], zs[:, 4:5]))
                    own.wait()
                    own.add(ts(NATT[:, :], NATT[:, :], zs[:, 5:6], 1 / WS, ALU.mult, ALU.mult))
                    own.wait()
                    dve.wait_ge(bias_added, 1)
                edge_low(s, t, range(1))
                edge_max(it + s, 1 - s, t + 1, LAST_CHUNK)
                edge_low(s, t, range(1, NCH))
                edge_update(it, s, t)

            def edge_pair(it, peeled):
                edge_step(it, 0, 2 * it, peeled)
                edge_step(it, 1, 2 * it + 1)

            dve.wait_ge(z_reduced, 1)
            ts(zs[:, 2:3], zs[:, 1:2], -1.0, None, ALU.mult).then_inc(z_neg, 1)
            edge_max(0, 0, 0, range(NCH))
            edge_pair(0, True)
            with own.loop(HT // 2 - 1, 8) as i:
                edge_pair(i + 1, False)
            low_weights(1)
            with own.loop(HT // 2 - 1, 8) as i:
                edge_pair(i + HT // 2, False)
            variances(0)
            edge_step(HT - 1, 0, NT - 2)
            reciprocals(1, 0)
            edge_low(1, NT - 1)
            edge_update(HT - 1, 1, NT - 1)
            for s in range(2):
                dve.wait_ge(o_read[s], HT + 1)
            dve.nop().then_inc(x_ready, 1)
            layernorm(1)
            low_weights(2)
            dve.wait_ge(lg_ready, NT)

            def softmax_shift(n, bias):
                lg, ps = LG[:, :, 0:n], PS[2 if n == E else 4]
                cols = n + (n == E)
                own.add(ts(LG[:, :, 0:cols], ps[:, 0:NT * cols].rearrange("p (t e) -> p t e", e=cols), 1 / WS, None, ALU.mult))
                own.wait()
                if bias is not None:
                    own.add(tt(lg, lg, bias.unsqueeze(1).to_broadcast([P, NT, n]), ALU.add))
                    own.wait()
                own.add(dve.tensor_reduce(GS[:, 0, :], lg, AX.X, ALU.max))
                own.wait()
                tt(lg, lg, GS[:, 0, :].unsqueeze(2).to_broadcast([P, NT, n]), ALU.subtract).then_inc(sh_ready, 1)

            def softmax_divide(n):
                own.add(dve.tensor_reduce(GS[:, 0, :], GW[:, :, 0:n], AX.X, ALU.add))
                own.wait()
                own.add(dve.reciprocal(GS[:, 1, :], GS[:, 0, :]))
                own.wait()
                own.add(tt(GW[:, :, 0:n], GW[:, :, 0:n], GS[:, 1, :].unsqueeze(2).to_broadcast([P, NT, n]), ALU.mult))
                own.wait()

            softmax_shift(E, None)
            dve.wait_ge(ex_ready, 2)
            softmax_divide(E)
            own.add(ts(GS[:, 3, :], GS[:, 3, :], 1.0, None, ALU.add))
            own.wait()
            own.add(dve.reciprocal(GS[:, 2, :], GS[:, 3, :]))
            own.wait()
            own.add(ts(GS[:, 2, :], GS[:, 2, :], 1.0 / E, None, ALU.mult))
            own.wait()
            own.add(tt(GW[:, :, 0:E], GW[:, :, 0:E], GS[:, 2, :].unsqueeze(2).to_broadcast([P, NT, E]), ALU.subtract))
            own.wait()
            own.add(ts(GW[:, :, 0:E], GW[:, :, 0:E], 0.0, None, ALU.max))
            own.wait()
            own.add(dve.tensor_reduce(GS[:, 0, :], GW[:, :, 0:E], AX.X, ALU.add))
            own.wait()
            own.add(ts(GS[:, 1, :], GS[:, 0, :], 0.0, None, ALU.is_equal))
            own.wait()
            own.add(tt(GS[:, 0, :], GS[:, 0, :], GS[:, 1, :], ALU.add))
            own.wait()
            own.add(dve.reciprocal(GS[:, 1, :], GS[:, 0, :]))
            own.wait()
            own.add(tt(GW[:, :, 0:E], GW[:, :, 0:E], GS[:, 1, :].unsqueeze(2).to_broadcast([P, NT, E]), ALU.mult))
            own.wait()
            dve.wait_ge(zeroed, 5)
            ts(GX[:, :, 0:ER].rearrange("p t (e r) -> p t e r", e=E), GW[:, :, 0:E].unsqueeze(3).to_broadcast([P, NT, E, R]),
               1.0, None, ALU.mult).then_inc(gx_ready, 1)
            dve.wait_ge(gt_ready, NCH)
            def gated(c):
                dve.wait_ge(low_psum, c + 1)
                tt(LOWT[0:ER, :], PS[0][0:ER, :], GT[0:ER, bass.ds(c * C, C)], ALU.mult).then_inc(low_ready, 1)

            def experts_added(c):
                for s in range(2):
                    dve.wait_ge(f0_psum[s], c + 1)
                    pair = X[:, bass.ds(c * TPC + 2 * s, 2), :]
                    tt(pair, PS[2 + s][:, :].rearrange("p (t d) -> p t d", t=2), pair, ALU.add).then_inc(f0_read[s], 1)
                for s in range(2):
                    dve.wait_ge(f0_read[s], c + 2)
                    for r in range(2):
                        stats(c * TPC + 2 * s + r)

            with own.loop(NCH - 1, TPC) as c:
                gated(c)
                experts_added(c)
            variances(0)
            gated(NCH - 1)
            reciprocals(2, 0)
            experts_added(NCH - 1)
            for s in range(2):
                dve.wait_ge(f0_read[s], NCH + 1)
            dve.nop().then_inc(x_ready, 1)
            layernorm(2)
            def early_max(row, c, n):
                b = (n + 1) % 2
                dve.wait_ge(rmax_psum[b], n // 2 + 1)
                dve.tensor_tensor_reduce(out=MJUNK0[b], in0=PS[MAX_BANKS[b]][:, :], in1=MASK[:, row, c * C:(c + 1) * C],
                                         scale=1.0, scalar=-3e38, op0=ALU.add, op1=ALU.max,
                                         accum_out=MQ0[:, row, c:c + 1]).then_inc(rmax_read[b], 1)

            def low_pair(pair, pieces):
                for q in range(2):
                    dve.wait_ge(qk_stored[q], 32 * pair + 1)
                    for c in range(NCH):
                        if pieces:
                            row = 2 * (pair - EARLY) + q
                            early_max(row, c, NCH * row + c)
                        dve.wait_ge(qk_high, 2 * NCH * pair + NCH * q + c + 1)
                        stt(out=QKS[q][1][:, c * C:(c + 1) * C], in0=PS[c][:, :], scalar=1 / WS,
                            in1=QKS[q][0][:, c * C:(c + 1) * C], op0=ALU.mult, op1=ALU.subtract).then_inc(qk_low[q], 1)

            with dve.Fori(0, EARLY) as pair:
                low_pair(pair, False)
            dve.wait_ge(eye_cleared, NT)
            for pair in range(EARLY, H // 2):
                low_pair(pair, True)
            for t in range(NT):
                for n in (2 * t, 2 * t + 1):
                    early_max(TPC + n // NCH, n % NCH, NT + n)
                s = t % 2
                dve.wait_ge(v_high[s], t // 2 + 1)
                stt(out=V[:, t, :, HD + 1:VW], in0=PS[s][:, :].rearrange("p (h d) -> p h d", h=H), scalar=1 / WS,
                    in1=V[:, t, :, 0:HD], op0=ALU.mult, op1=ALU.subtract).then_inc(v_read[s], 1)

            def row_max(n, g, qs):
                for q in qs:
                    b, i, c = (q + 1) % 2, g * TPC + q // NCH, q % NCH
                    dve.wait_ge(rmax_psum[b], n * 8 + q // 2 + 1)
                    take_waits(q)
                    dve.tensor_tensor_reduce(out=MJUNK[b], in0=PS[MAX_BANKS[b]][:, :], in1=MASK[:, i, c * C:(c + 1) * C],
                                             scale=1.0, scalar=-3e38, op0=ALU.add, op1=ALU.max,
                                             accum_out=MQ[:, q // NCH, c:c + 1]).then_inc(rmax_read[b], 1)

            def row_negate(n, parity, quarters=MQ):
                if not isinstance(n, int) or n >= 2:
                    dve.wait_ge(rrow_psum, n - 1)
                for b in range(2):
                    dve.wait_ge(rmax_read[b], n * 8 + 9)
                if not isinstance(n, int) or n >= 1:
                    dve.wait_ge(rneg_ready, n)
                dve.tensor_reduce(MR[:, :], quarters[:, :, :], AX.X, ALU.max).then_inc(rmax_ready, 1)
                dve.wait_ge(rmax_ready, n + 1)
                ts(MNEG[:, parity, :], MR[:, :], -1.0, None, ALU.mult).then_inc(rneg_ready, 1)

            def low_probs(u, j):
                dve.wait_ge(exp_done[j % 4], u * 4 + j // 4 + 2)
                tt(PL[j % 4], PF[j % 4], PH[j % 4], ALU.subtract).then_inc(pl_ready[j % 4], 1)

            def take_outputs(u):
                dve.wait_ge(pv_done[3], u * 4 + 5)
                dve.wait_ge(att_ready, u + 1)
                for b in range(2):
                    dve.tensor_copy(OC[:, 2 * b:2 * b + 2, :], PS[O_BANKS[b]][:, 0:2 * VW].rearrange("p (q d) -> p q d", q=2)
                                    ).then_inc(att_read[b], 1)
                for b in range(2):
                    dve.wait_ge(att_read[b], u + 2)
                dve.reciprocal(RD[:, :], OC[:, :, HD]).then_inc(rden_ready, 1)

            for g in range(NCH - 1):
                row_negate(g, g % 2, MQ0[:, g * TPC:(g + 1) * TPC, :])
            row_max(NCH - 1, NCH - 1, range(NT - SHIFT))

            def attend(head, ic, before, ahead, last):
                u = head * NCH + ic
                for j in range(NT):
                    if j == LAG - 1 and before:
                        take_outputs(u - 1)
                    n, next_head, g, q = maxima_piece(ic, j)
                    if ahead or not next_head:
                        row_max(u + n, g, (q,))
                        if q == NT - 1:
                            row_negate(u + n, (ic + 3) % 2)
                    if j % 2 == 0:
                        low_probs(u, j)
                if last:
                    take_outputs(u)

            with dve.Fori(0, H // 2 - 1) as pair:
                for s in range(2):
                    for ic in range(NCH):
                        attend(2 * pair + s, ic, s or ic, True, s == 1 and ic == NCH - 1)
            for s in range(2):
                for ic in range(NCH):
                    if s == 1 and ic == NCH - 1:
                        low_weights(3)
                    attend(H - 2 + s, ic, s or ic, s == 0, s == 1 and ic == NCH - 1)
            def heads_low(it, s):
                dve.wait_ge(ath_ready[s], it + 2)
                tt(ATl[s], PS[s][:, :], ATh[s], ALU.subtract).then_inc(atl_ready[s], 1)

            def heads_added(it, s):
                t = 2 * it + s
                dve.wait_ge(wo_psum[s], it + 2)
                stt(out=X[:, t, :], in0=PS[2 + s][:, 0:D], scalar=1 / WS, in1=X[:, t, :], op0=ALU.mult,
                    op1=ALU.add).then_inc(wo_read[s], 1)
                dve.wait_ge(wo_read[s], it + 2)
                stats(t)

            heads_low(0, 0)
            for n, (first, end) in enumerate(PROJECTED[:-1]):
                with own.loop(end - first, 2) as i:
                    it = first + i
                    heads_low(it, 1)
                    heads_added(it, 0)
                    heads_low(it + 1, 0)
                    heads_added(it, 1)
                if n == 1:
                    variances(0)
                low_piece(n)
            heads_low(HT - 1, 1)
            reciprocals(3, 0)
            for s in range(2):
                heads_added(HT - 1, s)
            for s in range(2):
                dve.wait_ge(wo_read[s], HT + 1)
            dve.nop().then_inc(x_ready, 1)
            layernorm(3)
            dve.wait_ge(w_high, SPLITS[4] + 1)
            low = slice(BIAS_ROWS[2], BIAS_ROWS[2] + 32)
            stt(out=BB[low, :], in0=BSTAGE[low, :], scalar=WS, in1=BB[low, :], op0=ALU.mult,
                op1=ALU.subtract).then_inc(w_low, 1)
            dve.wait_ge(lg_ready, 2 * NT)
            softmax_shift(NE, mbias[:, :])
            dve.wait_ge(ex_ready, 3)
            softmax_divide(NE)
            dve.wait_ge(zeroed, 8)
            ts(GX1[:, :, 0:3 * 32].rearrange("p t (a c) -> p t a c", a=3)[:, :, :, 0:NE],
               GW[:, :, 0:NE].unsqueeze(2).to_broadcast([P, NT, 3, NE]), 1.0, None, ALU.mult).then_inc(gx_ready, 1)
            dve.wait_ge(gx_ready, 2)
            own.add(ts(GW[:, :, 0:NE], GW[:, :, 0:NE], 1 / WS, None, ALU.mult))
            own.wait()
            def mix(t):
                for e in range(NE):
                    if e % 2 == 0:
                        dve.wait_ge(y_psum, NE // 2 * t + e // 2 + 1)
                    ins = stt(out=X[:, t, :], in0=PS[e // 2][:, (e % 2) * D:(e % 2 + 1) * D], scalar=GW[:, t, e:e + 1],
                              in1=X[:, t, :], op0=ALU.mult, op1=ALU.add)
                    if e % 2 == 0:
                        own.add(ins)
                        own.wait()
                    else:
                        ins.then_inc(y_read[e // 2], 1)
                        dve.wait_ge(y_read[e // 2], t + 2)

            def mix_biases(t):
                dve.wait_ge(bias_psum, t + 1)
                stt(out=X[:, t, :], in0=PS[7][:, 0:D], scalar=1 / WS, in1=X[:, t, :], op0=ALU.mult,
                    op1=ALU.add).then_inc(bias_read, 1)

            mix(0)
            low = slice(BIAS_ROWS[1], BIAS_ROWS[1] + 32)
            for g in range(NCH):
                cols = slice(g * C, (g + 1) * C)
                dve.wait_ge(gt_ready, NCH + g + 1)
                tt(GT1[low, cols], PS[5 + g % 2][low, :], GT1[low, cols], ALU.subtract).then_inc(gtl_ready, 1)
            mix(1)
            for t in range(2):
                mix_biases(t)
            with own.loop(HT - 1, NE) as it:
                for r in range(2):
                    mix(2 * it + 2 + r)
                    mix_biases(2 * it + 2 + r)


def kernel(x, adj, L0_gnn_weight, L0_gnn_bias, L0_gnn_node_w, L0_gnn_edge_w, L0_ffn_gate_w, L0_ffn_thr_w, L0_ffn_fc1_w,
           L0_ffn_lora_A, L0_ffn_lora_B, L0_ffn_fc2_w, L1_gnn_Wks, L1_gnn_Wqs, L1_gnn_Wvs, L1_gnn_Wo,
           L1_ffn_expert_weights, L1_ffn_expert_biases, L1_ffn_mixer_w, L1_ffn_mixer_b):
    import concourse.bacc as bacc
    from concourse.bass_utils import run_bass_kernel_spmd

    def heads(w):
        w = np.asarray(w).transpose(1, 0, 2)
        return w.reshape(w.shape[0], -1)

    def by_input(w):
        w = np.asarray(w).transpose(2, 0, 1)
        return w.reshape(w.shape[0], -1)

    def side_by_side(*ws):
        return np.concatenate([np.asarray(w) for w in ws], axis=1)

    wo = np.asarray(L1_gnn_Wo)
    arrays = {
        "x": x, "adj": adj, "w_gnn0": side_by_side(L0_gnn_edge_w, L0_gnn_weight, L0_gnn_node_w), "g_bias": L0_gnn_bias,
        "w_ffn0": side_by_side(by_input(L0_ffn_fc1_w), np.asarray(L0_ffn_gate_w).T, np.asarray(L0_ffn_thr_w).T),
        "lora_a": L0_ffn_lora_A, "lora_bt": np.asarray(L0_ffn_lora_B).transpose(0, 2, 1),
        "fc2": np.asarray(L0_ffn_fc2_w).transpose(0, 2, 1),
        "w_gnn1": side_by_side(heads(L1_gnn_Wqs), heads(L1_gnn_Wks), heads(L1_gnn_Wvs)), "wo": wo.reshape(-1, wo.shape[2]),
        "w_ffn1": side_by_side(by_input(L1_ffn_expert_weights), np.asarray(L1_ffn_mixer_w).T),
        "expert_biases": L1_ffn_expert_biases, "mixer_b": L1_ffn_mixer_b,
    }
    arrays = {name: np.ascontiguousarray(a) for name, a in arrays.items()}
    nc = bacc.Bacc("TRN2", target_bir_lowering=False, num_devices=1)
    ins = {name: nc.dram_tensor(name, a.shape, mybir.dt.from_np(a.dtype), kind="ExternalInput").ap()
           for name, a in arrays.items()}
    out = nc.dram_tensor("y", arrays["x"].shape, F32, kind="ExternalOutput").ap()
    gnn_moe_program(nc, **ins, out=out)
    r = run_bass_kernel_spmd(nc, [arrays], core_ids=[0])
    return r.results[0]["y"]
```
